# Optimizing a Trainium2 kernel written in Bass

```python
import numpy as np
import jax
import jax.numpy as jnp

def _softmax(x, axis=-1):
    return jax.nn.softmax(x, axis=axis)

def _gelu(x):
    return jax.nn.gelu(x, approximate=True)

def _silu(x):
    return jax.nn.silu(x)

def _sigmoid(x):
    return jax.nn.sigmoid(x)

def _layernorm(x, axis=-1, eps=1e-05):
    m = jnp.mean(x, axis=axis, keepdims=True)
    v = jnp.var(x, axis=axis, keepdims=True)
    return (x - m) / jnp.sqrt(v + eps)

def _scatter_add(tgt, idx, src, axis=0):
    return tgt.at[idx].add(src)

def _segment_sum(src, seg, n):
    return jax.ops.segment_sum(src, seg, n)
kernel_name = 'mk_adaln_d1_jaxref_r4_00b369'

def setup_inputs(seed: int=0):
    np.random.seed(seed)
    _w = jnp.asarray

    def _L0_attn_setup():
        import jax, jax.numpy as jnp
        import numpy as np
        key = jax.random.key(seed)
        ks = jax.random.split(key, 5)
        B, T, D = (4, 1024, 256)
        x = jax.random.normal(ks[0], (B, T, D), dtype=jnp.float32)
        Wqkv = jax.random.normal(ks[1], (D, 3 * D), dtype=jnp.float32) * D ** (-0.5)
        bqkv = jax.random.normal(ks[2], (3 * D,), dtype=jnp.float32) * 0.02
        Wout = jax.random.normal(ks[3], (D, D), dtype=jnp.float32) * D ** (-0.5)
        bout = jax.random.normal(ks[4], (D,), dtype=jnp.float32) * 0.02
        return {'x': x, 'Wqkv': Wqkv, 'bqkv': bqkv, 'Wout': Wout, 'bout': bout}
    _L0_attn_in = _L0_attn_setup()

    def _L0_ffn_setup():
        import jax, jax.numpy as jnp
        import numpy as np
        NUM_EXPERTS = 8
        TOP_K = 2
        CAPACITY_FACTOR = 1.0

        def _dispatch_compute(xf, top_expert, w1, w2, capacity):
            tokens, hs = xf.shape
            tpe = jnp.bincount(top_expert, length=NUM_EXPERTS)
            indices = jnp.argsort(top_expert)
            offsets = jnp.concatenate([jnp.zeros((1,), tpe.dtype), jnp.cumsum(tpe)[:-1]])
            slot = jnp.arange(capacity)
            pos = offsets[:, None] + slot[None, :]
            valid = slot[None, :] < tpe[:, None]
            tok_idx = indices[jnp.minimum(pos, tokens - 1)]
            xe = jnp.where(valid[..., None], xf[tok_idx], 0.0)
            h = jax.nn.gelu(jnp.einsum('ech,ehf->ecf', xe, w1), approximate=True)
            ye = jnp.einsum('ecf,efh->ech', h, w2)
            tok_safe = jnp.where(valid, tok_idx, tokens)
            out = jnp.zeros((tokens + 1, hs), xf.dtype).at[tok_safe.reshape(-1)].add(ye.reshape(-1, hs))
            return out[:tokens]
        key = jax.random.key(seed)
        k1, k2, k3, k4 = jax.random.split(key, 4)
        hs, ffn = (256, 1024)
        x = jax.random.normal(k1, (512, 2, hs), dtype=jnp.float32)
        router_w = jax.random.normal(k2, (hs, NUM_EXPERTS), dtype=jnp.float32) * hs ** (-0.5)
        w1 = jax.random.normal(k3, (NUM_EXPERTS, hs, ffn), dtype=jnp.float32) * 0.02
        w2 = jax.random.normal(k4, (NUM_EXPERTS, ffn, hs), dtype=jnp.float32) * 0.02
        bias = jnp.zeros((1, 1, hs), dtype=jnp.float32)
        return {'x': x, 'router_w': router_w, 'w1': w1, 'w2': w2, 'bias': bias}
    _L0_ffn_in = _L0_ffn_setup()
    _L0_c = _w((lambda *s: np.random.randn(*s).astype(np.float32) * 0.05)(16, 256))
    _L0_wmod = _w((lambda *s: np.random.randn(*s).astype(np.float32) * 0.05)(256, 6 * 256) * 256 ** (-0.5))
    _d = {'L0_attn_x': _L0_attn_in['x'], 'L0_attn_Wqkv': _L0_attn_in['Wqkv'], 'L0_attn_bqkv': _L0_attn_in['bqkv'], 'L0_attn_Wout': _L0_attn_in['Wout'], 'L0_attn_bout': _L0_attn_in['bout'], 'L0_ffn_router_w': _L0_ffn_in['router_w'], 'L0_ffn_w1': _L0_ffn_in['w1'], 'L0_ffn_w2': _L0_ffn_in['w2'], 'L0_ffn_bias': _L0_ffn_in['bias'], 'L0_c': _L0_c, 'L0_wmod': _L0_wmod}
    _x0 = _d['L0_attn_x']
    _d['L0_attn_x'] = jax.random.normal(jax.random.fold_in(jax.random.key(seed), 1), (16, 512, 256), dtype=_x0.dtype)
    del _x0
    return _d

def reference(L0_attn_x, L0_attn_Wqkv, L0_attn_bqkv, L0_attn_Wout, L0_attn_bout, L0_ffn_router_w, L0_ffn_w1, L0_ffn_w2, L0_ffn_bias, L0_c, L0_wmod):

    def _L0_attn_ref(x, Wqkv, bqkv, Wout, bout):
        import jax, jax.numpy as jnp
        import numpy as np
        qkv = jnp.einsum('btd,de->bte', x, Wqkv) + bqkv
        q, k, v = jnp.split(qkv, 3, axis=-1)
        q = q / jnp.linalg.norm(q, axis=-1, keepdims=True)
        k = k / jnp.linalg.norm(k, axis=-1, keepdims=True)
        kv = jnp.sum(k * v, axis=-2, keepdims=True)
        out = q * kv
        return jnp.einsum('btd,de->bte', out, Wout) + bout

    def _L0_ffn_ref(x, router_w, w1, w2, bias):
        import jax, jax.numpy as jnp
        import numpy as np
        NUM_EXPERTS = 8
        TOP_K = 2
        CAPACITY_FACTOR = 1.0

        def _dispatch_compute(xf, top_expert, w1, w2, capacity):
            tokens, hs = xf.shape
            tpe = jnp.bincount(top_expert, length=NUM_EXPERTS)
            indices = jnp.argsort(top_expert)
            offsets = jnp.concatenate([jnp.zeros((1,), tpe.dtype), jnp.cumsum(tpe)[:-1]])
            slot = jnp.arange(capacity)
            pos = offsets[:, None] + slot[None, :]
            valid = slot[None, :] < tpe[:, None]
            tok_idx = indices[jnp.minimum(pos, tokens - 1)]
            xe = jnp.where(valid[..., None], xf[tok_idx], 0.0)
            h = jax.nn.gelu(jnp.einsum('ech,ehf->ecf', xe, w1), approximate=True)
            ye = jnp.einsum('ecf,efh->ech', h, w2)
            tok_safe = jnp.where(valid, tok_idx, tokens)
            out = jnp.zeros((tokens + 1, hs), xf.dtype).at[tok_safe.reshape(-1)].add(ye.reshape(-1, hs))
            return out[:tokens]
        sl, bs, hs = x.shape
        tokens = sl * bs
        capacity = int(CAPACITY_FACTOR * tokens / NUM_EXPERTS)
        xf = x.reshape(tokens, hs)
        scores = jax.nn.softmax(xf @ router_w, axis=-1)
        expert_weights, top_experts = jax.lax.top_k(scores, TOP_K)
        out = jnp.zeros_like(xf)
        for k in range(TOP_K):
            y = _dispatch_compute(xf, top_experts[:, k].astype(jnp.int32), w1, w2, capacity)
            out = out + y * expert_weights[:, k][:, None]
        return out.reshape(sl, bs, hs) + bias
    x = L0_attn_x
    mod = (_silu(L0_c) @ L0_wmod).reshape(L0_c.shape[0], 6, 1, -1)
    sa, ca, ga, sb, cb, gb = (mod[:, 0], mod[:, 1], mod[:, 2], mod[:, 3], mod[:, 4], mod[:, 5])
    ga = (2 * (ga >= 0) - 1) * jnp.maximum(jnp.abs(ga), 0.25)
    gb = (2 * (gb >= 0) - 1) * jnp.maximum(jnp.abs(gb), 0.25)
    h = _layernorm(x, axis=-1) * (1 + ca) + sa
    x = x + ga * _L0_attn_ref(h, L0_attn_Wqkv, L0_attn_bqkv, L0_attn_Wout, L0_attn_bout)
    h = _layernorm(x, axis=-1) * (1 + cb) + sb
    x = x + gb * _L0_ffn_ref(h, L0_ffn_router_w, L0_ffn_w1, L0_ffn_w2, L0_ffn_bias)
    return x

_drawn_inputs = setup_inputs


def setup_inputs(seed=0):
    import zlib

    import numpy as np

    out = dict(_drawn_inputs(seed))
    spreads = {'L0_ffn_bias': (0.0, 0.308)}
    factors = {'L0_attn_bqkv': 8.0,
     'L0_attn_bout': 8.0,
     'L0_ffn_router_w': 5.29,
     'L0_ffn_w1': 4.768,
     'L0_ffn_w2': 4.652}
    for name, (base, spread) in spreads.items():
        noise = np.random.default_rng([zlib.crc32(name.encode()), seed]).standard_normal(out[name].shape)
        drawn = base * np.exp(spread * noise) if base else spread * noise
        out[name] = jnp.asarray(drawn.astype(out[name].dtype))
    for name, factor in factors.items():
        out[name] = (out[name] * factor).astype(out[name].dtype)
    return out
```

```python
from contextlib import ExitStack

import concourse.bass as bass
from concourse import mybir

F32 = mybir.dt.float32
F32R = mybir.dt.float32r
BF16 = mybir.dt.bfloat16
U32 = mybir.dt.uint32
ALU = mybir.AluOpType
ACT = mybir.ActivationFunctionType
AX = mybir.AxisListType

P = 128
B, T, D = 16, 512, 256
J = T // P
C = D // P
E, K = 8, 2
F = 1024
FC = F // P
CAP = B * T // E
ROWS = K * E * CAP
NOROW = ROWS
S = K * E
BLK = 512
NB = CAP // BLK
GATES = 6
GA, CB, SB, GB, GABOUT, GBBIAS = range(GATES)
EPS = 1e-5


def adaln_moe_kernel(nc, x, Wqkv, bqkv, Wout, bout, router_w, w1, w2, ffn_bias, cond, wmod, out):
    x_rows = x.rearrange("b (p j) d -> b p j d", j=J)
    out_rows = out.rearrange("b (p j) d -> b p j d", j=J)
    gates_dram = nc.dram_tensor("gates_dram", (B, GATES * D), F32, kind="Internal").ap()
    resid_dram = nc.dram_tensor("resid_dram", (B, T, D), F32, kind="Internal").ap()
    expert_in = nc.dram_tensor("expert_in", (ROWS, D), F32, kind="Internal").ap()
    expert_out = nc.dram_tensor("expert_out", (ROWS + 1, D), F32, kind="Internal").ap()
    resid_rows = resid_dram.rearrange("b (p j) d -> b p j d", j=J)
    in_blocks = expert_in.rearrange("(m p j) d -> m p j d", p=P, j=J)
    out_blocks = expert_out[0:ROWS, :].rearrange("(m p j) d -> m p j d", p=P, j=J)

    with ExitStack() as whole:
        def tensors(ctx):
            def sb(name, shape, dt=F32):
                return ctx.enter_context(nc.sbuf_tensor(name, shape, dt))

            def ps(name, shape, dt=F32):
                return ctx.enter_context(nc.psum_tensor(name, shape, dt))

            def sem(name):
                return ctx.enter_context(nc.semaphore(name))

            return sb, ps, sem

        sb, _, _ = tensors(whole)
        ident = sb("ident", [P, P])
        logits_all = sb("logits_all", [P, B * J, E])
        top_all = sb("top_all", [P, B * J, K])
        row_all = sb("row_all", [P, B, J * K], U32)

        with ExitStack() as first:
            sb, ps, sem = tensors(first)
            attend_and_route(nc, sb, ps, sem, x_rows, Wqkv, bqkv, Wout, bout, router_w, ffn_bias, cond, wmod,
                             gates_dram, resid_rows, expert_in, expert_out,
                             ident, logits_all, top_all, row_all)
        with ExitStack() as second:
            sb, ps, sem = tensors(second)
            experts(nc, sb, ps, sem, w1, w2, in_blocks, out_blocks, ident)
        with ExitStack() as third:
            sb, ps, sem = tensors(third)
            combine(nc, sb, ps, sem, gates_dram, resid_rows, expert_out, out_rows,
                    logits_all, top_all, row_all)


def held(engine, passed):
    engine.sem_inc(passed, 1)


def attend_and_route(nc, sb, ps, sem, x_rows, Wqkv, bqkv, Wout, bout, router_w, ffn_bias, cond, wmod,
                     gates_dram, resid_rows, expert_in, expert_out,
                     ident, logits_all, top_all, row_all):
    cond_sb = sb("cond_sb", [B, D])
    silu_c = sb("silu_c", [B, D])
    silu_cT = sb("silu_cT", [P, C, B])
    wmod_sb = sb("wmod_sb", [P, C, 6 * D])
    mod_cols = sb("mod_cols", [P, 2 * C, B])
    neg_gate = sb("neg_gate", [B, 2, D])
    sign_gate = sb("sign_gate", [B, 2, D])
    gate_rows = sb("gate_rows", [B, GATES, D])
    bias_rows = sb("bias_rows", [B, 2, D])
    wqkv_sb = sb("wqkv_sb", [P, C, 3 * D])
    wqkv_hi = sb("wqkv_hi", [P, C, 3 * D], F32R)
    wqkv_lo = sb("wqkv_lo", [P, C, 3 * D], F32R)
    bq_cols = sb("bq_cols", [P, C])
    bkv_f = sb("bkv_f", [P, 2 * D])
    bkv_part = sb("bkv_part", [P, 2 * D])
    bkv_r = sb("bkv_r", [P, 2 * D], F32R)
    pick_r = sb("pick_r", [P, P], F32R)
    wout_sb = sb("wout_sb", [P, C, D])
    router_sb = sb("router_sb", [P, C, E])
    ones_f = sb("ones_f", [P, P])
    ones_b = sb("ones_b", [P, P], BF16)
    ident_b = sb("ident_b", [P, P], BF16)
    before_b = sb("before_b", [P, P], BF16)
    expert_no = sb("expert_no", [P, E])
    choice_base = sb("choice_base", [P, J, K])
    eps_col = sb("eps_col", [P, 1])
    zeros = sb("zeros", [P, 4096])
    xt = sb("xt", [P, 2, J, D])
    gates = sb("gates", [P, 2, GATES, D])
    st1 = sb("st1", [P, J, 6])
    mv1 = sb("mv1", [P, J, 2])
    sd1 = sb("sd1", [P, J])
    rs1 = sb("rs1", [P, J])
    xn = sb("xn", [P, J, D])
    hT = sb("hT", [P, C, T])
    hT_hi = sb("hT_hi", [P, C, T], F32R)
    hT_lo = sb("hT_lo", [P, C, T], F32R)
    k_sb = sb("k_sb", [P, J, D])
    k_sq = sb("k_sq", [P, D])
    kn2 = sb("kn2", [P, J])
    kn = sb("kn", [P, J])
    rk = sb("rk", [P, J])
    kv = sb("kv", [P, J, D])
    kv_cols = sb("kv_cols", [P, C])
    q_hi = sb("q_hi", [P, C, T], F32R)
    q_lo = sb("q_lo", [P, C, T], F32R)
    q_sq = sb("q_sq", [P, C, T])
    q_sq1 = sb("q_sq1", [P, T])
    qn = sb("qn", [P, J])
    rq = sb("rq", [P, J])
    wo_g = sb("wo_g", [P, C, D])
    wo_hi = sb("wo_hi", [P, C, D], F32R)
    wo_lo = sb("wo_lo", [P, C, D], F32R)
    xg = sb("xg", [P, J, D])
    x1 = sb("x1", [P, J, D])
    resid = sb("resid", [P, 2, J, D])
    st2 = sb("st2", [P, J, 6])
    mv2 = sb("mv2", [P, J, 2])
    sd2 = sb("sd2", [P, J])
    rs2 = sb("rs2", [P, J])
    h2c = sb("h2c", [P, J, D])
    h2 = sb("h2", [P, 2, J, D])
    h2T = sb("h2T", [P, C, T])
    logits = sb("logits", [P, J, E])
    top8 = sb("top8", [P, J, 8])
    top8_no = sb("top8_no", [P, J, 8], U32)
    chosen = sb("chosen", [P, J, K])
    onehot = sb("onehot", [P, J, K, E], BF16)
    rank_all = sb("rank_all", [P, J, K, E])
    rank_own = sb("rank_own", [P, J * K, E])
    rank = sb("rank", [P, J, K])
    over = sb("over", [P, J, K])
    row_in = sb("row_in", [P, J, K])
    row_f = sb("row_f", [P, J, K])
    row = sb("row", [P, 2, J * K], U32)
    seen = sb("seen", [P, K * E])

    ps_T = ps("ps_T", [P, C, T])
    ps_kv = ps("ps_kv", [P, 2, 2 * D])
    ps_qo = ps("ps_qo", [P, 2, T])
    ps_s = ps("ps_s", [P, 512])
    ps_m = ps("ps_m", [P, 512])
    ps_kvc, ps_qn = ps_s[:, 0:C], ps_m[:, 0:J]
    ps_log = ps_s[:, 32:32 + J * E]
    ps_rank = ps_m[:, 128:128 + (J + 1) * K * E].rearrange("p (j c) -> p j c", j=J + 1)
    ps_o = ps_qo[:, :, :].rearrange("p a (b d) -> p (a b) d", d=D)

    cond_in, wmod_in, bias_in, wqkv_in, bqkv_in, small_in = map(sem, "cond_in wmod_in bias_in wqkv_in bqkv_in small_in".split())
    zeros_out, gates_out, resid_out, zrow_out = [sem("zeros_out"), sem("gates_out"), [sem("resid_out0"), sem("resid_out1")], sem("zrow_out")]
    x_in = [sem("x_in0"), sem("x_in1")]
    gates_in = [sem("gates_in0"), sem("gates_in1")]
    scattered = [sem("scattered0"), sem("scattered1")]
    names = """ident0 ident1 consts0 consts1 consts2 silu_ready cT_ready cT_copied mod_ready cols_ready
      gate_neg gate_sign gate_sign1 gate_abs gate_min gates_ready wq_hi wq_lo bkv_hi bkv_ready zeros_ready rows_mod
      st1_ready mv1_ready sd1_ready rs1_ready xn_ready xT_ready hT_ready hhi_ready hlo_ready
      kv_done k_copied kn2_ready kn_ready rk_ready kv_ready kvc_done kvc_ready
      q_done qhi_ready qsq_ready qlo_ready qsq1_ready qn_done qn_ready rq_ready
      wog_ready wohi_ready wolo_ready o_done xg_ready x1_ready resid_ready
      st2_ready mv2_ready sd2_ready rs2_ready h2c_ready h2_ready h2T_done h2T_ready
      log_done log_ready log_kept top_ready topno_ready top_kept chosen_ready onehot_ready rank_done
      rankall_ready seen_ready own_ready rank_ready over_ready rowin_ready rowf_ready row_ready dve_passed pool_passed""".split()
    s = {n: sem(n) for n in names}

    with nc.Block() as block:

        def after(engine, name, count):
            if not (isinstance(count, int) and count <= 0):
                engine.wait_ge(s[name], count)

        def counts(engine, i):
            return [2 * i + c if isinstance(i, int) else engine.snap(2 * i + c) for c in range(5)]

        @block.sync
        def _(sp):
            sp.dma_start(cond_sb[:, :], cond).then_inc(cond_in, 16)
            sp.dma_start(wmod_sb[:, :, :], wmod.rearrange("(c p) n -> p c n", p=P)).then_inc(wmod_in, 16)
            sp.dma_start(bias_rows[:, 0, :], bout.unsqueeze(0).broadcast_to([B, D])).then_inc(bias_in, 16)
            sp.dma_start(bias_rows[:, 1, :], ffn_bias[0, 0:1, :].broadcast_to([B, D])).then_inc(bias_in, 16)
            sp.dma_start(wqkv_sb[:, :, :], Wqkv.rearrange("(c p) n -> p c n", p=P)).then_inc(wqkv_in, 16)
            sp.dma_start(bkv_f[:, :], bqkv[D:3 * D].unsqueeze(0).broadcast_to([P, 2 * D])).then_inc(bqkv_in, 16)
            sp.dma_start(wout_sb[:, :, :], Wout.rearrange("(c p) n -> p c n", p=P)).then_inc(small_in, 16)
            sp.dma_start(router_sb[:, :, :], router_w.rearrange("(c p) n -> p c n", p=P)).then_inc(small_in, 16)
            with nc.allow_non_contiguous_dma(reason="256 values, once"):
                sp.dma_start(bq_cols[:, :], bqkv[0:D].rearrange("(c p) -> p c", p=P)).then_inc(small_in, 16)

            def load_x(n, i, par):
                after(sp, "x1_ready", n - 1)
                after(sp, "xn_ready", n - 1)
                after(sp, "xg_ready", n - 1)
                sp.dma_start(xt[:, par], x_rows[n]).then_inc(x_in[par], 16)

            def load_gates(n, i, par):
                after(sp, "h2_ready", n - 1)
                after(sp, "resid_ready", n - 1)
                after(sp, "wog_ready", n - 1)
                sp.dma_start(gates[:, par], gates_dram[n].rearrange("(a g d) -> a g d", a=1, g=GATES)
                             .broadcast_to([P, GATES, D])).then_inc(gates_in[par], 16)

            def store_resid(n, i, par):
                after(sp, "resid_ready", n + 1)
                sp.dma_start(resid_rows[n], resid[:, par]).then_inc(resid_out[par], 16)

            load_x(0, 0, 0)
            load_x(1, 0, 1)
            sp.wait_ge(s["zeros_ready"], 1)
            per = 4096 // D
            for z in range(ROWS // (P * per)):
                sp.dma_start(expert_in[z * P * per:(z + 1) * P * per, :].rearrange("(p r) d -> p (r d)", p=P),
                             zeros[:, :]).then_inc(zeros_out, 16)
            sp.dma_start(expert_out[ROWS:ROWS + 1, :], zeros[0:1, 0:D]).then_inc(zrow_out, 16)
            sp.wait_ge(s["gates_ready"], 1)
            sp.dma_start(gates_dram, gate_rows[:, :, :].rearrange("b g d -> b (g d)")).then_inc(gates_out, 16)
            sp.wait_ge(gates_out, 16)
            load_gates(0, 0, 0)
            load_gates(1, 0, 1)

            def step(i, ahead=True):
                n = counts(sp, i)
                for par in (0, 1):
                    store_resid(n[par], i, par)
                    if ahead:
                        load_x(n[par + 2], i + 1, par)
                        load_gates(n[par + 2], i + 1, par)

            with sp.Fori(0, B // 2 - 1) as i:
                step(i)
            step(B // 2 - 1, ahead=False)
            sp.wait_ge(zrow_out, 16)
            for par in (0, 1):
                sp.wait_ge(resid_out[par], 16 * B // 2)

        @block.gpsimd
        def _(pool):
            pool.memset(zeros[:, :], 0.0).then_inc(s["zeros_ready"], 1)
            pool.memset(ident[:, :], 0.0)
            pool.memset(ident_b[:, :], 0.0)
            pool.memset(before_b[:, :], 1.0)
            pool.memset(ones_b[:, :], 1.0)
            pool.memset(ones_f[:, :], 1.0)
            pool.memset(eps_col[:, :], EPS)
            pool.memset(seen[:, :], 0.0)
            pool.memset(choice_base[:, :, 0], 0.0)
            pool.memset(choice_base[:, :, 1], float(E * CAP))
            pool.iota(expert_no[:, :], pattern=[[1, E]], base=0, channel_multiplier=0,
                      allow_small_or_imprecise_dtypes=True).then_inc(s["ident0"], 1)
            pool.wait_ge(s["ident0"], 1)
            for m in (ident, ident_b):
                pool.affine_select(out=m[:, :], in_=m[:, :], compare_op=ALU.not_equal, fill=1.0,
                                   base=0, pattern=[[-1, P]], channel_multiplier=1)
            pool.affine_select(out=before_b[:, :], in_=before_b[:, :], compare_op=ALU.is_gt, fill=0.0,
                               base=0, pattern=[[1, P]], channel_multiplier=-1).then_inc(s["consts0"], 1)

            def attention_side(n, i, par):
                pool.wait_ge(s["qsq_ready"], n + 1)
                after(pool, "qn_done", n)
                pool.tensor_tensor(q_sq1[:, :], q_sq[:, 0], q_sq[:, 1], ALU.add).then_inc(s["qsq1_ready"], 1)
                pool.wait_ge(x_in[par], 16 * i + 16)
                pool.wait_ge(gates_in[par], 16 * i + 16)
                after(pool, "x1_ready", n)
                pool.tensor_tensor(xg[:, :, :], xt[:, par],
                                   gates[:, par, GABOUT].unsqueeze(1).broadcast_to([P, J, D]),
                                   ALU.add).then_inc(s["xg_ready"], 1)

            def residual(n, i, par):
                pool.wait_ge(s["x1_ready"], n + 1)
                if not isinstance(i, int) or i > 0:
                    pool.wait_ge(resid_out[par], 16 * i)
                pool.tensor_tensor(resid[:, par], x1[:, :, :],
                                   gates[:, par, GBBIAS].unsqueeze(1).broadcast_to([P, J, D]),
                                   ALU.add).then_inc(s["resid_ready"], 1)

            def scatter(n, i, par):
                pool.wait_ge(s["row_ready"], n + 1)
                pool.wait_ge(s["h2_ready"], n + 1)
                held(pool, s["pool_passed"])
                for j in range(J):
                    for k in range(K):
                        at = row[:, par, j * K + k:j * K + k + 1]
                        pool.indirect_dma_start(out=expert_in,
                                                out_offset=bass.IndirectOffsetOnAxis(ap=at, axis=0),
                                                in_=h2[:, par, j], in_offset=None,
                                                bounds_check=ROWS - 1, oob_is_err=False
                                                ).then_inc(scattered[par], 16)

            def step(i, front=True):
                n = counts(pool, i)
                for par in (0, 1):
                    residual(n[par], i, par)
                    if front or par == 0:
                        attention_side(n[par + 1], i + (par + 1) // 2, (par + 1) % 2)
                    scatter(n[par], i, par)

            attention_side(0, 0, 0)
            pool.wait_ge(zeros_out, 16 * (ROWS // (P * (4096 // D))))
            with pool.Fori(0, B // 2 - 1) as i:
                step(i)
            step(B // 2 - 1, front=False)
            for par in (0, 1):
                pool.wait_ge(scattered[par], 16 * J * K * B // 2)

        @block.scalar
        def _(act):
            act.wait_ge(cond_in, 16)
            act.activation(silu_c[:, :], cond_sb[:, :], ACT.Silu).then_inc(s["silu_ready"], 1)
            act.wait_ge(s["cT_ready"], 1)
            act.activation(silu_cT[:, :, :], ps_m[:, 0:C * B].rearrange("p (c b) -> p c b", c=C),
                           ACT.Copy).then_inc(s["cT_copied"], 1)
            act.wait_ge(s["consts0"], 1)
            act.wait_ge(small_in, 48)

            def deviation(n, stats, sd, name, waited):
                act.wait_ge(s[waited], n + 1)
                act.activation(sd[:, :], stats[:, :, 1], ACT.Sqrt, bias=eps_col[:, 0:1]).then_inc(s[name], 1)

            def normed(n, i, par):
                deviation(n, mv1, sd1, "sd1_ready", "mv1_ready")

            def front_h(n, i, par):
                act.wait_ge(s["xT_ready"], n + 1)
                after(act, "hlo_ready", n)
                for c in range(C):
                    last = act.activation(hT[:, c], ps_T[:, c], ACT.Identity,
                                          scale=mod_cols[:, C + c, bass.ds(n, 1)],
                                          bias=mod_cols[:, c, bass.ds(n, 1)])
                last.then_inc(s["hT_ready"], 1)
                act.wait_ge(s["hT_ready"], n + 1)
                after(act, "q_done", n)
                act.activation(hT_hi[:, :, :], hT[:, :, :], ACT.Copy).then_inc(s["hhi_ready"], 1)

            def front_k(n, i, par):
                after(act, "kv_ready", J * n)
                for j in range(J):
                    act.wait_ge(s["kv_done"], J * n + j + 1)
                    act.activation(k_sb[:, j], ps_kv[:, j % 2, 0:D], ACT.Copy).then_inc(s["k_copied"], 1)
                    act.wait_ge(s["k_copied"], J * n + j + 1)
                    act.activation(k_sq[:, :], k_sb[:, j], ACT.Square,
                                   accum_out=kn2[:, j:j + 1]).then_inc(s["kn2_ready"], 1)
                act.wait_ge(s["kn2_ready"], J * n + J)
                after(act, "rk_ready", n)
                act.activation(kn[:, :], kn2[:, :], ACT.Sqrt).then_inc(s["kn_ready"], 1)

            def front_q(n, i, par):
                act.wait_ge(s["q_done"], n + 1)
                after(act, "o_done", n)
                for c in range(C):
                    last = act.activation(q_hi[:, c], ps_qo[:, c], ACT.Identity, bias=bq_cols[:, c:c + 1])
                last.then_inc(s["qhi_ready"], 1)
                after(act, "qsq1_ready", n)
                for c in range(C):
                    last = act.activation(q_sq[:, c], ps_qo[:, c], ACT.Square, bias=bq_cols[:, c:c + 1])
                last.then_inc(s["qsq_ready"], 1)

            def front_w(n, i, par):
                act.wait_ge(s["wog_ready"], n + 1)
                after(act, "o_done", n)
                act.activation(wo_hi[:, :, :], wo_g[:, :, :], ACT.Copy).then_inc(s["wohi_ready"], 1)
                act.wait_ge(s["qn_done"], n + 1)
                after(act, "rq_ready", n)
                act.activation(qn[:, :], ps_qn, ACT.Sqrt).then_inc(s["qn_ready"], 1)

            def back_sd(n, i, par):
                deviation(n, mv2, sd2, "sd2_ready", "mv2_ready")

            def back_h2(n, i, par):
                act.wait_ge(s["h2T_done"], n + 1)
                after(act, "log_done", n)
                act.activation(h2T[:, :, :], ps_T[:, :, :], ACT.Copy).then_inc(s["h2T_ready"], 1)

            act.wait_ge(s["cols_ready"], 1)
            normed(0, 0, 0)
            front_h(0, 0, 0)
            front_k(0, 0, 0)
            front_q(0, 0, 0)
            normed(1, 0, 1)
            front_w(0, 0, 0)

            def step(i, last=False):
                n = counts(act, i)
                for par in (0, 1):
                    nxt = (n[par + 1], i + (par + 1) // 2, (par + 1) % 2)
                    front = not (last and par == 1)
                    if front:
                        front_h(*nxt)
                    back_sd(n[par], i, par)
                    if front:
                        front_k(*nxt)
                    back_h2(n[par], i, par)
                    if front:
                        front_q(*nxt)
                    if not last:
                        normed(n[par + 2], i + 1, par)
                    if front:
                        front_w(*nxt)

            with act.Fori(0, B // 2 - 1) as i:
                step(i)
            step(B // 2 - 1, last=True)

        @block.tensor
        def _(pe):
            pe.wait_ge(s["consts0"], 1)
            pe.wait_ge(s["silu_ready"], 1)
            for c in range(C):
                last = pe.transpose(ps_m[:, c * B:(c + 1) * B], silu_c[:, c * P:(c + 1) * P], ident[0:B, 0:B])
            last.then_inc(s["cT_ready"], 1)
            pe.wait_ge(s["cT_copied"], 1)
            pe.wait_ge(wmod_in, 16)
            for m in range(2 * C):
                for c in range(C):
                    last = pe.matmul(ps_m[:, m * B:(m + 1) * B], wmod_sb[:, c, m * P:(m + 1) * P],
                                     silu_cT[:, c], start=(c == 0), stop=(c == C - 1))
            last.then_inc(s["mod_ready"], 1)
            for m, (bank, lo, hi) in enumerate(((ps_T[:, 0], 2, 3), (ps_T[:, 1], 3, 5), (ps_qo[:, 0], 5, 6))):
                for c in range(C):
                    last = pe.matmul(bank[0:B, 0:(hi - lo) * D], silu_cT[:, c], wmod_sb[:, c, lo * D:hi * D],
                                     start=(c == 0), stop=(c == C - 1))
            last.then_inc(s["rows_mod"], 1)
            pe.wait_ge(s["wq_lo"], 1)
            pe.wait_ge(s["bkv_ready"], 1)
            pe.wait_ge(s["gates_ready"], 1)

            def front_T(n, i, par):
                pe.wait_ge(s["xn_ready"], n + 1)
                for j in range(J):
                    for c in range(C):
                        last = pe.transpose(ps_T[:, c, j * P:(j + 1) * P], xn[:, j, c * P:(c + 1) * P], ident[:, :])
                last.then_inc(s["xT_ready"], 1)

            def front_kv(n, i, par):
                pe.wait_ge(s["hlo_ready"], n + 1)
                pe.wait_ge(s["hhi_ready"], n + 1)
                for j in range(J):
                    after(pe, "kv_ready", J * n + j - 1)
                    to = ps_kv[:, j % 2]
                    pe.matmul(to, pick_r[:, :], bkv_r[:, :], start=True, stop=False)
                    tok = slice(j * P, (j + 1) * P)
                    for c in range(C):
                        pe.matmul(to, hT_hi[:, c, tok], wqkv_hi[:, c, D:3 * D], start=False, stop=False)
                        pe.matmul(to, hT_hi[:, c, tok], wqkv_lo[:, c, D:3 * D], start=False, stop=False)
                        last = pe.matmul(to, hT_lo[:, c, tok], wqkv_hi[:, c, D:3 * D],
                                         start=False, stop=(c == C - 1))
                    last.then_inc(s["kv_done"], 1)

            def front_q(n, i, par):
                after(pe, "x1_ready", n)
                for m in range(C):
                    to = ps_qo[:, m]
                    feat = slice(m * P, (m + 1) * P)
                    for c in range(C):
                        pe.matmul(to, wqkv_hi[:, c, feat], hT_hi[:, c], start=(c == 0), stop=False)
                        pe.matmul(to, wqkv_hi[:, c, feat], hT_lo[:, c], start=False, stop=False)
                        last = pe.matmul(to, wqkv_lo[:, c, feat], hT_hi[:, c], start=False, stop=(c == C - 1))
                last.then_inc(s["q_done"], 1)

            def front_sums(n, i, par):
                pe.wait_ge(s["rk_ready"], n + 1)
                pe.wait_ge(s["kv_ready"], J * n + J)
                after(pe, "log_ready", n)
                for c in range(C):
                    for j in range(J):
                        last = pe.matmul(ps_kvc[:, c:c + 1], kv[:, j, c * P:(c + 1) * P], rk[:, j:j + 1],
                                         start=(j == 0), stop=(j == J - 1))
                last.then_inc(s["kvc_done"], 1)
                pe.wait_ge(s["qsq1_ready"], n + 1)
                after(pe, "seen_ready", n - 1)
                for j in range(J):
                    last = pe.matmul(ps_qn[:, j:j + 1], q_sq1[:, j * P:(j + 1) * P], ones_f[:, 0:1],
                                     start=True, stop=True)
                last.then_inc(s["qn_done"], 1)

            def back_o(n, i, par):
                pe.wait_ge(s["wolo_ready"], n + 1)
                pe.wait_ge(s["wohi_ready"], n + 1)
                pe.wait_ge(s["qlo_ready"], n + 1)
                pe.wait_ge(s["qsq_ready"], n + 1)
                pe.wait_ge(s["qhi_ready"], n + 1)
                for j in range(J):
                    tok = slice(j * P, (j + 1) * P)
                    for c in range(C):
                        pe.matmul(ps_o[:, j], q_hi[:, c, tok], wo_hi[:, c], start=(c == 0), stop=False)
                        pe.matmul(ps_o[:, j], q_hi[:, c, tok], wo_lo[:, c], start=False, stop=False)
                        last = pe.matmul(ps_o[:, j], q_lo[:, c, tok], wo_hi[:, c], start=False, stop=(c == C - 1))
                last.then_inc(s["o_done"], 1)

            def back_T(n, i, par):
                pe.wait_ge(s["h2_ready"], n + 1)
                for j in range(J):
                    for c in range(C):
                        last = pe.transpose(ps_T[:, c, j * P:(j + 1) * P], h2[:, par, j, c * P:(c + 1) * P],
                                            ident[:, :])
                last.then_inc(s["h2T_done"], 1)

            def back_logits(n, i, par):
                pe.wait_ge(s["h2T_ready"], n + 1)
                pe.wait_ge(s["kvc_ready"], n + 1)
                for j in range(J):
                    for c in range(C):
                        last = pe.matmul(ps_log[:, j * E:(j + 1) * E], h2T[:, c, j * P:(j + 1) * P],
                                         router_sb[:, c], start=(c == 0), stop=(c == C - 1))
                last.then_inc(s["log_done"], 1)

            def back_ranks(n, i, par, front):
                pe.wait_ge(s["onehot_ready"], n + 1)
                pe.wait_ge(s["qn_ready"], n + 2 if front else n + 1)
                hot = onehot[:, :, :, :].rearrange("p j k e -> p j (k e)")
                for j in range(J):
                    pe.matmul(ps_rank[:, J], ones_b[:, :], hot[:, j], start=(j == 0), stop=(j == J - 1))
                for j in range(J):
                    pe.matmul(ps_rank[:, 0:J], before_b[:, :],
                              hot[:, j].unsqueeze(1).broadcast_to([P, J, K * E]), start=(j == 0), stop=False)
                for j in range(J - 1):
                    last = pe.matmul(ps_rank[:, j + 1:J], ident_b[:, :],
                                     hot[:, j].unsqueeze(1).broadcast_to([P, J - 1 - j, K * E]),
                                     start=False, stop=(j == J - 2))
                last.then_inc(s["rank_done"], 1)

            front_T(0, 0, 0)
            front_kv(0, 0, 0)
            front_q(0, 0, 0)
            front_sums(0, 0, 0)

            def step(i, last=False):
                n = counts(pe, i)
                for par in (0, 1):
                    nxt = (n[par + 1], i + (par + 1) // 2, (par + 1) % 2)
                    front = not (last and par == 1)
                    back_o(n[par], i, par)
                    if front:
                        pe.wait_ge(s["h2T_ready"], n[par])
                        front_T(*nxt)
                        front_kv(*nxt)
                        pe.wait_ge(s["hT_ready"], n[par + 1] + 1)
                    back_T(n[par], i, par)
                    if front:
                        front_q(*nxt)
                    back_logits(n[par], i, par)
                    if front:
                        front_sums(*nxt)
                    back_ranks(n[par], i, par, front)

            with pe.Fori(0, B // 2 - 1) as i:
                step(i)
            step(B // 2 - 1, last=True)

        @block.vector
        def _(dve):
            dve.wait_ge(s["mod_ready"], 1)
            dve.tensor_copy(mod_cols[:, 0:C], ps_m[:, 0:C * B].rearrange("p (c b) -> p c b", c=C))
            dve.tensor_scalar(mod_cols[:, C:2 * C], ps_m[:, C * B:2 * C * B].rearrange("p (c b) -> p c b", c=C),
                              1.0, None, ALU.add).then_inc(s["cols_ready"], 1)
            dve.wait_ge(s["rows_mod"], 1)
            gate_banks = (ps_T[0:B, 0, 0:D], ps_qo[0:B, 0, 0:D])
            for g in range(2):
                dve.tensor_scalar(neg_gate[:, g], gate_banks[g], -1.0, None, ALU.mult)
                last = dve.tensor_scalar(sign_gate[:, g], gate_banks[g], 0.0, 2.0, ALU.is_ge, ALU.mult)
            last.then_inc(s["gate_sign"], 1)
            dve.wait_ge(s["gate_sign"], 1)
            for g in range(2):
                dve.tensor_tensor(neg_gate[:, g], gate_banks[g], neg_gate[:, g], ALU.max)
                last = dve.tensor_scalar(sign_gate[:, g], sign_gate[:, g], -1.0, None, ALU.add)
            last.then_inc(s["gate_abs"], 1)
            dve.wait_ge(s["gate_abs"], 1)
            for g, to in enumerate((GA, GB)):
                dve.scalar_tensor_tensor(gate_rows[:, to], neg_gate[:, g], 0.25, sign_gate[:, g], ALU.max, ALU.mult)
            dve.tensor_copy(gate_rows[:, SB], ps_T[0:B, 1, 0:D])
            dve.tensor_scalar(gate_rows[:, CB], ps_T[0:B, 1, D:2 * D], 1.0, None, ALU.add).then_inc(s["gate_min"], 1)
            dve.wait_ge(s["gate_min"], 1)
            dve.wait_ge(bias_in, 32)
            dve.tensor_tensor(gate_rows[:, GABOUT], gate_rows[:, GA], bias_rows[:, 0], ALU.mult)
            dve.tensor_tensor(gate_rows[:, GBBIAS], gate_rows[:, GB], bias_rows[:, 1],
                              ALU.mult).then_inc(s["gates_ready"], 1)
            dve.wait_ge(wqkv_in, 16)
            dve.tensor_copy(wqkv_hi[:, :, :], wqkv_sb[:, :, :]).then_inc(s["wq_hi"], 1)
            dve.wait_ge(s["wq_hi"], 1)
            dve.tensor_tensor(wqkv_lo[:, :, :], wqkv_sb[:, :, :], wqkv_hi[:, :, :].bitcast(F32),
                              ALU.subtract).then_inc(s["wq_lo"], 1)
            dve.wait_ge(bqkv_in, 16)
            dve.memset(bkv_part[:, :], 0.0)
            dve.tensor_copy(bkv_r[:, :], bkv_f[:, :]).then_inc(s["bkv_hi"], 1)
            dve.wait_ge(s["bkv_hi"], 1)
            dve.tensor_tensor(bkv_f[:, :], bkv_f[:, :], bkv_r[:, :].bitcast(F32), ALU.subtract)
            dve.tensor_copy(bkv_part[0:1, :], bkv_r[0:1, :].bitcast(F32)).then_inc(s["bkv_hi"], 1)
            dve.wait_ge(s["bkv_hi"], 2)
            dve.tensor_copy(bkv_part[32:33, :], bkv_f[32:33, :]).then_inc(s["bkv_hi"], 1)
            dve.wait_ge(s["bkv_hi"], 3)
            dve.tensor_copy(bkv_r[:, :], bkv_part[:, :]).then_inc(s["bkv_hi"], 1)
            dve.memset(k_sb[:, 0, 0:P], 0.0).then_inc(s["consts1"], 1)
            dve.wait_ge(s["consts1"], 1)
            dve.memset(k_sb[0:1, 0, 0:P], 1.0)
            dve.memset(k_sb[32:33, 0, 0:P], 1.0).then_inc(s["consts1"], 1)
            dve.wait_ge(s["consts1"], 2)
            dve.tensor_copy(pick_r[:, :], k_sb[:, 0, 0:P]).then_inc(s["bkv_ready"], 1)
            dve.wait_ge(s["consts0"], 1)
            dve.wait_ge(small_in, 48)

            def ln1_stats(n, i, par):
                dve.wait_ge(x_in[par], 16 * i + 16)
                after(dve, "mv1_ready", n)
                for j in range(J):
                    last = dve.bn_stats(st1[:, j], xt[:, par, j])
                last.then_inc(s["st1_ready"], 1)
                dve.wait_ge(s["st1_ready"], n + 1)
                after(dve, "sd1_ready", n)
                after(dve, "xn_ready", n)
                held(dve, s["dve_passed"])
                for j in range(J):
                    last = dve.bn_aggr(mv1[:, j], st1[:, j])
                last.then_inc(s["mv1_ready"], 1)

            def ln1(n, i, par):
                dve.wait_ge(s["sd1_ready"], n + 1)
                dve.reciprocal(rs1[:, :], sd1[:, :]).then_inc(s["rs1_ready"], 1)
                dve.wait_ge(s["rs1_ready"], n + 1)
                after(dve, "xT_ready", n)
                for j in range(J):
                    last = dve.tensor_scalar(xn[:, j], xt[:, par, j], mv1[:, j, 0:1], rs1[:, j:j + 1],
                                             ALU.subtract, ALU.mult)
                last.then_inc(s["xn_ready"], 1)

            def h_lo(n, i, par):
                dve.wait_ge(s["hhi_ready"], n + 1)
                after(dve, "q_done", n)
                dve.tensor_tensor(hT_lo[:, :, :], hT[:, :, :], hT_hi[:, :, :].bitcast(F32),
                                  ALU.subtract).then_inc(s["hlo_ready"], 1)

            def kv_product(n, i, par):
                after(dve, "kvc_done", n)
                for j in range(J):
                    dve.wait_ge(s["k_copied"], J * n + j + 1)
                    dve.tensor_tensor(kv[:, j], ps_kv[:, j % 2, D:2 * D], k_sb[:, j],
                                      ALU.mult).then_inc(s["kv_ready"], 1)
                dve.wait_ge(s["kn_ready"], n + 1)
                dve.reciprocal(rk[:, :], kn[:, :]).then_inc(s["rk_ready"], 1)

            def q_rest(n, i, par):
                dve.wait_ge(s["qsq_ready"], n + 1)
                after(dve, "o_done", n)
                for c in range(C):
                    last = dve.scalar_tensor_tensor(q_lo[:, c], ps_qo[:, c], bq_cols[:, c:c + 1],
                                                    q_hi[:, c].bitcast(F32), ALU.add, ALU.subtract)
                last.then_inc(s["qlo_ready"], 1)

            def gated_weights(n, i, par):
                dve.wait_ge(s["kvc_done"], n + 1)
                dve.wait_ge(gates_in[par], 16 * i + 16)
                dve.tensor_copy(kv_cols[:, :], ps_kvc).then_inc(s["kvc_ready"], 1)
                dve.wait_ge(s["kvc_ready"], n + 1)
                after(dve, "wohi_ready", n)
                after(dve, "wolo_ready", n)
                for c in range(C):
                    last = dve.scalar_tensor_tensor(wo_g[:, c], wout_sb[:, c], kv_cols[:, c:c + 1],
                                                    gates[:, par, GA], ALU.mult, ALU.mult)
                last.then_inc(s["wog_ready"], 1)
                dve.wait_ge(s["wohi_ready"], n + 1)
                after(dve, "o_done", n)
                dve.tensor_tensor(wo_lo[:, :, :], wo_g[:, :, :], wo_hi[:, :, :].bitcast(F32),
                                  ALU.subtract).then_inc(s["wolo_ready"], 1)
                dve.wait_ge(s["qn_ready"], n + 1)
                dve.reciprocal(rq[:, :], qn[:, :]).then_inc(s["rq_ready"], 1)

            def attended(n, i, par):
                dve.wait_ge(s["o_done"], n + 1)
                dve.wait_ge(s["xg_ready"], n + 1)
                dve.wait_ge(s["rq_ready"], n + 1)
                after(dve, "resid_ready", n)
                after(dve, "h2c_ready", n)
                for j in range(J):
                    last = dve.scalar_tensor_tensor(x1[:, j], ps_o[:, j], rq[:, j:j + 1], xg[:, j],
                                                    ALU.mult, ALU.add)
                last.then_inc(s["x1_ready"], 1)

            def ln2_stats(n, i, par):
                dve.wait_ge(s["x1_ready"], n + 1)
                after(dve, "mv2_ready", n)
                for j in range(J):
                    last = dve.bn_stats(st2[:, j], x1[:, j])
                last.then_inc(s["st2_ready"], 1)
                dve.wait_ge(s["st2_ready"], n + 1)
                after(dve, "sd2_ready", n)
                held(dve, s["dve_passed"])
                for j in range(J):
                    last = dve.bn_aggr(mv2[:, j], st2[:, j])
                last.then_inc(s["mv2_ready"], 1)

            def modulated(n, i, par):
                dve.wait_ge(s["sd2_ready"], n + 1)
                dve.reciprocal(rs2[:, :], sd2[:, :]).then_inc(s["rs2_ready"], 1)
                after(dve, "h2_ready", n)
                for j in range(J):
                    last = dve.scalar_tensor_tensor(h2c[:, j], x1[:, j], mv2[:, j, 0:1], gates[:, par, CB],
                                                    ALU.subtract, ALU.mult)
                last.then_inc(s["h2c_ready"], 1)
                dve.wait_ge(s["rs2_ready"], n + 1)
                dve.wait_ge(s["h2c_ready"], n + 1)
                if not isinstance(i, int) or i > 0:
                    dve.wait_ge(scattered[par], 16 * J * K * i)
                for j in range(J):
                    last = dve.scalar_tensor_tensor(h2[:, par, j], h2c[:, j], rs2[:, j:j + 1], gates[:, par, SB],
                                                    ALU.mult, ALU.add)
                last.then_inc(s["h2_ready"], 1)

            def choose(n, i, par):
                dve.wait_ge(s["log_done"], n + 1)
                after(dve, "topno_ready", n)
                dve.tensor_copy(logits[:, :, :], ps_log.rearrange("p (j e) -> p j e", j=J)).then_inc(s["log_ready"], 1)
                dve.wait_ge(s["log_ready"], n + 1)
                dve.tensor_copy(logits_all[:, bass.ds(J * n, J), :], logits[:, :, :])
                after(dve, "top_kept", n)
                held(dve, s["dve_passed"])
                for j in range(J):
                    last = dve.max(top8[:, j], logits[:, j])
                last.then_inc(s["top_ready"], 1)
                dve.wait_ge(s["top_ready"], n + 1)
                dve.tensor_copy(top_all[:, bass.ds(J * n, J), :], top8[:, :, 0:K]).then_inc(s["top_kept"], 1)
                after(dve, "chosen_ready", n)
                held(dve, s["dve_passed"])
                for j in range(J):
                    last = dve.max_index(top8_no[:, j], top8[:, j], logits[:, j])
                last.then_inc(s["topno_ready"], 1)
                dve.wait_ge(s["topno_ready"], n + 1)
                after(dve, "rowin_ready", n)
                dve.tensor_copy(chosen[:, :, :], top8_no[:, :, 0:K]).then_inc(s["chosen_ready"], 1)
                dve.wait_ge(s["chosen_ready"], n + 1)
                after(dve, "rank_done", n)
                after(dve, "own_ready", n)
                dve.tensor_tensor(onehot[:, :, :, :].rearrange("p j k e -> p (j k) e"),
                                  expert_no[:, :].unsqueeze(1).broadcast_to([P, J * K, E]),
                                  chosen[:, :, :].rearrange("p j k -> p (j k)").unsqueeze(2)
                                  .broadcast_to([P, J * K, E]), ALU.is_equal).then_inc(s["onehot_ready"], 1)

            def rows(n, i, par):
                dve.wait_ge(s["rank_done"], n + 1)
                after(dve, "own_ready", n)
                after(dve, "seen_ready", n)
                dve.tensor_tensor(rank_all[:, :, :, :].rearrange("p j k e -> p j (k e)"), ps_rank[:, 0:J],
                                  seen[:, :].unsqueeze(1).broadcast_to([P, J, K * E]),
                                  ALU.add).then_inc(s["rankall_ready"], 1)
                dve.wait_ge(s["rankall_ready"], n + 1)
                dve.tensor_tensor(seen[:, :], ps_rank[:, J], seen[:, :], ALU.add).then_inc(s["seen_ready"], 1)
                after(dve, "rank_ready", n)
                dve.tensor_tensor(rank_own[:, :, :], rank_all[:, :, :, :].rearrange("p j k e -> p (j k) e"),
                                  onehot[:, :, :, :].rearrange("p j k e -> p (j k) e"),
                                  ALU.mult).then_inc(s["own_ready"], 1)
                dve.wait_ge(s["own_ready"], n + 1)
                after(dve, "rowf_ready", n)
                dve.tensor_reduce(rank[:, :, :].rearrange("p j k -> p (j k)"), rank_own[:, :, :], AX.X,
                                  ALU.add).then_inc(s["rank_ready"], 1)
                dve.wait_ge(s["rank_ready"], n + 1)
                dve.tensor_scalar(over[:, :, :], rank[:, :, :], float(CAP), float(2 * ROWS), ALU.is_ge, ALU.mult)
                dve.scalar_tensor_tensor(row_in[:, :, :], chosen[:, :, :], float(CAP), choice_base[:, :, :],
                                         ALU.mult, ALU.add).then_inc(s["rowin_ready"], 1)
                dve.wait_ge(s["rowin_ready"], n + 1)
                dve.tensor_tensor(over[:, :, :], over[:, :, :], rank[:, :, :], ALU.add).then_inc(s["over_ready"], 1)
                dve.wait_ge(s["over_ready"], n + 1)
                after(dve, "row_ready", n)
                dve.tensor_tensor(row_f[:, :, :], over[:, :, :], row_in[:, :, :], ALU.add).then_inc(s["rowf_ready"], 1)
                dve.wait_ge(s["rowf_ready"], n + 1)
                if not isinstance(i, int) or i > 0:
                    dve.wait_ge(scattered[par], 16 * J * K * i)
                last_row = row_f[:, :, :].rearrange("p j k -> p (j k)")
                dve.tensor_scalar(row[:, par], last_row, float(NOROW), None, ALU.min)
                dve.tensor_scalar(row_all[:, bass.ds(n, 1), :].rearrange("p a c -> p (a c)"), last_row,
                                  float(NOROW), None, ALU.min).then_inc(s["row_ready"], 1)

            ln1_stats(0, 0, 0)
            ln1(0, 0, 0)
            h_lo(0, 0, 0)
            ln1_stats(1, 0, 1)
            kv_product(0, 0, 0)
            q_rest(0, 0, 0)
            ln1(1, 0, 1)
            gated_weights(0, 0, 0)

            def step(i, last=False):
                n = counts(dve, i)
                for par in (0, 1):
                    nxt = (n[par + 1], i + (par + 1) // 2, (par + 1) % 2)
                    front = not (last and par == 1)
                    attended(n[par], i, par)
                    ln2_stats(n[par], i, par)
                    if front:
                        h_lo(*nxt)
                    modulated(n[par], i, par)
                    if front:
                        kv_product(*nxt)
                    if not last:
                        ln1_stats(n[par + 2], i + 1, par)
                    if front:
                        q_rest(*nxt)
                    if not last:
                        ln1(n[par + 2], i + 1, par)
                    choose(n[par], i, par)
                    if front:
                        gated_weights(*nxt)
                    rows(n[par], i, par)

            with dve.Fori(0, B // 2 - 1) as i:
                step(i)
            step(B // 2 - 1, last=True)


def experts(nc, sb, ps, sem, w1, w2, in_blocks, out_blocks, ident):
    w1_raw = sb("w1_raw", [P, C, F])
    w2_raw = sb("w2_raw", [P, FC, D])
    w1_hi = sb("w1_hi", [P, 2, C, F], F32R)
    w1_lo = sb("w1_lo", [P, 2, C, F], F32R)
    w2_hi = sb("w2_hi", [P, 2, FC, D], F32R)
    w2_lo = sb("w2_lo", [P, 2, FC, D], F32R)
    xin = sb("xin", [P, 2, J, D])
    xT_hi = sb("xT_hi", [P, 2, C, BLK], F32R)
    xT_lo = sb("xT_lo", [P, 2, C, BLK], F32R)
    g = sb("g", [P, 2, 2, BLK])
    g_hi = sb("g_hi", [P, 2, FC, BLK], F32R)
    g_lo = sb("g_lo", [P, 2, FC, BLK], F32R)
    y = sb("y", [P, 2, J, D])
    ps_x = ps("ps_x", [P, C, BLK])
    ps_h = ps("ps_h", [P, 2, 2, BLK])
    ps_y = ps("ps_y", [P, 2, 512])
    PAIRS = FC // 2
    M = S * NB

    w1_in, w2_in, passed = sem("w1_in"), sem("w2_in"), sem("w_passed")
    w1hi_ready, w1lo_ready, w2hi_ready, w2lo_ready = map(sem, "w1hi_ready w1lo_ready w2hi_ready w2lo_ready".split())
    xin_in = [sem("xin_in0"), sem("xin_in1")]
    y_out = [sem("y_out0"), sem("y_out1")]
    xT_done, xhi_ready, xlo_ready, h_done, g_ready, ghi_ready, glo_ready, y_done, y_ready = map(
        sem, "xT_done xhi_ready xlo_ready h_done g_ready ghi_ready glo_ready y_done y_ready".split())

    with nc.Block() as block:

        def after(engine, what, count):
            if not (isinstance(count, int) and count <= 0):
                engine.wait_ge(what, count)

        @block.sync
        def _(sp):
            def load_weights(s, e):
                after(sp, w1lo_ready, s)
                after(sp, w2lo_ready, s)
                sp.dma_start(w1_raw[:, :, :], w1[e].rearrange("(c p) f -> p c f", p=P)).then_inc(w1_in, 16)
                sp.dma_start(w2_raw[:, :, :], w2[e].rearrange("(c p) d -> p c d", p=P)).then_inc(w2_in, 16)

            def load_block(m, i, par):
                after(sp, xT_done, m - 1)
                sp.dma_start(xin[:, par], in_blocks[m]).then_inc(xin_in[par], 16)

            def store_block(m, par):
                sp.wait_ge(y_ready, J * m + J)
                sp.dma_start(out_blocks[m], y[:, par]).then_inc(y_out[par], 16)

            load_block(0, 0, 0)
            load_weights(0, 0)
            load_block(1, 0, 1)
            load_weights(1, 1)

            def turn(i, last=False):
                m = 4 * i if isinstance(i, int) else sp.snap(4 * i)
                for b in range(4):
                    if not (last and b >= 2):
                        load_block(m + b + 2, 0, b % 2)
                    if b % 2 == 0 and not last:
                        load_weights(2 * i + 2 + b // 2, (2 * i + 2 + b // 2) % E)
                    if not (isinstance(i, int) and i == 0 and b == 0):
                        store_block(m + b - 1, (b - 1) % 2)

            turn(0)
            with sp.Fori(1, M // 4 - 1) as i:
                turn(i)
            turn(M // 4 - 1, last=True)
            store_block(M - 1, (M - 1) % 2)
            for par in (0, 1):
                sp.wait_ge(y_out[par], 16 * M // 2)

        @block.gpsimd
        def _(pool):
            def split(s, par, guard):
                pool.wait_ge(w1_in, 16 * s + 16)
                if guard:
                    pool.wait_ge(h_done, (s - 1) * NB * PAIRS)
                    held(pool, passed)
                pool.tensor_copy(w1_hi[:, par], w1_raw[:, :, :]).then_inc(w1hi_ready, 1)
                pool.wait_ge(w1hi_ready, s + 1)
                pool.tensor_tensor(w1_lo[:, par], w1_raw[:, :, :], w1_hi[:, par].bitcast(F32),
                                   ALU.subtract).then_inc(w1lo_ready, 1)
                pool.wait_ge(w2_in, 16 * s + 16)
                if guard:
                    pool.wait_ge(y_done, (s - 1) * NB * J)
                    held(pool, passed)
                pool.tensor_copy(w2_hi[:, par], w2_raw[:, :, :]).then_inc(w2hi_ready, 1)
                pool.wait_ge(w2hi_ready, s + 1)
                pool.tensor_tensor(w2_lo[:, par], w2_raw[:, :, :], w2_hi[:, par].bitcast(F32),
                                   ALU.subtract).then_inc(w2lo_ready, 1)

            split(0, 0, False)
            split(1, 1, False)
            with pool.Fori(1, S // 2) as i:
                split(2 * i, 0, True)
                split(2 * i + 1, 1, True)

        @block.scalar
        def _(act):
            def x_hi(m, par):
                act.wait_ge(xT_done, m + 1)
                after(act, h_done, PAIRS * (m - 1))
                act.activation(xT_hi[:, par], ps_x[:, :, :], ACT.Copy).then_inc(xhi_ready, 1)

            def gelu(m, par, q):
                act.wait_ge(h_done, PAIRS * m + q + 1)
                after(act, glo_ready, PAIRS * m + q - 1)
                act.activation(g[:, q % 2], ps_h[:, q % 2], ACT.Gelu_apprx_tanh).then_inc(g_ready, 1)
                act.wait_ge(g_ready, PAIRS * m + q + 1)
                if q == 0:
                    after(act, y_done, J * (m - 1))
                act.activation(g_hi[:, par, 2 * q:2 * q + 2], g[:, q % 2], ACT.Copy).then_inc(ghi_ready, 1)

            x_hi(0, 0)

            def block_of(m, par, last=False):
                for q in range(PAIRS):
                    gelu(m, par, q)
                    if q == 1 and not last:
                        x_hi(m + 1, 1 - par)

            block_of(0, 0)
            block_of(1, 1)
            with act.Fori(1, M // 2 - 1) as i:
                block_of(2 * i, 0)
                block_of(2 * i + 1, 1)
            block_of(M - 2, 0)
            block_of(M - 1, 1, last=True)

        @block.tensor
        def _(pe):
            def turn_x(m, i, par):
                pe.wait_ge(xin_in[par], 16 * i + 16)
                after(pe, xhi_ready, m)
                after(pe, xlo_ready, m)
                for j in range(J):
                    for c in range(C):
                        last = pe.transpose(ps_x[:, c, j * P:(j + 1) * P], xin[:, par, j, c * P:(c + 1) * P],
                                            ident[:, :])
                last.then_inc(xT_done, 1)

            def hidden(m, par, w, q):
                if q == 0:
                    pe.wait_ge(xhi_ready, m + 1)
                    pe.wait_ge(xlo_ready, m + 1)
                after(pe, g_ready, PAIRS * m + q - 1)
                for f in (2 * q, 2 * q + 1):
                    to = ps_h[:, q % 2, f % 2]
                    fs = slice(f * P, (f + 1) * P)
                    for c in range(C):
                        pe.matmul(to, w1_hi[:, w, c, fs], xT_hi[:, par, c], start=(c == 0), stop=False)
                        pe.matmul(to, w1_hi[:, w, c, fs], xT_lo[:, par, c], start=False, stop=False)
                        last = pe.matmul(to, w1_lo[:, w, c, fs], xT_hi[:, par, c], start=False, stop=(c == C - 1))
                last.then_inc(h_done, 1)

            def result(m, par, w, j):
                if j == 0:
                    pe.wait_ge(ghi_ready, PAIRS * m + PAIRS)
                    pe.wait_ge(glo_ready, PAIRS * m + PAIRS)
                after(pe, y_ready, J * m + j - 1)
                to = ps_y[:, j % 2, 0:D]
                rows = slice(j * P, (j + 1) * P)
                for f in range(FC):
                    pe.matmul(to, g_hi[:, par, f, rows], w2_hi[:, w, f], start=(f == 0), stop=False)
                    pe.matmul(to, g_hi[:, par, f, rows], w2_lo[:, w, f], start=False, stop=False)
                    last = pe.matmul(to, g_lo[:, par, f, rows], w2_hi[:, w, f], start=False, stop=(f == FC - 1))
                last.then_inc(y_done, 1)

            def block_of(m, i, b, first=False, last=False):
                if b % 2 == 0:
                    pe.wait_ge(w1lo_ready, 2 * i + b // 2 + 1)
                if b % 2 == 1:
                    pe.wait_ge(w2lo_ready, 2 * i + b // 2 + 1)
                for q in range(PAIRS):
                    hidden(m, b % 2, b // 2, q)
                    if q == 0 and not last:
                        turn_x(m + 1, 2 * i + (b + 1) // 2, (b + 1) % 2)
                    if not first:
                        result(m - 1, (b - 1) % 2, (b - 1) % 4 // 2, q)

            turn_x(0, 0, 0)
            for b in range(4):
                block_of(b, 0, b, first=(b == 0))
            with pe.Fori(1, M // 4 - 1) as i:
                for b in range(4):
                    block_of(4 * i + b, i, b)
            for b in range(4):
                block_of(M - 4 + b, M // 4 - 1, b, last=(b == 3))
            for j in range(J):
                result(M - 1, 1, 1, j)

        @block.vector
        def _(dve):
            def x_lo(m, par):
                dve.wait_ge(xhi_ready, m + 1)
                dve.tensor_tensor(xT_lo[:, par], ps_x[:, :, :], xT_hi[:, par].bitcast(F32),
                                  ALU.subtract).then_inc(xlo_ready, 1)

            def g_rest(m, par, q):
                dve.wait_ge(ghi_ready, PAIRS * m + q + 1)
                dve.tensor_tensor(g_lo[:, par, 2 * q:2 * q + 2], g[:, q % 2],
                                  g_hi[:, par, 2 * q:2 * q + 2].bitcast(F32), ALU.subtract).then_inc(glo_ready, 1)

            def result(m, i, par, j):
                dve.wait_ge(y_done, J * m + j + 1)
                if j == 0 and not (isinstance(i, int) and i == 0):
                    dve.wait_ge(y_out[par], 16 * i)
                dve.tensor_copy(y[:, par, j], ps_y[:, j % 2, 0:D]).then_inc(y_ready, 1)

            x_lo(0, 0)

            def block_of(m, i, par, first=False, last=False):
                for q in range(PAIRS):
                    g_rest(m, par, q)
                    if q == 1 and not last:
                        x_lo(m + 1, 1 - par)
                    if not first:
                        result(m - 1, i + (par - 1) // 2, 1 - par, q)

            block_of(0, 0, 0, first=True)
            block_of(1, 0, 1)
            with dve.Fori(1, M // 2 - 1) as i:
                block_of(2 * i, i, 0)
                block_of(2 * i + 1, i, 1)
            block_of(M - 2, M // 2 - 1, 0)
            block_of(M - 1, M // 2 - 1, 1, last=True)
            for j in range(J):
                result(M - 1, M // 2 - 1, 1, j)


def combine(nc, sb, ps, sem, gates_dram, resid_rows, expert_out, out_rows, logits_all, top_all, row_all):
    R = B * J
    shifted = sb("shifted", [P, R, E])
    total = sb("total", [P, R])
    second = sb("second", [P, R])
    weight = sb("weight", [P, R, K])
    rows = sb("rows", [P, 2, J * K], U32)
    picked = sb("picked", [P, 2, K, J, D])
    resid = sb("resid_c", [P, 2, J, D])
    gb = sb("gb", [P, 2, D])
    mix = sb("mix", [P, J, D])
    mix2 = sb("mix2", [P, J, D])
    res = sb("res", [P, 2, J, D])
    resid_in = [sem("residc_in0"), sem("residc_in1")]
    gb_in = [sem("gb_in0"), sem("gb_in1")]
    passed = sem("c_passed")
    gathered = [sem("gathered0"), sem("gathered1")]
    out_done = [sem("out_done0"), sem("out_done1")]
    shift_ready, exp_ready, total_ready, weight_ready, rows_ready, mix_ready, mix2_ready, mix3_ready, res_ready = map(
        sem, "shift_ready exp_ready total_ready weight_ready rows_ready mix_ready mix2_ready mix3_ready res_ready".split())

    with nc.Block() as block:
        def after(engine, what, count):
            if not (isinstance(count, int) and count <= 0):
                engine.wait_ge(what, count)

        @block.sync
        def _(sp):
            def load(n, par):
                after(sp, res_ready, n - 1)
                sp.dma_start(resid[:, par], resid_rows[n]).then_inc(resid_in[par], 16)
                sp.dma_start(gb[:, par], gates_dram[n].rearrange("(a g d) -> a g d", a=1, g=GATES)[:, GB]
                             .broadcast_to([P, D])).then_inc(gb_in[par], 16)

            def store(n, par):
                sp.wait_ge(res_ready, n + 1)
                sp.dma_start(out_rows[n], res[:, par]).then_inc(out_done[par], 16)

            load(0, 0)
            load(1, 1)
            with sp.Fori(0, B // 2 - 1) as i:
                for par in (0, 1):
                    store(2 * i + par, par)
                    load(2 * i + par + 2, par)
            store(B - 2, 0)
            store(B - 1, 1)
            for par in (0, 1):
                sp.wait_ge(out_done[par], 16 * B // 2)

        @block.gpsimd
        def _(pool):
            def gather(n, i, par, first):
                if not first:
                    pool.wait_ge(gathered[par], 16 * J * K * i)
                    held(pool, passed)
                pool.tensor_copy(rows[:, par], row_all[:, bass.ds(n, 1), :].rearrange("p a c -> p (a c)")
                                 ).then_inc(rows_ready, 1)
                pool.wait_ge(rows_ready, n + 1)
                if not first:
                    pool.wait_ge(mix2_ready, n - 1)
                    held(pool, passed)
                for j in range(J):
                    for k in range(K):
                        at = rows[:, par, j * K + k:j * K + k + 1]
                        pool.indirect_dma_start(out=picked[:, par, k, j], out_offset=None, in_=expert_out,
                                                in_offset=bass.IndirectOffsetOnAxis(ap=at, axis=0)
                                                ).then_inc(gathered[par], 16)

            gather(0, 0, 0, True)
            gather(1, 0, 1, True)
            with pool.Fori(1, B // 2) as i:
                gather(2 * i, i, 0, False)
                gather(2 * i + 1, i, 1, False)

        @block.scalar
        def _(act):
            act.wait_ge(shift_ready, 1)
            act.activation(shifted[:, :, :], shifted[:, :, :], ACT.Exp).then_inc(exp_ready, 1)
            act.activation(second[:, :], second[:, :], ACT.Exp).then_inc(exp_ready, 1)
            act.wait_ge(weight_ready, 1)

            def scaled(n, i, par):
                act.wait_ge(gathered[par], 16 * J * K * (i + 1))
                after(act, mix2_ready, n)
                for j in range(J):
                    last = act.activation(mix[:, j], picked[:, par, 0, j], ACT.Copy,
                                          scale=weight[:, bass.ds(J * n + j, 1), 0])
                last.then_inc(mix_ready, 1)

            with act.Fori(0, B // 2) as i:
                scaled(2 * i, i, 0)
                scaled(2 * i + 1, i, 1)

        @block.vector
        def _(dve):
            dve.tensor_tensor(shifted[:, :, :], logits_all[:, :, :], top_all[:, :, 0:1].broadcast_to([P, R, E]),
                              ALU.subtract)
            dve.tensor_tensor(second[:, :], top_all[:, :, 1], top_all[:, :, 0], ALU.subtract).then_inc(shift_ready, 1)
            dve.wait_ge(exp_ready, 2)
            dve.tensor_reduce(total[:, :], shifted[:, :, :], AX.X, ALU.add).then_inc(total_ready, 1)
            dve.wait_ge(total_ready, 1)
            dve.reciprocal(weight[:, :, 0], total[:, :]).then_inc(total_ready, 1)
            dve.wait_ge(total_ready, 2)
            dve.tensor_tensor(weight[:, :, 1], second[:, :], weight[:, :, 0], ALU.mult).then_inc(weight_ready, 1)
            dve.wait_ge(weight_ready, 1)

            def mixed(n, i, par):
                dve.wait_ge(mix_ready, n + 1)
                after(dve, res_ready, n)
                for j in range(J):
                    last = dve.scalar_tensor_tensor(mix2[:, j], picked[:, par, 1, j],
                                                    weight[:, bass.ds(J * n + j, 1), 1], mix[:, j],
                                                    ALU.mult, ALU.add)
                last.then_inc(mix2_ready, 1)
                dve.wait_ge(mix2_ready, n + 1)
                dve.wait_ge(gb_in[par], 16 * i + 16)
                if not isinstance(i, int) or i > 0:
                    dve.wait_ge(out_done[par], 16 * i)
                dve.tensor_tensor(mix2[:, :, :], mix2[:, :, :], gb[:, par].unsqueeze(1).broadcast_to([P, J, D]),
                                  ALU.mult).then_inc(mix3_ready, 1)
                dve.wait_ge(mix3_ready, n + 1)
                dve.wait_ge(resid_in[par], 16 * i + 16)
                dve.tensor_tensor(res[:, par], mix2[:, :, :], resid[:, par], ALU.add).then_inc(res_ready, 1)

            with dve.Fori(0, B // 2) as i:
                mixed(2 * i, i, 0)
                mixed(2 * i + 1, i, 1)


_INS = ["L0_attn_x", "L0_attn_Wqkv", "L0_attn_bqkv", "L0_attn_Wout", "L0_attn_bout", "L0_ffn_router_w",
        "L0_ffn_w1", "L0_ffn_w2", "L0_ffn_bias", "L0_c", "L0_wmod"]


def kernel(**inputs):
    import numpy as np
    import concourse.bacc as bacc
    from concourse.bass_utils import run_bass_kernel_spmd

    nc = bacc.Bacc("TRN2", target_bir_lowering=False, num_devices=1)
    arrays, args = {}, []
    for name in _INS:
        a = np.ascontiguousarray(inputs[name])
        arrays[f"in_{name}"] = a
        args.append(nc.dram_tensor(f"in_{name}", a.shape, mybir.dt.from_np(a.dtype), kind="ExternalInput").ap())
    args.append(nc.dram_tensor("out_dram", (B, T, D), F32, kind="ExternalOutput").ap())
    adaln_moe_kernel(nc, *args)
    result = run_bass_kernel_spmd(nc, [arrays], core_ids=[0])
    return result.results[0]["out_dram"]
```

```python
from contextlib import ExitStack

import concourse.bass as bass
from concourse import mybir

F32 = mybir.dt.float32
F32R = mybir.dt.float32r
BF16 = mybir.dt.bfloat16
U32 = mybir.dt.uint32
ALU = mybir.AluOpType
ACT = mybir.ActivationFunctionType
AX = mybir.AxisListType

P = 128
B, T, D = 16, 512, 256
J = T // P
C = D // P
E, K = 8, 2
F = 1024
FC = F // P
CAP = B * T // E
ROWS = K * E * CAP
NOROW = ROWS
S = K * E
BLK = 512
NB = CAP // BLK
GATES = 6
GA, CB, SB, GB, GBBIAS, GABOUT = range(GATES)
ROW_GATES = 5
EPS = 1e-5


def adaln_moe_kernel(nc, x, Wqkv, bqkv, Wout, bout, router_w, w1, w2, ffn_bias, cond, wmod, out):
    x_rows = x.rearrange("b (p j) d -> b p j d", j=J)
    out_rows = out.rearrange("b (p j) d -> b p j d", j=J)
    gates_dram = nc.dram_tensor("gates_dram", (B, GATES * D), F32, kind="Internal").ap()
    resid_dram = nc.dram_tensor("resid_dram", (B, T, D), F32, kind="Internal").ap()
    expert_in = nc.dram_tensor("expert_in", (ROWS, D), F32, kind="Internal").ap()
    expert_out = nc.dram_tensor("expert_out", (ROWS + 1, D), F32, kind="Internal").ap()
    resid_rows = resid_dram.rearrange("b (p j) d -> b p j d", j=J)
    in_blocks = expert_in.rearrange("(m p j) d -> m p j d", p=P, j=J)
    out_blocks = expert_out[0:ROWS, :].rearrange("(m p j) d -> m p j d", p=P, j=J)

    with ExitStack() as whole:
        def tensors(ctx):
            def sb(name, shape, dt=F32):
                return ctx.enter_context(nc.sbuf_tensor(name, shape, dt))

            def ps(name, shape, dt=F32):
                return ctx.enter_context(nc.psum_tensor(name, shape, dt))

            def sem(name):
                return ctx.enter_context(nc.semaphore(name))

            return sb, ps, sem

        sb, _, _ = tensors(whole)
        ident = sb("ident", [P, P])
        logits_all = sb("logits_all", [P, B * J, E])
        top_all = sb("top_all", [P, B * J, K])
        row_all = sb("row_all", [P, B, J * K], U32)

        with ExitStack() as first:
            sb, ps, sem = tensors(first)
            attend_and_route(nc, sb, ps, sem, x_rows, Wqkv, bqkv, Wout, bout, router_w, ffn_bias, cond, wmod,
                             gates_dram, resid_rows, expert_in, expert_out,
                             ident, logits_all, top_all, row_all)
        with ExitStack() as second:
            sb, ps, sem = tensors(second)
            experts(nc, sb, ps, sem, w1, w2, in_blocks, out_blocks, ident)
        with ExitStack() as third:
            sb, ps, sem = tensors(third)
            combine(nc, sb, ps, sem, gates_dram, resid_rows, expert_out, out_rows,
                    logits_all, top_all, row_all)


def held(engine, passed):
    engine.sem_inc(passed, 1)


def attend_and_route(nc, sb, ps, sem, x_rows, Wqkv, bqkv, Wout, bout, router_w, ffn_bias, cond, wmod,
                     gates_dram, resid_rows, expert_in, expert_out,
                     ident, logits_all, top_all, row_all):
    ZERO = 2048
    cond_sb = sb("cond_sb", [B, D])
    silu_c = sb("silu_c", [B, D])
    silu_cT = sb("silu_cT", [P, C, B])
    wmod_sb = sb("wmod_sb", [P, C, 6 * D])
    mod_cols = sb("mod_cols", [P, 2 * C, B])
    neg_gate = sb("neg_gate", [B, 2, D])
    sign_gate = sb("sign_gate", [B, 2, D])
    gate_rows = sb("gate_rows", [B, GATES, D])
    bias_rows = sb("bias_rows", [B, 2, D])
    wqkv_sb = sb("wqkv_sb", [P, C, 3 * D])
    wqkv_hi = sb("wqkv_hi", [P, C, 3 * D], F32R)
    wqkv_lo = sb("wqkv_lo", [P, C, 3 * D], F32R)
    bq_cols = sb("bq_cols", [P, C])
    bkv_f = sb("bkv_f", [P, 2 * D])
    bkv_part = sb("bkv_part", [P, 2 * D])
    bkv_r = sb("bkv_r", [P, 2 * D], F32R)
    pick_f = sb("pick_f", [P, P])
    pick_r = sb("pick_r", [P, P], F32R)
    wout_sb = sb("wout_sb", [P, C, D])
    router_sb = sb("router_sb", [P, C, E])
    ones_f = sb("ones_f", [P, P])
    ones_b = sb("ones_b", [P, P], BF16)
    ident_b = sb("ident_b", [P, P], BF16)
    before_b = sb("before_b", [P, P], BF16)
    expert_no = sb("expert_no", [P, E])
    choice_base = sb("choice_base", [P, J, K])
    eps_col = sb("eps_col", [P, 1])
    zeros = sb("zeros", [P, ZERO])
    xt = sb("xt", [P, 2, J, D])
    gates = sb("gates", [P, 2, ROW_GATES, D])
    bout_gate = sb("bout_gate", [P, 2, D])
    st1 = sb("st1", [P, J, 6])
    mv1 = sb("mv1", [P, J, 2])
    sd1 = sb("sd1", [P, J])
    rs1 = sb("rs1", [P, J])
    xn = sb("xn", [P, J, D])
    hT = sb("hT", [P, C, T])
    hT_hi = sb("hT_hi", [P, 2, C, T], F32R)
    hT_lo = sb("hT_lo", [P, 2, C, T], F32R)
    neg_mr1 = sb("neg_mr1", [P, J])
    k_sb = sb("k_sb", [P, J, D])
    k_sq = sb("k_sq", [P, D])
    kn2 = sb("kn2", [P, J])
    kn = sb("kn", [P, J])
    rk = sb("rk", [P, J])
    kv = sb("kv", [P, J, D])
    kv_cols = sb("kv_cols", [P, C])
    q_hi = sb("q_hi", [P, C, T], F32R)
    q_lo = sb("q_lo", [P, C, T], F32R)
    q_sq = sb("q_sq", [P, C, T])
    q_sq1 = sb("q_sq1", [P, T])
    qn = sb("qn", [P, J])
    rq = sb("rq", [P, J])
    wo_g = sb("wo_g", [P, C, D])
    wo_hi = sb("wo_hi", [P, C, D], F32R)
    wo_lo = sb("wo_lo", [P, C, D], F32R)
    xg = sb("xg", [P, 2, J, D])
    x1 = sb("x1", [P, J, D])
    resid = sb("resid", [P, 2, J, D])
    st2 = sb("st2", [P, J, 6])
    mv2 = sb("mv2", [P, J, 2])
    sd2 = sb("sd2", [P, J])
    rs2 = sb("rs2", [P, J])
    neg_mr2 = sb("neg_mr2", [P, J])
    xn2 = sb("xn2", [P, J, D])
    h2c = sb("h2c", [P, J, D])
    h2 = sb("h2", [P, 2, J, D])
    h2T = sb("h2T", [P, C, T])
    logits = sb("logits", [P, J, E])
    top8 = sb("top8", [P, J, 8])
    top8_no = sb("top8_no", [P, J, 8], U32)
    chosen = sb("chosen", [P, 2, J, K])
    onehot = sb("onehot", [P, 2, J, K, E], BF16)
    rank_all = sb("rank_all", [P, J, K, E])
    rank_own = sb("rank_own", [P, J * K, E])
    rank = sb("rank", [P, J, K])
    over = sb("over", [P, J, K])
    row_in = sb("row_in", [P, J, K])
    row_f = sb("row_f", [P, J, K])
    row = sb("row", [P, 2, J * K], U32)
    seen = sb("seen", [P, K * E])

    ps_T = ps("ps_T", [P, C, T])
    ps_kv = ps("ps_kv", [P, 2, 2 * D])
    ps_qo = ps("ps_qo", [P, 2, T])
    ps_s = ps("ps_s", [P, 512])
    ps_m = ps("ps_m", [P, 512])
    ps_kvc, ps_qn = ps_m[:, 0:C], ps_s[:, 0:J]
    ps_log = ps_s[:, 32:32 + J * E]
    ps_rank = ps_m[:, 128:128 + (J + 1) * K * E].rearrange("p (j c) -> p j c", j=J + 1)
    ps_o = ps_qo[:, :, :].rearrange("p a (b d) -> p (a b) d", d=D)

    kv_done, k_copied, kn2_ready, kv_ready = map(sem, "kv_done k_copied kn2_ready kv_ready".split())
    cond_in, wmod_in, bias_in, wqkv_in, bqkv_in, small_in = map(sem, "cond_in wmod_in bias_in wqkv_in bqkv_in small_in".split())
    zeros_out, gates_out, resid_out, zrow_out = [sem("zeros_out"), sem("gates_out"), [sem("resid_out0"), sem("resid_out1")], sem("zrow_out")]
    x_in = [sem("x_in0"), sem("x_in1")]
    gates_in = [sem("gates_in0"), sem("gates_in1")]
    bout_in = [sem("bout_in0"), sem("bout_in1")]
    scattered = [sem("scattered0"), sem("scattered1")]
    names = """ident0 ident1 consts0 consts1 consts2 silu_ready cT_ready cT_copied mod_ready cols_ready
      gate_neg gate_sign gate_sign1 gate_abs gate_min gates_ready wq_hi wq_lo bkv_hi bkv_ready zeros_ready rows_mod
      st1_ready mv1_ready sd1_ready rs1_ready nmr1_ready xn_ready xT_ready hT_ready hhi_ready hlo_ready
      kn_ready rk_ready kvc_done kvc_ready
      q_done qhi_ready qsq_ready qlo_ready qsq1_ready qn_done qn_ready rq_ready
      wog_ready wohi_ready wolo_ready o_done xg_ready x1_ready resid_ready
      st2_ready mv2_ready sd2_ready rs2_ready nmr2_ready xn2_ready h2c_ready h2_ready h2T_done h2T_ready
      log_done log_ready log_kept top_ready topno_ready top_kept chosen_ready onehot_ready rank_done
      rankall_ready seen_ready own_ready rank_ready over_ready rowin_ready rowf_ready row_ready dve_passed pool_passed""".split()
    s = {n: sem(n) for n in names}

    ZSTORES = ROWS * D // (P * ZERO)

    def after(engine, name, count):
        if not isinstance(count, int):
            engine.wait_ge(s[name], count)
        elif count > 0:
            engine.wait_ge(s[name], min(count, B))

    def step(stages, n, i, par):
        for stage, off in stages:
            m = n + off
            if isinstance(m, int) and not 0 <= m < B:
                continue
            stage(m, i + (par + off) // 2, (par + off) % 2)

    def pipeline(engine, stages, first=lambda: None):
        step(stages, -3, -2, 1)
        step(stages, -2, -1, 0)
        first()
        for n in range(-1, 2):
            step(stages, n, n // 2, n % 2)
        with engine.Fori(1, B // 2 - 2) as i:
            step(stages, 2 * i, i, 0)
            step(stages, 2 * i + 1, i, 1)
        for n in range(B - 4, B + 2):
            step(stages, n, n // 2, n % 2)

    with nc.Block() as block:
        @block.sync
        def _(sp):
            sp.dma_start(cond_sb[:, :], cond).then_inc(cond_in, 16)

            def gate_rows_of(m):
                return gates_dram[m].rearrange("(a g d) -> a g d", a=1, g=GATES)

            def load_x(m, i, par):
                after(sp, "xg_ready", m - 1)
                after(sp, "xn_ready", m - 1)
                sp.dma_start(xt[:, par], x_rows[m]).then_inc(x_in[par], 16)

            def load_gates(m, i, par):
                after(sp, "h2_ready", m - 1)
                after(sp, "resid_ready", m - 1)
                sp.dma_start(gates[:, par], gate_rows_of(m)[:, 0:ROW_GATES]
                             .broadcast_to([P, ROW_GATES, D])).then_inc(gates_in[par], 16)

            def load_bout_gate(m, i, par):
                sp.dma_start(bout_gate[:, par], gate_rows_of(m)[:, GABOUT]
                             .broadcast_to([P, D])).then_inc(bout_in[par], 16)

            def store_resid(m, i, par):
                after(sp, "resid_ready", m + 1)
                sp.dma_start(resid_rows[m], resid[:, par]).then_inc(resid_out[par], 16)

            def store_zeros(z):
                per = P * ZERO // D
                sp.dma_start(expert_in[z * per:(z + 1) * per, :].rearrange("(p r) d -> p (r d)", p=P),
                             zeros[:, :]).then_inc(zeros_out, 16)

            load_x(0, 0, 0)
            sp.dma_start(wmod_sb[:, :, :], wmod.rearrange("(c p) n -> p c n", p=P)).then_inc(wmod_in, 16)
            with nc.allow_non_contiguous_dma(reason="256 values, once"):
                sp.dma_start(bq_cols[:, :], bqkv[0:D].rearrange("(c p) -> p c", p=P)).then_inc(small_in, 16)
            sp.dma_start(wqkv_sb[:, :, :], Wqkv.rearrange("(c p) n -> p c n", p=P)).then_inc(wqkv_in, 16)
            sp.dma_start(bkv_f[:, :], bqkv[D:3 * D].unsqueeze(0).broadcast_to([P, 2 * D])).then_inc(bqkv_in, 16)
            sp.dma_start(bias_rows[:, 0, :], bout.unsqueeze(0).broadcast_to([B, D])).then_inc(bias_in, 16)
            sp.dma_start(bias_rows[:, 1, :], ffn_bias[0, 0:1, :].broadcast_to([B, D])).then_inc(bias_in, 16)
            load_x(1, 0, 1)
            sp.dma_start(wout_sb[:, :, :], Wout.rearrange("(c p) n -> p c n", p=P)).then_inc(small_in, 16)
            sp.dma_start(router_sb[:, :, :], router_w.rearrange("(c p) n -> p c n", p=P)).then_inc(small_in, 16)
            sp.wait_ge(s["zeros_ready"], 1)
            sp.dma_start(expert_out[ROWS:ROWS + 1, :], zeros[0:1, 0:D]).then_inc(zrow_out, 16)
            for z in range(ZSTORES // 4):
                store_zeros(z)
            sp.wait_ge(s["gates_ready"], 1)
            sp.dma_start(gates_dram, gate_rows[:, :, :].rearrange("b g d -> b (g d)")).then_inc(gates_out, 16)
            sp.wait_ge(gates_out, 16)
            load_gates(0, 0, 0)
            load_gates(1, 0, 1)
            load_bout_gate(0, 0, 0)
            load_bout_gate(1, 0, 1)
            load_x(2, 1, 0)
            load_bout_gate(2, 1, 0)
            load_x(3, 1, 1)
            load_bout_gate(3, 1, 1)
            for z in range(ZSTORES // 4, ZSTORES // 2):
                store_zeros(z)
            for z in range(ZSTORES // 2, ZSTORES):
                store_zeros(z)

            def ahead(n, i, par):
                if not isinstance(n, int) or n + 4 < B:
                    load_x(n + 4, i + 2, par)
                    load_bout_gate(n + 4, i + 2, par)
                store_resid(n, i, par)
                if not isinstance(n, int) or n + 2 < B:
                    load_gates(n + 2, i + 1, par)

            ahead(0, 0, 0)
            ahead(1, 0, 1)
            with sp.Fori(1, B // 2 - 2) as i:
                ahead(2 * i, i, 0)
                ahead(2 * i + 1, i, 1)
            for n in range(B - 4, B):
                ahead(n, n // 2, n % 2)
            sp.wait_ge(zrow_out, 16)
            for par in (0, 1):
                sp.wait_ge(resid_out[par], 16 * B // 2)

        @block.gpsimd
        def _(pool):
            pool.memset(ident[:, :], 0.0)
            pool.memset(ident_b[:, :], 0.0)
            pool.memset(before_b[:, :], 1.0).then_inc(s["ident0"], 1)
            pool.wait_ge(s["ident0"], 1)
            for m in (ident, ident_b):
                pool.affine_select(out=m[:, :], in_=m[:, :], compare_op=ALU.not_equal, fill=1.0,
                                   base=0, pattern=[[-1, P]], channel_multiplier=1)
            pool.affine_select(out=before_b[:, :], in_=before_b[:, :], compare_op=ALU.is_gt, fill=0.0,
                               base=0, pattern=[[1, P]], channel_multiplier=-1).then_inc(s["ident1"], 1)
            pool.memset(ones_b[:, :], 1.0)
            pool.memset(ones_f[:, :], 1.0)
            pool.memset(eps_col[:, :], EPS)
            pool.memset(seen[:, :], 0.0)
            pool.memset(choice_base[:, :, 0], 0.0)
            pool.memset(choice_base[:, :, 1], float(E * CAP))
            pool.iota(expert_no[:, :], pattern=[[1, E]], base=0, channel_multiplier=0,
                      allow_small_or_imprecise_dtypes=True).then_inc(s["consts0"], 1)
            pool.memset(zeros[:, :], 0.0).then_inc(s["zeros_ready"], 1)

            def q_squares(m, i, par):
                pool.wait_ge(s["qsq_ready"], m + 1)
                after(pool, "qn_done", m)
                pool.tensor_tensor(q_sq1[:, :], q_sq[:, 0], q_sq[:, 1], ALU.add).then_inc(s["qsq1_ready"], 1)

            def scatter(m, i, par):
                if isinstance(m, int) and m == 0:
                    pool.wait_ge(zeros_out, 16 * ZSTORES)
                pool.wait_ge(s["row_ready"], m + 1)
                held(pool, s["pool_passed"])
                for j in range(J):
                    for k in range(K):
                        at = row[:, par, j * K + k:j * K + k + 1]
                        pool.indirect_dma_start(out=expert_in,
                                                out_offset=bass.IndirectOffsetOnAxis(ap=at, axis=0),
                                                in_=h2[:, par, j], in_offset=None,
                                                bounds_check=ROWS - 1, oob_is_err=False
                                                ).then_inc(scattered[par], 16)

            def residual(m, i, par):
                pool.wait_ge(s["x1_ready"], m + 1)
                if not isinstance(m, int) or m > 1:
                    pool.wait_ge(resid_out[par], 16 * i)
                pool.tensor_tensor(resid[:, par], x1[:, :, :],
                                   gates[:, par, GBBIAS].unsqueeze(1).broadcast_to([P, J, D]),
                                   ALU.add).then_inc(s["resid_ready"], 1)

            def x_gated(m, i, par):
                pool.wait_ge(x_in[par], 16 * i + 16)
                pool.wait_ge(bout_in[par], 16 * i + 16)
                after(pool, "x1_ready", m - 1)
                pool.tensor_tensor(xg[:, par], xt[:, par],
                                   bout_gate[:, par].unsqueeze(1).broadcast_to([P, J, D]),
                                   ALU.add).then_inc(s["xg_ready"], 1)

            def shifted(m, i, par):
                pool.wait_ge(s["h2c_ready"], m + 1)
                if not isinstance(m, int) or m > 1:
                    pool.wait_ge(scattered[par], 16 * J * K * i)
                pool.tensor_tensor(h2[:, par], h2c[:, :, :],
                                   gates[:, par, SB].unsqueeze(1).broadcast_to([P, J, D]),
                                   ALU.add).then_inc(s["h2_ready"], 1)

            pipeline(pool, [(scatter, -2), (x_gated, 2), (q_squares, 1), (shifted, 0), (residual, 0)])
            for par in (0, 1):
                pool.wait_ge(scattered[par], 16 * J * K * B // 2)

        @block.scalar
        def _(act):
            act.wait_ge(cond_in, 16)
            act.activation(silu_c[:, :], cond_sb[:, :], ACT.Silu).then_inc(s["silu_ready"], 1)
            act.wait_ge(s["cT_ready"], 1)
            act.activation(silu_cT[:, :, :], ps_m[:, 0:C * B].rearrange("p (c b) -> p c b", c=C),
                           ACT.Copy).then_inc(s["cT_copied"], 1)
            act.wait_ge(s["consts0"], 1)
            act.wait_ge(s["cols_ready"], 1)

            def deviation1(m, i, par):
                act.wait_ge(s["mv1_ready"], m + 1)
                act.activation(sd1[:, :], mv1[:, :, 1], ACT.Sqrt, bias=eps_col[:, 0:1]).then_inc(s["sd1_ready"], 1)

            def norm1(m, i, par):
                act.wait_ge(s["nmr1_ready"], m + 1)
                after(act, "xT_ready", m)
                for j in range(J):
                    last = act.activation(xn[:, j], xt[:, par, j], ACT.Identity, scale=rs1[:, j:j + 1],
                                          bias=neg_mr1[:, j:j + 1])
                last.then_inc(s["xn_ready"], 1)

            def norm2(m, i, par):
                act.wait_ge(s["mv2_ready"], m + 1)
                act.activation(sd2[:, :], mv2[:, :, 1], ACT.Sqrt, bias=eps_col[:, 0:1]).then_inc(s["sd2_ready"], 1)
                act.wait_ge(s["nmr2_ready"], m + 1)
                after(act, "h2c_ready", m)
                for j in range(J):
                    last = act.activation(xn2[:, j], x1[:, j], ACT.Identity, scale=rs2[:, j:j + 1],
                                          bias=neg_mr2[:, j:j + 1])
                last.then_inc(s["xn2_ready"], 1)

            def modulated(m, i, par):
                act.wait_ge(s["xT_ready"], m + 1)
                after(act, "hlo_ready", m)
                for c in range(C):
                    last = act.activation(hT[:, c], ps_T[:, c], ACT.Identity,
                                          scale=mod_cols[:, C + c, bass.ds(m, 1)],
                                          bias=mod_cols[:, c, bass.ds(m, 1)])
                last.then_inc(s["hT_ready"], 1)
                act.wait_ge(s["hT_ready"], m + 1)
                after(act, "q_done", m - 1)
                act.activation(hT_hi[:, par], hT[:, :, :], ACT.Copy).then_inc(s["hhi_ready"], 1)

            def k_tiles(m, i, par, tiles):
                if tiles[0] == 0:
                    after(act, "kn_ready", m)
                for j in tiles:
                    act.wait_ge(kv_done, J * m + j + 1)
                    if j == 0 and not (isinstance(m, int) and m == 0):
                        act.wait_ge(kv_ready, J * m)
                    act.activation(k_sb[:, j], ps_kv[:, j % 2, 0:D], ACT.Copy).then_inc(k_copied, 1)
                    act.wait_ge(k_copied, J * m + j + 1)
                    act.activation(k_sq[:, :], k_sb[:, j], ACT.Square,
                                   accum_out=kn2[:, j:j + 1]).then_inc(kn2_ready, 1)

            def k_first(m, i, par):
                k_tiles(m, i, par, (0, 1))

            def k_rest(m, i, par):
                k_tiles(m, i, par, (2, 3))
                act.wait_ge(kn2_ready, J * m + J)
                after(act, "rk_ready", m)
                act.activation(kn[:, :], kn2[:, :], ACT.Sqrt).then_inc(s["kn_ready"], 1)

            def out_weights(m, i, par):
                act.wait_ge(s["wog_ready"], m + 1)
                after(act, "o_done", m)
                act.activation(wo_hi[:, :, :], wo_g[:, :, :], ACT.Copy).then_inc(s["wohi_ready"], 1)

            def q_length(m, i, par):
                act.wait_ge(s["qn_done"], m + 1)
                after(act, "rq_ready", m)
                act.activation(qn[:, :], ps_qn, ACT.Sqrt).then_inc(s["qn_ready"], 1)

            def h2_turned(m, i, par):
                act.wait_ge(s["h2T_done"], m + 1)
                after(act, "log_done", m)
                act.activation(h2T[:, :, :], ps_T[:, :, :], ACT.Copy).then_inc(s["h2T_ready"], 1)

            def q_parts(m, i, par):
                act.wait_ge(s["q_done"], m + 1)
                after(act, "o_done", m)
                for c in range(C):
                    last = act.activation(q_hi[:, c], ps_qo[:, c], ACT.Identity, bias=bq_cols[:, c:c + 1])
                last.then_inc(s["qhi_ready"], 1)
                after(act, "qsq1_ready", m)
                for c in range(C):
                    last = act.activation(q_sq[:, c], ps_qo[:, c], ACT.Square, bias=bq_cols[:, c:c + 1])
                last.then_inc(s["qsq_ready"], 1)

            def small_loads():
                act.wait_ge(small_in, 48)

            pipeline(act, [(k_first, 1), (norm1, 2), (out_weights, 0), (k_rest, 1), (q_length, 0), (modulated, 2),
                           (deviation1, 3), (h2_turned, -1), (norm2, 0), (q_parts, 1)], small_loads)

        @block.tensor
        def _(pe):
            pe.wait_ge(s["ident1"], 1)
            pe.wait_ge(s["silu_ready"], 1)
            for c in range(C):
                last = pe.transpose(ps_m[:, c * B:(c + 1) * B], silu_c[:, c * P:(c + 1) * P], ident[0:B, 0:B])
            last.then_inc(s["cT_ready"], 1)
            pe.wait_ge(s["cT_copied"], 1)
            pe.wait_ge(wmod_in, 16)
            for m in range(2 * C):
                for c in range(C):
                    last = pe.matmul(ps_m[:, m * B:(m + 1) * B], wmod_sb[:, c, m * P:(m + 1) * P],
                                     silu_cT[:, c], start=(c == 0), stop=(c == C - 1))
            last.then_inc(s["mod_ready"], 1)

            def gate_products():
                for bank, lo, hi in ((ps_kv[:, 0], 2, 3), (ps_kv[:, 1], 3, 5), (ps_qo[:, 0], 5, 6)):
                    for c in range(C):
                        last = pe.matmul(bank[0:B, 0:(hi - lo) * D], silu_cT[:, c], wmod_sb[:, c, lo * D:hi * D],
                                         start=(c == 0), stop=(c == C - 1))
                last.then_inc(s["rows_mod"], 1)
                pe.wait_ge(s["wq_lo"], 1)
                pe.wait_ge(s["bkv_ready"], 1)
                pe.wait_ge(s["consts0"], 1)
                pe.wait_ge(small_in, 48)
                pe.wait_ge(s["gates_ready"], 1)

            def x_turned(m, i, par):
                pe.wait_ge(s["xn_ready"], m + 1)
                after(pe, "h2T_ready", m - 3)
                for j in range(J):
                    for c in range(C):
                        last = pe.transpose(ps_T[:, c, j * P:(j + 1) * P], xn[:, j, c * P:(c + 1) * P], ident[:, :])
                last.then_inc(s["xT_ready"], 1)

            def kv_tiles(m, i, par):
                pe.wait_ge(s["hlo_ready"], m + 1)
                pe.wait_ge(s["hhi_ready"], m + 1)
                for j in range(J):
                    if not (isinstance(m, int) and J * m + j < 2):
                        pe.wait_ge(kv_ready, J * m + j - 1)
                    to = ps_kv[:, j % 2]
                    pe.matmul(to, pick_r[:, :], bkv_r[:, :], start=True, stop=False)
                    tok = slice(j * P, (j + 1) * P)
                    for c in range(C):
                        pe.matmul(to, hT_hi[:, par, c, tok], wqkv_hi[:, c, D:3 * D], start=False, stop=False)
                        pe.matmul(to, hT_hi[:, par, c, tok], wqkv_lo[:, c, D:3 * D], start=False, stop=False)
                        last = pe.matmul(to, hT_lo[:, par, c, tok], wqkv_hi[:, c, D:3 * D],
                                         start=False, stop=(c == C - 1))
                    last.then_inc(kv_done, 1)

            def q_product(m, i, par):
                after(pe, "x1_ready", m)
                for f in range(C):
                    to = ps_qo[:, f]
                    feat = slice(f * P, (f + 1) * P)
                    for c in range(C):
                        pe.matmul(to, wqkv_hi[:, c, feat], hT_hi[:, par, c], start=(c == 0), stop=False)
                        pe.matmul(to, wqkv_hi[:, c, feat], hT_lo[:, par, c], start=False, stop=False)
                        last = pe.matmul(to, wqkv_lo[:, c, feat], hT_hi[:, par, c], start=False, stop=(c == C - 1))
                last.then_inc(s["q_done"], 1)

            def kv_sums(m, i, par):
                pe.wait_ge(s["rk_ready"], m + 1)
                pe.wait_ge(kv_ready, J * m + J)
                after(pe, "seen_ready", m - 2)
                for c in range(C):
                    for j in range(J):
                        last = pe.matmul(ps_kvc[:, c:c + 1], kv[:, j, c * P:(c + 1) * P], rk[:, j:j + 1],
                                         start=(j == 0), stop=(j == J - 1))
                last.then_inc(s["kvc_done"], 1)

            def q_lengths(m, i, par):
                pe.wait_ge(s["qsq1_ready"], m + 1)
                after(pe, "log_ready", m - 1)
                for j in range(J):
                    last = pe.matmul(ps_qn[:, j:j + 1], q_sq1[:, j * P:(j + 1) * P], ones_f[:, 0:1],
                                     start=True, stop=True)
                last.then_inc(s["qn_done"], 1)

            def output(m, i, par):
                pe.wait_ge(s["wolo_ready"], m + 1)
                pe.wait_ge(s["wohi_ready"], m + 1)
                pe.wait_ge(s["qlo_ready"], m + 1)
                pe.wait_ge(s["qhi_ready"], m + 1)
                for j in range(J):
                    tok = slice(j * P, (j + 1) * P)
                    for c in range(C):
                        pe.matmul(ps_o[:, j], q_hi[:, c, tok], wo_hi[:, c], start=(c == 0), stop=False)
                        pe.matmul(ps_o[:, j], q_hi[:, c, tok], wo_lo[:, c], start=False, stop=False)
                        last = pe.matmul(ps_o[:, j], q_lo[:, c, tok], wo_hi[:, c], start=False, stop=(c == C - 1))
                last.then_inc(s["o_done"], 1)

            def h2_turn(m, i, par):
                pe.wait_ge(s["h2_ready"], m + 1)
                after(pe, "hT_ready", m + 4)
                for j in range(J):
                    for c in range(C):
                        last = pe.transpose(ps_T[:, c, j * P:(j + 1) * P], h2[:, par, j, c * P:(c + 1) * P],
                                            ident[:, :])
                last.then_inc(s["h2T_done"], 1)

            def route(m, i, par):
                pe.wait_ge(s["h2T_ready"], m + 1)
                after(pe, "qn_ready", m + 2)
                for j in range(J):
                    for c in range(C):
                        last = pe.matmul(ps_log[:, j * E:(j + 1) * E], h2T[:, c, j * P:(j + 1) * P],
                                         router_sb[:, c], start=(c == 0), stop=(c == C - 1))
                last.then_inc(s["log_done"], 1)

            def ranks(m, i, par):
                pe.wait_ge(s["onehot_ready"], m + 1)
                after(pe, "kvc_ready", m + 3)
                hot = onehot[:, par].rearrange("p j k e -> p j (k e)")
                for j in range(J):
                    pe.matmul(ps_rank[:, J], ones_b[:, :], hot[:, j], start=(j == 0), stop=(j == J - 1))
                for j in range(J):
                    pe.matmul(ps_rank[:, 0:J], before_b[:, :],
                              hot[:, j].unsqueeze(1).broadcast_to([P, J, K * E]), start=(j == 0), stop=False)
                for j in range(J - 1):
                    last = pe.matmul(ps_rank[:, j + 1:J], ident_b[:, :],
                                     hot[:, j].unsqueeze(1).broadcast_to([P, J - 1 - j, K * E]),
                                     start=False, stop=(j == J - 2))
                last.then_inc(s["rank_done"], 1)

            pipeline(pe, [(kv_tiles, 1), (ranks, -2), (q_lengths, 0), (x_turned, 2), (output, 0), (h2_turn, -1),
                          (kv_sums, 1), (q_product, 1), (route, -1)], gate_products)

        @block.vector
        def _(dve):
            dve.wait_ge(s["mod_ready"], 1)
            dve.tensor_copy(mod_cols[:, 0:C], ps_m[:, 0:C * B].rearrange("p (c b) -> p c b", c=C))
            dve.tensor_scalar(mod_cols[:, C:2 * C], ps_m[:, C * B:2 * C * B].rearrange("p (c b) -> p c b", c=C),
                              1.0, None, ALU.add).then_inc(s["cols_ready"], 1)

            def weights_and_gates():
                dve.wait_ge(wqkv_in, 16)
                dve.tensor_copy(wqkv_hi[:, :, :], wqkv_sb[:, :, :]).then_inc(s["wq_hi"], 1)
                dve.wait_ge(s["wq_hi"], 1)
                dve.tensor_tensor(wqkv_lo[:, :, :], wqkv_sb[:, :, :], wqkv_hi[:, :, :].bitcast(F32),
                                  ALU.subtract).then_inc(s["wq_lo"], 1)
                dve.wait_ge(s["rows_mod"], 1)
                gate_banks = (ps_kv[0:B, 0, 0:D], ps_qo[0:B, 0, 0:D])
                for g in range(2):
                    dve.tensor_scalar(neg_gate[:, g], gate_banks[g], -1.0, None, ALU.mult)
                    last = dve.tensor_scalar(sign_gate[:, g], gate_banks[g], 0.0, 2.0, ALU.is_ge, ALU.mult)
                last.then_inc(s["gate_sign"], 1)
                dve.wait_ge(s["gate_sign"], 1)
                for g in range(2):
                    dve.tensor_tensor(neg_gate[:, g], gate_banks[g], neg_gate[:, g], ALU.max)
                    last = dve.tensor_scalar(sign_gate[:, g], sign_gate[:, g], -1.0, None, ALU.add)
                last.then_inc(s["gate_abs"], 1)
                dve.wait_ge(s["gate_abs"], 1)
                for g, to in enumerate((GA, GB)):
                    dve.scalar_tensor_tensor(gate_rows[:, to], neg_gate[:, g], 0.25, sign_gate[:, g],
                                             ALU.max, ALU.mult)
                dve.tensor_copy(gate_rows[:, SB], ps_kv[0:B, 1, 0:D])
                dve.tensor_scalar(gate_rows[:, CB], ps_kv[0:B, 1, D:2 * D], 1.0, None,
                                  ALU.add).then_inc(s["gate_min"], 1)
                dve.wait_ge(s["gate_min"], 1)
                dve.wait_ge(bias_in, 32)
                dve.tensor_tensor(gate_rows[:, GABOUT], gate_rows[:, GA], bias_rows[:, 0], ALU.mult)
                dve.tensor_tensor(gate_rows[:, GBBIAS], gate_rows[:, GB], bias_rows[:, 1],
                                  ALU.mult).then_inc(s["gates_ready"], 1)
                dve.wait_ge(bqkv_in, 16)
                dve.memset(bkv_part[:, :], 0.0)
                dve.memset(pick_f[:, :], 0.0)
                dve.tensor_copy(bkv_r[:, :], bkv_f[:, :]).then_inc(s["bkv_hi"], 1)
                dve.wait_ge(s["bkv_hi"], 1)
                dve.memset(pick_f[0:1, :], 1.0)
                dve.memset(pick_f[32:33, :], 1.0)
                dve.tensor_tensor(bkv_f[:, :], bkv_f[:, :], bkv_r[:, :].bitcast(F32), ALU.subtract)
                dve.tensor_copy(bkv_part[0:1, :], bkv_r[0:1, :].bitcast(F32)).then_inc(s["bkv_hi"], 1)
                dve.wait_ge(s["bkv_hi"], 2)
                dve.tensor_copy(pick_r[:, :], pick_f[:, :])
                dve.tensor_copy(bkv_part[32:33, :], bkv_f[32:33, :]).then_inc(s["bkv_hi"], 1)
                dve.wait_ge(s["bkv_hi"], 3)
                dve.tensor_copy(bkv_r[:, :], bkv_part[:, :]).then_inc(s["bkv_ready"], 1)
                dve.wait_ge(s["consts0"], 1)
                dve.wait_ge(small_in, 48)

            def norm1(m, i, par):
                dve.wait_ge(x_in[par], 16 * i + 16)
                for j in range(J):
                    last = dve.bn_stats(st1[:, j], xt[:, par, j])
                last.then_inc(s["st1_ready"], 1)
                dve.wait_ge(s["st1_ready"], m + 1)
                after(dve, "nmr1_ready", m)
                held(dve, s["dve_passed"])
                for j in range(J):
                    last = dve.bn_aggr(mv1[:, j], st1[:, j])
                last.then_inc(s["mv1_ready"], 1)

            def norm1_scale(m, i, par):
                dve.wait_ge(s["sd1_ready"], m + 1)
                after(dve, "xn_ready", m)
                dve.reciprocal(rs1[:, :], sd1[:, :]).then_inc(s["rs1_ready"], 1)
                dve.wait_ge(s["rs1_ready"], m + 1)
                dve.scalar_tensor_tensor(neg_mr1[:, :], mv1[:, :, 0], -1.0, rs1[:, :],
                                         ALU.mult, ALU.mult).then_inc(s["nmr1_ready"], 1)

            def h_rest(m, i, par):
                dve.wait_ge(s["hhi_ready"], m + 1)
                after(dve, "q_done", m - 1)
                dve.tensor_tensor(hT_lo[:, par], hT[:, :, :], hT_hi[:, par].bitcast(F32),
                                  ALU.subtract).then_inc(s["hlo_ready"], 1)

            def kv_tile(j):
                def product(m, i, par):
                    if j == 0:
                        after(dve, "kvc_done", m)
                    dve.wait_ge(k_copied, J * m + j + 1)
                    dve.tensor_tensor(kv[:, j], ps_kv[:, j % 2, D:2 * D], k_sb[:, j],
                                      ALU.mult).then_inc(kv_ready, 1)
                return product

            def k_inverse(m, i, par):
                dve.wait_ge(s["kn_ready"], m + 1)
                dve.reciprocal(rk[:, :], kn[:, :]).then_inc(s["rk_ready"], 1)

            def q_rest(m, i, par):
                dve.wait_ge(s["qsq_ready"], m + 1)
                after(dve, "o_done", m)
                for c in range(C):
                    last = dve.scalar_tensor_tensor(q_lo[:, c], ps_qo[:, c], bq_cols[:, c:c + 1],
                                                    q_hi[:, c].bitcast(F32), ALU.add, ALU.subtract)
                last.then_inc(s["qlo_ready"], 1)

            def gated_weights(m, i, par):
                dve.wait_ge(s["kvc_done"], m + 1)
                dve.wait_ge(gates_in[par], 16 * i + 16)
                dve.tensor_copy(kv_cols[:, :], ps_kvc).then_inc(s["kvc_ready"], 1)
                dve.wait_ge(s["kvc_ready"], m + 1)
                after(dve, "wohi_ready", m)
                after(dve, "wolo_ready", m)
                for c in range(C):
                    last = dve.scalar_tensor_tensor(wo_g[:, c], wout_sb[:, c], kv_cols[:, c:c + 1],
                                                    gates[:, par, GA], ALU.mult, ALU.mult)
                last.then_inc(s["wog_ready"], 1)

            def gated_rest(m, i, par):
                dve.wait_ge(s["wohi_ready"], m + 1)
                after(dve, "o_done", m)
                dve.tensor_tensor(wo_lo[:, :, :], wo_g[:, :, :], wo_hi[:, :, :].bitcast(F32),
                                  ALU.subtract).then_inc(s["wolo_ready"], 1)

            def attended(m, i, par):
                dve.wait_ge(s["qn_ready"], m + 1)
                after(dve, "x1_ready", m)
                dve.reciprocal(rq[:, :], qn[:, :]).then_inc(s["rq_ready"], 1)
                dve.wait_ge(s["rq_ready"], m + 1)
                dve.wait_ge(s["o_done"], m + 1)
                dve.wait_ge(s["xg_ready"], m + 1)
                after(dve, "resid_ready", m)
                after(dve, "xn2_ready", m)
                for j in range(J):
                    last = dve.scalar_tensor_tensor(x1[:, j], ps_o[:, j], rq[:, j:j + 1], xg[:, par, j],
                                                    ALU.mult, ALU.add)
                last.then_inc(s["x1_ready"], 1)

            def norm2(m, i, par):
                dve.wait_ge(s["x1_ready"], m + 1)
                for j in range(J):
                    last = dve.bn_stats(st2[:, j], x1[:, j])
                last.then_inc(s["st2_ready"], 1)
                dve.wait_ge(s["st2_ready"], m + 1)
                after(dve, "nmr2_ready", m)
                held(dve, s["dve_passed"])
                for j in range(J):
                    last = dve.bn_aggr(mv2[:, j], st2[:, j])
                last.then_inc(s["mv2_ready"], 1)

            def norm2_scale(m, i, par):
                dve.wait_ge(s["sd2_ready"], m + 1)
                after(dve, "xn2_ready", m)
                dve.reciprocal(rs2[:, :], sd2[:, :]).then_inc(s["rs2_ready"], 1)
                dve.wait_ge(s["rs2_ready"], m + 1)
                dve.scalar_tensor_tensor(neg_mr2[:, :], mv2[:, :, 0], -1.0, rs2[:, :],
                                         ALU.mult, ALU.mult).then_inc(s["nmr2_ready"], 1)

            def scaled(m, i, par):
                dve.wait_ge(s["xn2_ready"], m + 1)
                after(dve, "h2_ready", m)
                dve.tensor_tensor(h2c[:, :, :], xn2[:, :, :], gates[:, par, CB].unsqueeze(1).broadcast_to([P, J, D]),
                                  ALU.mult).then_inc(s["h2c_ready"], 1)

            def choose(m, i, par):
                dve.wait_ge(s["log_done"], m + 1)
                after(dve, "topno_ready", m)
                dve.tensor_copy(logits[:, :, :], ps_log.rearrange("p (j e) -> p j e", j=J)).then_inc(s["log_ready"], 1)
                dve.wait_ge(s["log_ready"], m + 1)
                dve.tensor_copy(logits_all[:, bass.ds(J * m, J), :], logits[:, :, :])
                after(dve, "top_kept", m)
                held(dve, s["dve_passed"])
                for j in range(J):
                    last = dve.max(top8[:, j], logits[:, j])
                last.then_inc(s["top_ready"], 1)
                dve.wait_ge(s["top_ready"], m + 1)
                dve.tensor_copy(top_all[:, bass.ds(J * m, J), :], top8[:, :, 0:K]).then_inc(s["top_kept"], 1)
                after(dve, "chosen_ready", m)
                held(dve, s["dve_passed"])
                for j in range(J):
                    last = dve.max_index(top8_no[:, j], top8[:, j], logits[:, j])
                last.then_inc(s["topno_ready"], 1)
                dve.wait_ge(s["topno_ready"], m + 1)
                after(dve, "rowin_ready", m - 1)
                dve.tensor_copy(chosen[:, par], top8_no[:, :, 0:K]).then_inc(s["chosen_ready"], 1)
                dve.wait_ge(s["chosen_ready"], m + 1)
                after(dve, "own_ready", m - 1)
                dve.tensor_tensor(onehot[:, par].rearrange("p j k e -> p (j k) e"),
                                  expert_no[:, :].unsqueeze(1).broadcast_to([P, J * K, E]),
                                  chosen[:, par].rearrange("p j k -> p (j k)").unsqueeze(2)
                                  .broadcast_to([P, J * K, E]), ALU.is_equal).then_inc(s["onehot_ready"], 1)

            def rows(m, i, par):
                dve.wait_ge(s["rank_done"], m + 1)
                after(dve, "own_ready", m)
                after(dve, "seen_ready", m)
                dve.tensor_tensor(rank_all[:, :, :, :].rearrange("p j k e -> p j (k e)"), ps_rank[:, 0:J],
                                  seen[:, :].unsqueeze(1).broadcast_to([P, J, K * E]),
                                  ALU.add).then_inc(s["rankall_ready"], 1)
                dve.wait_ge(s["rankall_ready"], m + 1)
                dve.tensor_tensor(seen[:, :], ps_rank[:, J], seen[:, :], ALU.add).then_inc(s["seen_ready"], 1)
                after(dve, "rank_ready", m)
                dve.tensor_tensor(rank_own[:, :, :], rank_all[:, :, :, :].rearrange("p j k e -> p (j k) e"),
                                  onehot[:, par].rearrange("p j k e -> p (j k) e"),
                                  ALU.mult).then_inc(s["own_ready"], 1)
                dve.wait_ge(s["own_ready"], m + 1)
                after(dve, "rowf_ready", m)
                dve.tensor_reduce(rank[:, :, :].rearrange("p j k -> p (j k)"), rank_own[:, :, :], AX.X,
                                  ALU.add).then_inc(s["rank_ready"], 1)
                dve.wait_ge(s["rank_ready"], m + 1)
                dve.tensor_scalar(over[:, :, :], rank[:, :, :], float(CAP), float(2 * ROWS), ALU.is_ge, ALU.mult)
                dve.scalar_tensor_tensor(row_in[:, :, :], chosen[:, par], float(CAP), choice_base[:, :, :],
                                         ALU.mult, ALU.add).then_inc(s["rowin_ready"], 1)
                dve.wait_ge(s["rowin_ready"], m + 1)
                dve.tensor_tensor(over[:, :, :], over[:, :, :], rank[:, :, :], ALU.add).then_inc(s["over_ready"], 1)
                dve.wait_ge(s["over_ready"], m + 1)
                after(dve, "row_ready", m)
                dve.tensor_tensor(row_f[:, :, :], over[:, :, :], row_in[:, :, :], ALU.add).then_inc(s["rowf_ready"], 1)
                dve.wait_ge(s["rowf_ready"], m + 1)
                if not isinstance(m, int) or m > 1:
                    dve.wait_ge(scattered[par], 16 * J * K * i)
                last_row = row_f[:, :, :].rearrange("p j k -> p (j k)")
                dve.tensor_scalar(row[:, par], last_row, float(NOROW), None, ALU.min)
                dve.tensor_scalar(row_all[:, bass.ds(m, 1), :].rearrange("p a c -> p (a c)"), last_row,
                                  float(NOROW), None, ALU.min).then_inc(s["row_ready"], 1)

            pipeline(dve, [(kv_tile(0), 1), (kv_tile(1), 1), (q_rest, 0), (gated_rest, 0), (kv_tile(2), 1),
                           (kv_tile(3), 1), (rows, -2), (k_inverse, 1), (norm1, 3), (attended, 0), (norm2, 0),
                           (gated_weights, 1), (norm2_scale, 0), (norm1_scale, 3), (h_rest, 2), (scaled, 0),
                           (choose, -1)], weights_and_gates)


def experts(nc, sb, ps, sem, w1, w2, in_blocks, out_blocks, ident):
    w1_raw = sb("w1_raw", [P, C, F])
    w2_raw = sb("w2_raw", [P, FC, D])
    w1_hi = sb("w1_hi", [P, 2, C, F], F32R)
    w1_lo = sb("w1_lo", [P, 2, C, F], F32R)
    w2_hi = sb("w2_hi", [P, 2, FC, D], F32R)
    w2_lo = sb("w2_lo", [P, 2, FC, D], F32R)
    xin = sb("xin", [P, 2, J, D])
    xT_hi = sb("xT_hi", [P, 2, C, BLK], F32R)
    xT_lo = sb("xT_lo", [P, 2, C, BLK], F32R)
    g = sb("g", [P, 2, 2, BLK])
    g_hi = sb("g_hi", [P, 2, FC, BLK], F32R)
    g_lo = sb("g_lo", [P, 2, FC, BLK], F32R)
    y = sb("y", [P, 2, J, D])
    ps_x = ps("ps_x", [P, C, BLK])
    ps_h = ps("ps_h", [P, 2, 2, BLK])
    ps_y = ps("ps_y", [P, 2, 512])
    PAIRS = FC // 2
    M = S * NB

    w1_in, w2_in, passed = sem("w1_in"), sem("w2_in"), sem("w_passed")
    w1hi_ready, w1lo_ready, w2hi_ready, w2lo_ready = map(sem, "w1hi_ready w1lo_ready w2hi_ready w2lo_ready".split())
    xin_in = [sem("xin_in0"), sem("xin_in1")]
    y_out = [sem("y_out0"), sem("y_out1")]
    xT_done, xhi_ready, xlo_ready, h_done, g_ready, ghi_ready, glo_ready, y_done, y_ready = map(
        sem, "xT_done xhi_ready xlo_ready h_done g_ready ghi_ready glo_ready y_done y_ready".split())

    with nc.Block() as block:

        def after(engine, what, count):
            if not (isinstance(count, int) and count <= 0):
                engine.wait_ge(what, count)

        @block.sync
        def _(sp):
            def load_weights(s, e):
                after(sp, w1lo_ready, s)
                after(sp, w2lo_ready, s)
                sp.dma_start(w1_raw[:, :, :], w1[e].rearrange("(c p) f -> p c f", p=P)).then_inc(w1_in, 16)
                sp.dma_start(w2_raw[:, :, :], w2[e].rearrange("(c p) d -> p c d", p=P)).then_inc(w2_in, 16)

            def load_block(m, i, par):
                after(sp, xT_done, m - 1)
                sp.dma_start(xin[:, par], in_blocks[m]).then_inc(xin_in[par], 16)

            def store_block(m, par):
                sp.wait_ge(y_ready, J * m + J)
                sp.dma_start(out_blocks[m], y[:, par]).then_inc(y_out[par], 16)

            load_block(0, 0, 0)
            load_weights(0, 0)
            load_block(1, 0, 1)
            load_weights(1, 1)

            def turn(i, last=False):
                m = 4 * i if isinstance(i, int) else sp.snap(4 * i)
                for b in range(4):
                    if not (last and b >= 2):
                        load_block(m + b + 2, 0, b % 2)
                    if b % 2 == 0 and not last:
                        load_weights(2 * i + 2 + b // 2, (2 * i + 2 + b // 2) % E)
                    if not (isinstance(i, int) and i == 0 and b == 0):
                        store_block(m + b - 1, (b - 1) % 2)

            turn(0)
            with sp.Fori(1, M // 4 - 1) as i:
                turn(i)
            turn(M // 4 - 1, last=True)
            store_block(M - 1, (M - 1) % 2)
            for par in (0, 1):
                sp.wait_ge(y_out[par], 16 * M // 2)

        @block.gpsimd
        def _(pool):
            def split(s, par, guard):
                pool.wait_ge(w1_in, 16 * s + 16)
                if guard:
                    pool.wait_ge(h_done, (s - 1) * NB * PAIRS)
                    held(pool, passed)
                pool.tensor_copy(w1_hi[:, par], w1_raw[:, :, :]).then_inc(w1hi_ready, 1)
                pool.wait_ge(w1hi_ready, s + 1)
                pool.tensor_tensor(w1_lo[:, par], w1_raw[:, :, :], w1_hi[:, par].bitcast(F32),
                                   ALU.subtract).then_inc(w1lo_ready, 1)
                pool.wait_ge(w2_in, 16 * s + 16)
                if guard:
                    pool.wait_ge(y_done, (s - 1) * NB * J)
                    held(pool, passed)
                pool.tensor_copy(w2_hi[:, par], w2_raw[:, :, :]).then_inc(w2hi_ready, 1)
                pool.wait_ge(w2hi_ready, s + 1)
                pool.tensor_tensor(w2_lo[:, par], w2_raw[:, :, :], w2_hi[:, par].bitcast(F32),
                                   ALU.subtract).then_inc(w2lo_ready, 1)

            split(0, 0, False)
            split(1, 1, False)
            with pool.Fori(1, S // 2) as i:
                split(2 * i, 0, True)
                split(2 * i + 1, 1, True)

        @block.scalar
        def _(act):
            def x_hi(m, par):
                act.wait_ge(xT_done, m + 1)
                after(act, h_done, PAIRS * (m - 1))
                act.activation(xT_hi[:, par], ps_x[:, :, :], ACT.Copy).then_inc(xhi_ready, 1)

            def gelu(m, par, q):
                act.wait_ge(h_done, PAIRS * m + q + 1)
                after(act, glo_ready, PAIRS * m + q - 1)
                act.activation(g[:, q % 2], ps_h[:, q % 2], ACT.Gelu_apprx_tanh).then_inc(g_ready, 1)
                act.wait_ge(g_ready, PAIRS * m + q + 1)
                if q == 0:
                    after(act, y_done, J * (m - 1))
                act.activation(g_hi[:, par, 2 * q:2 * q + 2], g[:, q % 2], ACT.Copy).then_inc(ghi_ready, 1)

            x_hi(0, 0)

            def block_of(m, par, last=False):
                for q in range(PAIRS):
                    gelu(m, par, q)
                    if q == 1 and not last:
                        x_hi(m + 1, 1 - par)

            block_of(0, 0)
            block_of(1, 1)
            with act.Fori(1, M // 2 - 1) as i:
                block_of(2 * i, 0)
                block_of(2 * i + 1, 1)
            block_of(M - 2, 0)
            block_of(M - 1, 1, last=True)

        @block.tensor
        def _(pe):
            def turn_x(m, i, par):
                pe.wait_ge(xin_in[par], 16 * i + 16)
                after(pe, xhi_ready, m)
                after(pe, xlo_ready, m)
                for j in range(J):
                    for c in range(C):
                        last = pe.transpose(ps_x[:, c, j * P:(j + 1) * P], xin[:, par, j, c * P:(c + 1) * P],
                                            ident[:, :])
                last.then_inc(xT_done, 1)

            def hidden(m, par, w, q):
                if q == 0:
                    pe.wait_ge(xhi_ready, m + 1)
                    pe.wait_ge(xlo_ready, m + 1)
                after(pe, g_ready, PAIRS * m + q - 1)
                for f in (2 * q, 2 * q + 1):
                    to = ps_h[:, q % 2, f % 2]
                    fs = slice(f * P, (f + 1) * P)
                    for c in range(C):
                        pe.matmul(to, w1_hi[:, w, c, fs], xT_hi[:, par, c], start=(c == 0), stop=False)
                        pe.matmul(to, w1_hi[:, w, c, fs], xT_lo[:, par, c], start=False, stop=False)
                        last = pe.matmul(to, w1_lo[:, w, c, fs], xT_hi[:, par, c], start=False, stop=(c == C - 1))
                last.then_inc(h_done, 1)

            def result(m, par, w, j):
                if j == 0:
                    pe.wait_ge(ghi_ready, PAIRS * m + PAIRS)
                    pe.wait_ge(glo_ready, PAIRS * m + PAIRS)
                after(pe, y_ready, J * m + j - 1)
                to = ps_y[:, j % 2, 0:D]
                rows = slice(j * P, (j + 1) * P)
                for f in range(FC):
                    pe.matmul(to, g_hi[:, par, f, rows], w2_hi[:, w, f], start=(f == 0), stop=False)
                    pe.matmul(to, g_hi[:, par, f, rows], w2_lo[:, w, f], start=False, stop=False)
                    last = pe.matmul(to, g_lo[:, par, f, rows], w2_hi[:, w, f], start=False, stop=(f == FC - 1))
                last.then_inc(y_done, 1)

            def block_of(m, i, b, first=False, last=False):
                if b % 2 == 0:
                    pe.wait_ge(w1lo_ready, 2 * i + b // 2 + 1)
                if b % 2 == 1:
                    pe.wait_ge(w2lo_ready, 2 * i + b // 2 + 1)
                for q in range(PAIRS):
                    hidden(m, b % 2, b // 2, q)
                    if q == 0 and not last:
                        turn_x(m + 1, 2 * i + (b + 1) // 2, (b + 1) % 2)
                    if not first:
                        result(m - 1, (b - 1) % 2, (b - 1) % 4 // 2, q)

            turn_x(0, 0, 0)
            for b in range(4):
                block_of(b, 0, b, first=(b == 0))
            with pe.Fori(1, M // 4 - 1) as i:
                for b in range(4):
                    block_of(4 * i + b, i, b)
            for b in range(4):
                block_of(M - 4 + b, M // 4 - 1, b, last=(b == 3))
            for j in range(J):
                result(M - 1, 1, 1, j)

        @block.vector
        def _(dve):
            def x_lo(m, par):
                dve.wait_ge(xhi_ready, m + 1)
                dve.tensor_tensor(xT_lo[:, par], ps_x[:, :, :], xT_hi[:, par].bitcast(F32),
                                  ALU.subtract).then_inc(xlo_ready, 1)

            def g_rest(m, par, q):
                dve.wait_ge(ghi_ready, PAIRS * m + q + 1)
                dve.tensor_tensor(g_lo[:, par, 2 * q:2 * q + 2], g[:, q % 2],
                                  g_hi[:, par, 2 * q:2 * q + 2].bitcast(F32), ALU.subtract).then_inc(glo_ready, 1)

            def result(m, i, par, j):
                dve.wait_ge(y_done, J * m + j + 1)
                if j == 0 and not (isinstance(i, int) and i == 0):
                    dve.wait_ge(y_out[par], 16 * i)
                dve.tensor_copy(y[:, par, j], ps_y[:, j % 2, 0:D]).then_inc(y_ready, 1)

            x_lo(0, 0)

            def block_of(m, i, par, first=False, last=False):
                for q in range(PAIRS):
                    g_rest(m, par, q)
                    if q == 1 and not last:
                        x_lo(m + 1, 1 - par)
                    if not first:
                        result(m - 1, i + (par - 1) // 2, 1 - par, q)

            block_of(0, 0, 0, first=True)
            block_of(1, 0, 1)
            with dve.Fori(1, M // 2 - 1) as i:
                block_of(2 * i, i, 0)
                block_of(2 * i + 1, i, 1)
            block_of(M - 2, M // 2 - 1, 0)
            block_of(M - 1, M // 2 - 1, 1, last=True)
            for j in range(J):
                result(M - 1, M // 2 - 1, 1, j)


def combine(nc, sb, ps, sem, gates_dram, resid_rows, expert_out, out_rows, logits_all, top_all, row_all):
    R = B * J
    shifted = sb("shifted", [P, R, E])
    total = sb("total", [P, R])
    second = sb("second", [P, R])
    weight = sb("weight", [P, R, K])
    rows = sb("rows", [P, 2, J * K], U32)
    picked = sb("picked", [P, 2, K, J, D])
    resid = sb("resid_c", [P, 2, J, D])
    gb = sb("gb", [P, 2, D])
    mix = sb("mix", [P, J, D])
    mix2 = sb("mix2", [P, J, D])
    res = sb("res", [P, 2, J, D])
    resid_in = [sem("residc_in0"), sem("residc_in1")]
    gb_in = [sem("gb_in0"), sem("gb_in1")]
    passed = sem("c_passed")
    gathered = [sem("gathered0"), sem("gathered1")]
    out_done = [sem("out_done0"), sem("out_done1")]
    shift_ready, exp_ready, total_ready, weight_ready, rows_ready, mix_ready, mix2_ready, mix3_ready, res_ready = map(
        sem, "shift_ready exp_ready total_ready weight_ready rows_ready mix_ready mix2_ready mix3_ready res_ready".split())

    with nc.Block() as block:
        def after(engine, what, count):
            if not (isinstance(count, int) and count <= 0):
                engine.wait_ge(what, count)

        @block.sync
        def _(sp):
            def load(n, par):
                after(sp, res_ready, n - 1)
                sp.dma_start(resid[:, par], resid_rows[n]).then_inc(resid_in[par], 16)
                sp.dma_start(gb[:, par], gates_dram[n].rearrange("(a g d) -> a g d", a=1, g=GATES)[:, GB]
                             .broadcast_to([P, D])).then_inc(gb_in[par], 16)

            def store(n, par):
                sp.wait_ge(res_ready, n + 1)
                sp.dma_start(out_rows[n], res[:, par]).then_inc(out_done[par], 16)

            load(0, 0)
            load(1, 1)
            with sp.Fori(0, B // 2 - 1) as i:
                for par in (0, 1):
                    store(2 * i + par, par)
                    load(2 * i + par + 2, par)
            store(B - 2, 0)
            store(B - 1, 1)
            for par in (0, 1):
                sp.wait_ge(out_done[par], 16 * B // 2)

        @block.gpsimd
        def _(pool):
            def gather(n, i, par, first):
                if not first:
                    pool.wait_ge(gathered[par], 16 * J * K * i)
                    held(pool, passed)
                pool.tensor_copy(rows[:, par], row_all[:, bass.ds(n, 1), :].rearrange("p a c -> p (a c)")
                                 ).then_inc(rows_ready, 1)
                pool.wait_ge(rows_ready, n + 1)
                if not first:
                    pool.wait_ge(mix2_ready, n - 1)
                    held(pool, passed)
                for j in range(J):
                    for k in range(K):
                        at = rows[:, par, j * K + k:j * K + k + 1]
                        pool.indirect_dma_start(out=picked[:, par, k, j], out_offset=None, in_=expert_out,
                                                in_offset=bass.IndirectOffsetOnAxis(ap=at, axis=0)
                                                ).then_inc(gathered[par], 16)

            gather(0, 0, 0, True)
            gather(1, 0, 1, True)
            with pool.Fori(1, B // 2) as i:
                gather(2 * i, i, 0, False)
                gather(2 * i + 1, i, 1, False)

        @block.scalar
        def _(act):
            act.wait_ge(shift_ready, 1)
            act.activation(shifted[:, :, :], shifted[:, :, :], ACT.Exp).then_inc(exp_ready, 1)
            act.activation(second[:, :], second[:, :], ACT.Exp).then_inc(exp_ready, 1)
            act.wait_ge(weight_ready, 1)

            def scaled(n, i, par):
                act.wait_ge(gathered[par], 16 * J * K * (i + 1))
                after(act, mix2_ready, n)
                for j in range(J):
                    last = act.activation(mix[:, j], picked[:, par, 0, j], ACT.Copy,
                                          scale=weight[:, bass.ds(J * n + j, 1), 0])
                last.then_inc(mix_ready, 1)

            with act.Fori(0, B // 2) as i:
                scaled(2 * i, i, 0)
                scaled(2 * i + 1, i, 1)

        @block.vector
        def _(dve):
            dve.tensor_tensor(shifted[:, :, :], logits_all[:, :, :], top_all[:, :, 0:1].broadcast_to([P, R, E]),
                              ALU.subtract)
            dve.tensor_tensor(second[:, :], top_all[:, :, 1], top_all[:, :, 0], ALU.subtract).then_inc(shift_ready, 1)
            dve.wait_ge(exp_ready, 2)
            dve.tensor_reduce(total[:, :], shifted[:, :, :], AX.X, ALU.add).then_inc(total_ready, 1)
            dve.wait_ge(total_ready, 1)
            dve.reciprocal(weight[:, :, 0], total[:, :]).then_inc(total_ready, 1)
            dve.wait_ge(total_ready, 2)
            dve.tensor_tensor(weight[:, :, 1], second[:, :], weight[:, :, 0], ALU.mult).then_inc(weight_ready, 1)
            dve.wait_ge(weight_ready, 1)

            def mixed(n, i, par):
                dve.wait_ge(mix_ready, n + 1)
                after(dve, res_ready, n)
                for j in range(J):
                    last = dve.scalar_tensor_tensor(mix2[:, j], picked[:, par, 1, j],
                                                    weight[:, bass.ds(J * n + j, 1), 1], mix[:, j],
                                                    ALU.mult, ALU.add)
                last.then_inc(mix2_ready, 1)
                dve.wait_ge(mix2_ready, n + 1)
                dve.wait_ge(gb_in[par], 16 * i + 16)
                if not isinstance(i, int) or i > 0:
                    dve.wait_ge(out_done[par], 16 * i)
                dve.tensor_tensor(mix2[:, :, :], mix2[:, :, :], gb[:, par].unsqueeze(1).broadcast_to([P, J, D]),
                                  ALU.mult).then_inc(mix3_ready, 1)
                dve.wait_ge(mix3_ready, n + 1)
                dve.wait_ge(resid_in[par], 16 * i + 16)
                dve.tensor_tensor(res[:, par], mix2[:, :, :], resid[:, par], ALU.add).then_inc(res_ready, 1)

            with dve.Fori(0, B // 2) as i:
                mixed(2 * i, i, 0)
                mixed(2 * i + 1, i, 1)


_INS = ["L0_attn_x", "L0_attn_Wqkv", "L0_attn_bqkv", "L0_attn_Wout", "L0_attn_bout", "L0_ffn_router_w",
        "L0_ffn_w1", "L0_ffn_w2", "L0_ffn_bias", "L0_c", "L0_wmod"]


def kernel(**inputs):
    import numpy as np
    import concourse.bacc as bacc
    from concourse.bass_utils import run_bass_kernel_spmd

    nc = bacc.Bacc("TRN2", target_bir_lowering=False, num_devices=1)
    arrays, args = {}, []
    for name in _INS:
        a = np.ascontiguousarray(inputs[name])
        arrays[f"in_{name}"] = a
        args.append(nc.dram_tensor(f"in_{name}", a.shape, mybir.dt.from_np(a.dtype), kind="ExternalInput").ap())
    args.append(nc.dram_tensor("out_dram", (B, T, D), F32, kind="ExternalOutput").ap())
    adaln_moe_kernel(nc, *args)
    result = run_bass_kernel_spmd(nc, [arrays], core_ids=[0])
    return result.results[0]["out_dram"]
```

```python
from contextlib import ExitStack

import concourse.bass as bass
from concourse import mybir

F32 = mybir.dt.float32
F32R = mybir.dt.float32r
BF16 = mybir.dt.bfloat16
U32 = mybir.dt.uint32
ALU = mybir.AluOpType
ACT = mybir.ActivationFunctionType
AX = mybir.AxisListType

P = 128
B, T, D = 16, 512, 256
J = T // P
C = D // P
E, K = 8, 2
F = 1024
FC = F // P
CAP = B * T // E
HALF = E * CAP
ROWS = K * HALF
NOROW = HALF
S = K * E
BLK = 512
NB = CAP // BLK
GATES = 6
GA, CB, SB, GB, GBBIAS, GABOUT = range(GATES)
ROW_GATES = 5
EPS = 1e-5


def adaln_moe_kernel(nc, x, Wqkv, bqkv, Wout, bout, router_w, w1, w2, ffn_bias, cond, wmod, out):
    x_rows = x.rearrange("b (p j) d -> b p j d", j=J)
    out_rows = out.rearrange("b (p j) d -> b p j d", j=J)
    gates_dram = nc.dram_tensor("gates_dram", (B, GATES * D), F32, kind="Internal").ap()
    resid_dram = nc.dram_tensor("resid_dram", (B, T, D), F32, kind="Internal").ap()
    expert_in = nc.dram_tensor("expert_in", (ROWS, D), F32, kind="Internal").ap()
    expert_out = [nc.dram_tensor(f"expert_out{k}", (HALF + 1, D), F32, kind="Internal").ap() for k in range(K)]
    resid_rows = resid_dram.rearrange("b (p j) d -> b p j d", j=J)
    in_blocks = expert_in.rearrange("(m p j) d -> m p j d", p=P, j=J)
    out_blocks = [o[0:HALF, :].rearrange("(m p j) d -> m p j d", p=P, j=J) for o in expert_out]

    with ExitStack() as whole:
        def tensors(ctx):
            def sb(name, shape, dt=F32):
                return ctx.enter_context(nc.sbuf_tensor(name, shape, dt))

            def ps(name, shape, dt=F32):
                return ctx.enter_context(nc.psum_tensor(name, shape, dt))

            def sem(name):
                return ctx.enter_context(nc.semaphore(name))

            return sb, ps, sem

        sb, _, _ = tensors(whole)
        ident = sb("ident", [P, P])
        logits_all = sb("logits_all", [P, B * J, E])
        top_all = sb("top_all", [P, B * J, K])
        row_all = sb("row_all", [P, B, J * K], U32)
        weight = sb("weight", [P, B * J, K])
        part = sb("part", [P, J, D])
        w1_raw = sb("w1_raw", [P, C, F])
        w2_raw = sb("w2_raw", [P, FC, D])

        with ExitStack() as first:
            sb, ps, sem = tensors(first)
            attend_and_route(nc, sb, ps, sem, x_rows, Wqkv, bqkv, Wout, bout, router_w, ffn_bias, cond, wmod,
                             gates_dram, resid_rows, expert_in, expert_out,
                             ident, logits_all, top_all, row_all, w1, w2, w1_raw, w2_raw)
        with ExitStack() as second:
            sb, ps, sem = tensors(second)
            experts(nc, sb, ps, sem, w1, w2, w1_raw, w2_raw, in_blocks, out_blocks, ident,
                    gates_dram, resid_rows, expert_out[0], logits_all, top_all, row_all, weight, part)
        with ExitStack() as third:
            sb, ps, sem = tensors(third)
            combine(nc, sb, ps, sem, gates_dram, resid_rows, expert_out[1], out_rows, row_all, weight, part, ident)


def held(engine, passed):
    engine.sem_inc(passed, 1)


def attend_and_route(nc, sb, ps, sem, x_rows, Wqkv, bqkv, Wout, bout, router_w, ffn_bias, cond, wmod,
                     gates_dram, resid_rows, expert_in, expert_out,
                     ident, logits_all, top_all, row_all, w1, w2, w1_raw, w2_raw):
    ZERO = 2048
    cond_sb = sb("cond_sb", [B, D])
    silu_c = sb("silu_c", [B, D])
    silu_cT = sb("silu_cT", [P, C, B])
    wmod_sb = sb("wmod_sb", [P, C, 6 * D])
    mod_cols = sb("mod_cols", [P, 2 * C, B])
    neg_gate = sb("neg_gate", [B, 2, D])
    sign_gate = sb("sign_gate", [B, 2, D])
    gate_rows = sb("gate_rows", [B, GATES, D])
    bias_rows = sb("bias_rows", [B, 2, D])
    wqkv_sb = sb("wqkv_sb", [P, C, 3 * D])
    wqkv_hi = sb("wqkv_hi", [P, C, 3 * D], F32R)
    wqkv_lo = sb("wqkv_lo", [P, C, 3 * D], F32R)
    bq_cols = sb("bq_cols", [P, C])
    bkv_f = sb("bkv_f", [P, 2 * D])
    bkv_part = sb("bkv_part", [P, 2 * D])
    bkv_r = sb("bkv_r", [P, 2 * D], F32R)
    pick_f = sb("pick_f", [P, P])
    pick_r = sb("pick_r", [P, P], F32R)
    wout_sb = sb("wout_sb", [P, C, D])
    router_sb = sb("router_sb", [P, C, E])
    ones_f = sb("ones_f", [P, P])
    ones_b = sb("ones_b", [P, P], BF16)
    ident_b = sb("ident_b", [P, P], BF16)
    before_b = sb("before_b", [P, P], BF16)
    expert_no = sb("expert_no", [P, E])
    choice_base = sb("choice_base", [P, J, K])
    eps_col = sb("eps_col", [P, 1])
    root_eps = sb("root_eps", [P, 1])
    zeros = sb("zeros", [P, ZERO])
    xt = sb("xt", [P, 2, J, D])
    gates = sb("gates", [P, 2, ROW_GATES, D])
    bout_gate = sb("bout_gate", [P, 2, D])
    st1 = sb("st1", [P, J, 6])
    mv1 = sb("mv1", [P, J, 2])
    sd1 = sb("sd1", [P, J])
    rs1 = sb("rs1", [P, J])
    xn = sb("xn", [P, J, D])
    hT = sb("hT", [P, C, T])
    hT_hi = sb("hT_hi", [P, 2, C, T], F32R)
    hT_lo = sb("hT_lo", [P, 2, C, T], F32R)
    neg_mr1 = sb("neg_mr1", [P, J])
    k_sb = sb("k_sb", [P, J, D])
    k_sq = sb("k_sq", [P, D])
    kn2 = sb("kn2", [P, J])
    kn = sb("kn", [P, J])
    rk = sb("rk", [P, J])
    kv = sb("kv", [P, J, D])
    kv_cols = sb("kv_cols", [P, C])
    q_hi = sb("q_hi", [P, C, T], F32R)
    q_lo = sb("q_lo", [P, C, T], F32R)
    q_sq = sb("q_sq", [P, C, T])
    q_sq1 = sb("q_sq1", [P, T])
    qn = sb("qn", [P, J])
    rq = sb("rq", [P, J])
    wo_g = sb("wo_g", [P, C, D])
    wo_hi = sb("wo_hi", [P, C, D], F32R)
    wo_lo = sb("wo_lo", [P, C, D], F32R)
    xg = sb("xg", [P, 2, J, D])
    x1 = sb("x1", [P, J, D])
    resid = sb("resid", [P, 2, J, D])
    st2 = sb("st2", [P, J, 6])
    mv2 = sb("mv2", [P, J, 2])
    sd2 = sb("sd2", [P, J])
    rs2 = sb("rs2", [P, J])
    neg_mr2 = sb("neg_mr2", [P, J])
    xn2 = sb("xn2", [P, J, D])
    h2c = sb("h2c", [P, J, D])
    h2 = sb("h2", [P, 2, J, D])
    h2T = sb("h2T", [P, C, T])
    logits = sb("logits", [P, J, E])
    top8 = sb("top8", [P, J, 8])
    top8_no = sb("top8_no", [P, J, 8], U32)
    chosen = sb("chosen", [P, 2, J, K])
    onehot = sb("onehot", [P, 2, J, K, E], BF16)
    rank_all = sb("rank_all", [P, J, K, E])
    rank_own = sb("rank_own", [P, J * K, E])
    rank = sb("rank", [P, J, K])
    over = sb("over", [P, J, K])
    row_in = sb("row_in", [P, J, K])
    row_f = sb("row_f", [P, J, K])
    row = sb("row", [P, 2, J * K], U32)
    seen = sb("seen", [P, K * E])

    ps_T = ps("ps_T", [P, C, T])
    ps_kv = ps("ps_kv", [P, 2, 2 * D])
    ps_qo = ps("ps_qo", [P, 2, T])
    ps_s = ps("ps_s", [P, 512])
    ps_m = ps("ps_m", [P, 512])
    ps_kvc, ps_qn = ps_m[:, 0:C], ps_s[:, 0:J]
    ps_log = ps_s[:, 32:32 + J * E]
    ps_rank = ps_m[:, 128:128 + (J + 1) * K * E].rearrange("p (j c) -> p j c", j=J + 1)
    ps_o = ps_qo[:, :, :].rearrange("p a (b d) -> p (a b) d", d=D)

    kv_done, k_copied, kn2_ready, kv_ready = map(sem, "kv_done k_copied kn2_ready kv_ready".split())
    cond_in, wmod_in, bias_in, wqkv_in, bqkv_in, small_in, first_w_in = map(
        sem, "cond_in wmod_in bias_in wqkv_in bqkv_in small_in first_w_in".split())
    zeros_out, gates_out, zrow_out = map(sem, "zeros_out gates_out zrow_out".split())
    resid_out = [sem("resid_out0"), sem("resid_out1")]
    x_in = [sem("x_in0"), sem("x_in1")]
    gates_in = [sem("gates_in0"), sem("gates_in1")]
    bout_in = [sem("bout_in0"), sem("bout_in1")]
    scattered = [sem("scattered0"), sem("scattered1")]
    names = """ident0 ident1 consts0 silu_ready cT_ready cT_copied mod_ready cols_ready gate_sign gate_abs gate_min
      gates_ready wq_hi wq_lo bkv_hi bkv_ready zeros_ready rows_mod root_ready st1_ready mv1_ready
      sd1_ready rs1_ready nmr1_ready xn_ready xT_ready hT_ready hhi_ready hlo_ready kn_ready rk_ready
      kvc_done kvc_ready q_done qhi_ready qsq_ready qlo_ready qsq1_ready qn_done qn_ready rq_ready
      wog_ready wohi_ready wolo_ready o_done xg_ready x1_ready resid_ready st2_ready mv2_ready sd2_ready
      rs2_ready nmr2_ready xn2_ready h2c_ready h2_ready h2T_done h2T_ready log_done log_ready top_ready
      topno_ready top_kept chosen_ready onehot_ready rank_done rankall_ready seen_ready own_ready
      rank_ready rowin_ready rowf_ready row_ready dve_passed pool_passed""".split()
    s = {n: sem(n) for n in names}

    ZSTORES = ROWS * D // (P * ZERO)

    def after(engine, name, count):
        if not isinstance(count, int):
            engine.wait_ge(s[name], count)
        elif count > 0:
            engine.wait_ge(s[name], min(count, B))

    def h2_of(m, par):
        return xn[:, :, :] if isinstance(m, int) and m == B - 1 else h2[:, par]

    def step(stages, n, i, par):
        for stage, off in stages:
            m = n + off
            if isinstance(m, int) and not 0 <= m < B:
                continue
            stage(m, i + (par + off) // 2, (par + off) % 2)

    def pipeline(engine, stages, before=(None, None), ends=None):
        for n in range(-3, 4):
            if n == before[0]:
                before[1]()
            step(stages, n, n // 2, n % 2)
        with engine.Fori(2, B // 2 - 2) as i:
            step(stages, 2 * i, i, 0)
            step(stages, 2 * i + 1, i, 1)
        for n in range(B - 4, B + 2):
            step(ends if ends and n >= B else stages, n, n // 2, n % 2)

    with nc.Block() as block:
        @block.sync
        def _(sp):
            sp.dma_start(cond_sb[:, :], cond).then_inc(cond_in, 16)

            def gate_rows_of(m):
                return gates_dram[m].rearrange("(a g d) -> a g d", a=1, g=GATES)

            def load_x(m, i, par):
                after(sp, "xg_ready", m - 1)
                after(sp, "xn_ready", m - 1)
                sp.dma_start(xt[:, par], x_rows[m]).then_inc(x_in[par], 16)

            def load_gates(m, i, par):
                after(sp, "h2_ready", m - 1)
                after(sp, "resid_ready", m - 1)
                sp.dma_start(gates[:, par], gate_rows_of(m)[:, 0:ROW_GATES]
                             .broadcast_to([P, ROW_GATES, D])).then_inc(gates_in[par], 16)

            def load_bout_gate(m, i, par):
                sp.dma_start(bout_gate[:, par], gate_rows_of(m)[:, GABOUT]
                             .broadcast_to([P, D])).then_inc(bout_in[par], 16)

            def store_resid(m, i, par):
                after(sp, "resid_ready", m + 1)
                sp.dma_start(resid_rows[m], resid[:, par]).then_inc(resid_out[par], 16)

            def store_zeros(z):
                per = P * ZERO // D
                sp.dma_start(expert_in[z * per:(z + 1) * per, :].rearrange("(p r) d -> p (r d)", p=P),
                             zeros[:, :]).then_inc(zeros_out, 16)

            sp.dma_start(bkv_f[:, :], bqkv[D:3 * D].unsqueeze(0).broadcast_to([P, 2 * D])).then_inc(bqkv_in, 16)
            sp.dma_start(wmod_sb[:, :, :], wmod.rearrange("(c p) n -> p c n", p=P)).then_inc(wmod_in, 16)
            load_x(0, 0, 0)
            sp.dma_start(wqkv_sb[:, :, :], Wqkv.rearrange("(c p) n -> p c n", p=P)).then_inc(wqkv_in, 16)
            sp.dma_start(bias_rows[:, 0, :], bout.unsqueeze(0).broadcast_to([B, D])).then_inc(bias_in, 16)
            sp.dma_start(bias_rows[:, 1, :], ffn_bias[0, 0:1, :].broadcast_to([B, D])).then_inc(bias_in, 16)
            load_x(1, 0, 1)
            with nc.allow_non_contiguous_dma(reason="256 values, once"):
                sp.dma_start(bq_cols[:, :], bqkv[0:D].rearrange("(c p) -> p c", p=P)).then_inc(small_in, 16)
            sp.dma_start(wout_sb[:, :, :], Wout.rearrange("(c p) n -> p c n", p=P)).then_inc(small_in, 16)
            sp.dma_start(router_sb[:, :, :], router_w.rearrange("(c p) n -> p c n", p=P)).then_inc(small_in, 16)
            sp.wait_ge(s["zeros_ready"], 1)
            for o in expert_out:
                sp.dma_start(o[NOROW:NOROW + 1, :], zeros[0:1, 0:D]).then_inc(zrow_out, 16)
            for z in range(0, 3):
                store_zeros(z)
            sp.wait_ge(s["gates_ready"], 1)
            sp.dma_start(gates_dram, gate_rows[:, :, :].rearrange("b g d -> b (g d)")).then_inc(gates_out, 16)
            sp.wait_ge(gates_out, 16)
            for m in (0, 1):
                load_bout_gate(m, 0, m)
            for m in (0, 1):
                load_gates(m, 0, m)
            for z in range(3, 5):
                store_zeros(z)
            for m in (2, 3):
                load_x(m, 1, m % 2)
                load_bout_gate(m, 1, m % 2)
            for z in range(5, 13):
                store_zeros(z)

            def ahead(n, i, par):
                if not isinstance(n, int) or n + 4 < B:
                    load_x(n + 4, i + 2, par)
                    load_bout_gate(n + 4, i + 2, par)
                store_resid(n, i, par)
                if not isinstance(n, int) or n + 2 < B:
                    load_gates(n + 2, i + 1, par)

            ahead(0, 0, 0)
            for z in range(13, ZSTORES):
                store_zeros(z)
            ahead(1, 0, 1)
            with sp.Fori(1, B // 2 - 2) as i:
                ahead(2 * i, i, 0)
                ahead(2 * i + 1, i, 1)
            sp.dma_start(w1_raw[:, :, :], w1[0].rearrange("(c p) f -> p c f", p=P)).then_inc(first_w_in, 16)
            sp.dma_start(w2_raw[:, :, :], w2[0].rearrange("(c p) d -> p c d", p=P)).then_inc(first_w_in, 16)
            for n in range(B - 4, B):
                ahead(n, n // 2, n % 2)
            sp.wait_ge(zrow_out, 16 * K)
            sp.wait_ge(first_w_in, 32)
            for par in (0, 1):
                sp.wait_ge(resid_out[par], 16 * B // 2)

        @block.gpsimd
        def _(pool):
            pool.memset(ident[:, :], 0.0)
            pool.memset(ident_b[:, :], 0.0)
            pool.memset(before_b[:, :], 1.0).then_inc(s["ident0"], 1)
            pool.wait_ge(s["ident0"], 1)
            for m in (ident, ident_b):
                pool.affine_select(out=m[:, :], in_=m[:, :], compare_op=ALU.not_equal, fill=1.0,
                                   base=0, pattern=[[-1, P]], channel_multiplier=1)
            pool.affine_select(out=before_b[:, :], in_=before_b[:, :], compare_op=ALU.is_gt, fill=0.0,
                               base=0, pattern=[[1, P]], channel_multiplier=-1).then_inc(s["ident1"], 1)
            pool.memset(ones_b[:, :], 1.0)
            pool.memset(ones_f[:, :], 1.0)
            pool.memset(eps_col[:, :], EPS)
            pool.memset(seen[:, :], 0.0)
            pool.memset(choice_base[:, :, 0], 0.0)
            pool.memset(choice_base[:, :, 1], float(HALF))
            pool.iota(expert_no[:, :], pattern=[[1, E]], base=0, channel_multiplier=0,
                      allow_small_or_imprecise_dtypes=True).then_inc(s["consts0"], 1)
            pool.memset(zeros[:, :], 0.0).then_inc(s["zeros_ready"], 1)

            def q_squares(m, i, par):
                pool.wait_ge(s["qsq_ready"], m + 1)
                after(pool, "qn_done", m)
                pool.tensor_tensor(q_sq1[:, :], q_sq[:, 0], q_sq[:, 1], ALU.add).then_inc(s["qsq1_ready"], 1)

            def scatter(m, i, par):
                pool.wait_ge(s["row_ready"], m + 1)
                held(pool, s["pool_passed"])
                for j in range(J):
                    for k in range(K):
                        at = row[:, par, j * K + k:j * K + k + 1]
                        pool.indirect_dma_start(out=expert_in,
                                                out_offset=bass.IndirectOffsetOnAxis(ap=at, axis=0),
                                                in_=h2_of(m, par)[:, j], in_offset=None,
                                                bounds_check=ROWS - 1, oob_is_err=False
                                                ).then_inc(scattered[par], 16)

            def residual(m, i, par):
                if isinstance(m, int) and m == B - 1:
                    return
                pool.wait_ge(s["x1_ready"], m + 1)
                if not isinstance(m, int) or m > 1:
                    pool.wait_ge(resid_out[par], 16 * i)
                pool.tensor_tensor(resid[:, par], x1[:, :, :],
                                   gates[:, par, GBBIAS].unsqueeze(1).broadcast_to([P, J, D]),
                                   ALU.add).then_inc(s["resid_ready"], 1)

            def x_gated(m, i, par):
                pool.wait_ge(x_in[par], 16 * i + 16)
                pool.wait_ge(bout_in[par], 16 * i + 16)
                after(pool, "x1_ready", m - 1)
                pool.tensor_tensor(xg[:, par], xt[:, par],
                                   bout_gate[:, par].unsqueeze(1).broadcast_to([P, J, D]),
                                   ALU.add).then_inc(s["xg_ready"], 1)

            def shifted(m, i, par):
                if isinstance(m, int) and m == B - 1:
                    return
                pool.wait_ge(s["h2c_ready"], m + 1)
                if not isinstance(m, int) or m > 1:
                    pool.wait_ge(scattered[par], 16 * J * K * i)
                pool.tensor_tensor(h2[:, par], h2c[:, :, :],
                                   gates[:, par, SB].unsqueeze(1).broadcast_to([P, J, D]),
                                   ALU.add).then_inc(s["h2_ready"], 1)

            pipeline(pool, [(scatter, -2), (x_gated, 2), (q_squares, 1), (shifted, 0), (residual, 0)],
                     (2, lambda: pool.wait_ge(zeros_out, 16 * ZSTORES)))
            for par in (0, 1):
                pool.wait_ge(scattered[par], 16 * J * K * B // 2)

        @block.scalar
        def _(act):
            act.wait_ge(cond_in, 16)
            act.activation(silu_c[:, :], cond_sb[:, :], ACT.Silu).then_inc(s["silu_ready"], 1)
            act.wait_ge(s["cT_ready"], 1)
            act.activation(silu_cT[:, :, :], ps_m[:, 0:C * B].rearrange("p (c b) -> p c b", c=C),
                           ACT.Copy).then_inc(s["cT_copied"], 1)
            act.wait_ge(s["consts0"], 1)
            act.activation(root_eps[:, :], eps_col[:, :], ACT.Sqrt).then_inc(s["root_ready"], 1)

            def deviation1(m, i, par):
                act.wait_ge(s["mv1_ready"], m + 1)
                act.activation(sd1[:, :], mv1[:, :, 1], ACT.Sqrt, bias=eps_col[:, 0:1]).then_inc(s["sd1_ready"], 1)

            def norm1(m, i, par):
                act.wait_ge(s["nmr1_ready"], m + 1)
                after(act, "xT_ready", m)
                for j in range(J):
                    last = act.activation(xn[:, j], xt[:, par, j], ACT.Identity, scale=rs1[:, j:j + 1],
                                          bias=neg_mr1[:, j:j + 1])
                last.then_inc(s["xn_ready"], 1)

            def norm2(m, i, par):
                act.wait_ge(s["mv2_ready"], m + 1)
                act.activation(sd2[:, :], mv2[:, :, 1], ACT.Sqrt, bias=eps_col[:, 0:1]).then_inc(s["sd2_ready"], 1)
                act.wait_ge(s["nmr2_ready"], m + 1)
                after(act, "h2c_ready", m)
                for j in range(J):
                    last = act.activation(xn2[:, j], x1[:, j], ACT.Identity, scale=rs2[:, j:j + 1],
                                          bias=neg_mr2[:, j:j + 1])
                last.then_inc(s["xn2_ready"], 1)

            def modulated(m, i, par):
                act.wait_ge(s["xT_ready"], m + 1)
                if isinstance(m, int) and m == 0:
                    act.wait_ge(s["cols_ready"], 1)
                after(act, "hlo_ready", m)
                for c in range(C):
                    last = act.activation(hT[:, c], ps_T[:, c], ACT.Identity,
                                          scale=mod_cols[:, C + c, bass.ds(m, 1)],
                                          bias=mod_cols[:, c, bass.ds(m, 1)])
                last.then_inc(s["hT_ready"], 1)
                act.wait_ge(s["hT_ready"], m + 1)
                after(act, "q_done", m - 1)
                act.activation(hT_hi[:, par], hT[:, :, :], ACT.Copy).then_inc(s["hhi_ready"], 1)

            def k_tiles(m, i, par, tiles):
                if tiles[0] == 0:
                    after(act, "kn_ready", m)
                for j in tiles:
                    act.wait_ge(kv_done, J * m + j + 1)
                    if j == 0 and not (isinstance(m, int) and m == 0):
                        act.wait_ge(kv_ready, J * m)
                    act.activation(k_sb[:, j], ps_kv[:, j % 2, 0:D], ACT.Copy).then_inc(k_copied, 1)
                    act.wait_ge(k_copied, J * m + j + 1)
                    act.activation(k_sq[:, :], k_sb[:, j], ACT.Square,
                                   accum_out=kn2[:, j:j + 1]).then_inc(kn2_ready, 1)

            def k_first(m, i, par):
                k_tiles(m, i, par, (0, 1))

            def k_rest(m, i, par):
                k_tiles(m, i, par, (2, 3))
                act.wait_ge(kn2_ready, J * m + J)
                after(act, "rk_ready", m)
                act.activation(kn[:, :], kn2[:, :], ACT.Sqrt).then_inc(s["kn_ready"], 1)

            def out_weights(m, i, par):
                act.wait_ge(s["wog_ready"], m + 1)
                after(act, "o_done", m)
                act.activation(wo_hi[:, :, :], wo_g[:, :, :], ACT.Copy).then_inc(s["wohi_ready"], 1)

            def q_length(m, i, par):
                act.wait_ge(s["qn_done"], m + 1)
                after(act, "rq_ready", m)
                act.activation(qn[:, :], ps_qn, ACT.Sqrt).then_inc(s["qn_ready"], 1)

            def h2_turned(m, i, par):
                act.wait_ge(s["h2T_done"], m + 1)
                after(act, "log_done", m)
                act.activation(h2T[:, :, :], ps_T[:, :, :], ACT.Copy).then_inc(s["h2T_ready"], 1)

            def q_parts(m, i, par):
                act.wait_ge(s["q_done"], m + 1)
                after(act, "o_done", m)
                for c in range(C):
                    last = act.activation(q_hi[:, c], ps_qo[:, c], ACT.Identity, bias=bq_cols[:, c:c + 1])
                last.then_inc(s["qhi_ready"], 1)
                after(act, "qsq1_ready", m)
                for c in range(C):
                    last = act.activation(q_sq[:, c], ps_qo[:, c], ACT.Square, bias=bq_cols[:, c:c + 1])
                last.then_inc(s["qsq_ready"], 1)

            def small_loads():
                act.wait_ge(small_in, 48)

            pipeline(act, [(k_first, 1), (norm1, 2), (out_weights, 0), (k_rest, 1), (q_length, 0), (modulated, 2),
                           (deviation1, 3), (h2_turned, -1), (norm2, 0), (q_parts, 1)], (-1, small_loads))

        @block.tensor
        def _(pe):
            pe.wait_ge(s["ident1"], 1)
            pe.wait_ge(s["silu_ready"], 1)
            for c in range(C):
                last = pe.transpose(ps_m[:, c * B:(c + 1) * B], silu_c[:, c * P:(c + 1) * P], ident[0:B, 0:B])
            last.then_inc(s["cT_ready"], 1)
            pe.wait_ge(s["cT_copied"], 1)
            pe.wait_ge(wmod_in, 16)
            for m in range(2 * C):
                for c in range(C):
                    last = pe.matmul(ps_m[:, m * B:(m + 1) * B], wmod_sb[:, c, m * P:(m + 1) * P],
                                     silu_cT[:, c], start=(c == 0), stop=(c == C - 1))
            last.then_inc(s["mod_ready"], 1)

            for bank, lo, hi in ((ps_kv[:, 0], 2, 3), (ps_kv[:, 1], 3, 5), (ps_qo[:, 0], 5, 6)):
                for c in range(C):
                    last = pe.matmul(bank[0:B, 0:(hi - lo) * D], silu_cT[:, c], wmod_sb[:, c, lo * D:hi * D],
                                     start=(c == 0), stop=(c == C - 1))
            last.then_inc(s["rows_mod"], 1)

            def setup_waits():
                pe.wait_ge(s["wq_lo"], 1)
                pe.wait_ge(s["bkv_ready"], 1)
                pe.wait_ge(s["consts0"], 1)
                pe.wait_ge(small_in, 48)
                pe.wait_ge(s["gates_ready"], 1)

            def x_turned(m, i, par):
                pe.wait_ge(s["xn_ready"], m + 1)
                after(pe, "h2T_ready", m - 3)
                for j in range(J):
                    for c in range(C):
                        last = pe.transpose(ps_T[:, c, j * P:(j + 1) * P], xn[:, j, c * P:(c + 1) * P], ident[:, :])
                last.then_inc(s["xT_ready"], 1)

            def kv_tiles(m, i, par):
                pe.wait_ge(s["hlo_ready"], m + 1)
                pe.wait_ge(s["hhi_ready"], m + 1)
                for j in range(J):
                    if not (isinstance(m, int) and J * m + j < 2):
                        pe.wait_ge(kv_ready, J * m + j - 1)
                    to = ps_kv[:, j % 2]
                    pe.matmul(to, pick_r[:, :], bkv_r[:, :], start=True, stop=False)
                    tok = slice(j * P, (j + 1) * P)
                    for c in range(C):
                        pe.matmul(to, hT_hi[:, par, c, tok], wqkv_hi[:, c, D:3 * D], start=False, stop=False)
                        pe.matmul(to, hT_hi[:, par, c, tok], wqkv_lo[:, c, D:3 * D], start=False, stop=False)
                        last = pe.matmul(to, hT_lo[:, par, c, tok], wqkv_hi[:, c, D:3 * D],
                                         start=False, stop=(c == C - 1))
                    last.then_inc(kv_done, 1)

            def q_product(m, i, par):
                after(pe, "x1_ready", m)
                for f in range(C):
                    to = ps_qo[:, f]
                    feat = slice(f * P, (f + 1) * P)
                    for c in range(C):
                        pe.matmul(to, wqkv_hi[:, c, feat], hT_hi[:, par, c], start=(c == 0), stop=False)
                        pe.matmul(to, wqkv_hi[:, c, feat], hT_lo[:, par, c], start=False, stop=False)
                        last = pe.matmul(to, wqkv_lo[:, c, feat], hT_hi[:, par, c], start=False, stop=(c == C - 1))
                last.then_inc(s["q_done"], 1)

            def kv_sums(m, i, par):
                pe.wait_ge(s["rk_ready"], m + 1)
                pe.wait_ge(kv_ready, J * m + J)
                after(pe, "seen_ready", m - 2)
                for c in range(C):
                    for j in range(J):
                        last = pe.matmul(ps_kvc[:, c:c + 1], kv[:, j, c * P:(c + 1) * P], rk[:, j:j + 1],
                                         start=(j == 0), stop=(j == J - 1))
                last.then_inc(s["kvc_done"], 1)

            def q_lengths(m, i, par):
                pe.wait_ge(s["qsq1_ready"], m + 1)
                after(pe, "log_ready", m - 1)
                for j in range(J):
                    last = pe.matmul(ps_qn[:, j:j + 1], q_sq1[:, j * P:(j + 1) * P], ones_f[:, 0:1],
                                     start=True, stop=True)
                last.then_inc(s["qn_done"], 1)

            def output(m, i, par):
                pe.wait_ge(s["wolo_ready"], m + 1)
                pe.wait_ge(s["wohi_ready"], m + 1)
                pe.wait_ge(s["qlo_ready"], m + 1)
                pe.wait_ge(s["qhi_ready"], m + 1)
                for j in range(J):
                    tok = slice(j * P, (j + 1) * P)
                    for c in range(C):
                        pe.matmul(ps_o[:, j], q_hi[:, c, tok], wo_hi[:, c], start=(c == 0), stop=False)
                        pe.matmul(ps_o[:, j], q_hi[:, c, tok], wo_lo[:, c], start=False, stop=False)
                        last = pe.matmul(ps_o[:, j], q_lo[:, c, tok], wo_hi[:, c], start=False, stop=(c == C - 1))
                last.then_inc(s["o_done"], 1)

            def h2_turn(m, i, par):
                pe.wait_ge(s["h2_ready"], m + 1)
                after(pe, "hT_ready", m + 4)
                for j in range(J):
                    for c in range(C):
                        last = pe.transpose(ps_T[:, c, j * P:(j + 1) * P], h2_of(m, par)[:, j, c * P:(c + 1) * P],
                                            ident[:, :])
                last.then_inc(s["h2T_done"], 1)

            def route(m, i, par):
                pe.wait_ge(s["h2T_ready"], m + 1)
                after(pe, "qn_ready", m + 2)
                for j in range(J):
                    for c in range(C):
                        last = pe.matmul(ps_log[:, j * E:(j + 1) * E], h2T[:, c, j * P:(j + 1) * P],
                                         router_sb[:, c], start=(c == 0), stop=(c == C - 1))
                last.then_inc(s["log_done"], 1)

            def ranks(m, i, par):
                pe.wait_ge(s["onehot_ready"], m + 1)
                after(pe, "kvc_ready", m + 3)
                hot = onehot[:, par].rearrange("p j k e -> p j (k e)")
                for j in range(J):
                    pe.matmul(ps_rank[:, J], ones_b[:, :], hot[:, j], start=(j == 0), stop=(j == J - 1))
                for j in range(J):
                    pe.matmul(ps_rank[:, 0:J], before_b[:, :],
                              hot[:, j].unsqueeze(1).broadcast_to([P, J, K * E]), start=(j == 0), stop=False)
                for j in range(J - 1):
                    last = pe.matmul(ps_rank[:, j + 1:J], ident_b[:, :],
                                     hot[:, j].unsqueeze(1).broadcast_to([P, J - 1 - j, K * E]),
                                     start=False, stop=(j == J - 2))
                last.then_inc(s["rank_done"], 1)

            pipeline(pe, [(kv_tiles, 1), (q_lengths, 0), (x_turned, 2), (ranks, -2), (output, 0), (h2_turn, -1),
                          (kv_sums, 1), (q_product, 1), (route, -1)], (-1, setup_waits),
                     [(h2_turn, -1), (ranks, -2), (route, -1)])

        @block.vector
        def _(dve):
            dve.wait_ge(bqkv_in, 16)
            dve.memset(bkv_part[:, :], 0.0)
            dve.memset(pick_f[:, :], 0.0)
            dve.tensor_copy(bkv_r[:, :], bkv_f[:, :]).then_inc(s["bkv_hi"], 1)
            dve.wait_ge(s["bkv_hi"], 1)
            dve.memset(pick_f[0:1, :], 1.0)
            dve.memset(pick_f[32:33, :], 1.0)
            dve.tensor_tensor(bkv_f[:, :], bkv_f[:, :], bkv_r[:, :].bitcast(F32), ALU.subtract)
            dve.tensor_copy(bkv_part[0:1, :], bkv_r[0:1, :].bitcast(F32)).then_inc(s["bkv_hi"], 1)
            dve.wait_ge(s["bkv_hi"], 2)
            dve.tensor_copy(pick_r[:, :], pick_f[:, :])
            dve.tensor_copy(bkv_part[32:33, :], bkv_f[32:33, :]).then_inc(s["bkv_hi"], 1)
            dve.wait_ge(s["bkv_hi"], 3)
            dve.tensor_copy(bkv_r[:, :], bkv_part[:, :]).then_inc(s["bkv_ready"], 1)
            dve.wait_ge(wqkv_in, 16)
            dve.tensor_copy(wqkv_hi[:, :, :], wqkv_sb[:, :, :]).then_inc(s["wq_hi"], 1)
            dve.wait_ge(s["wq_hi"], 1)
            dve.tensor_tensor(wqkv_lo[:, :, :], wqkv_sb[:, :, :], wqkv_hi[:, :, :].bitcast(F32),
                              ALU.subtract).then_inc(s["wq_lo"], 1)
            dve.wait_ge(s["mod_ready"], 1)
            dve.tensor_copy(mod_cols[:, 0:C], ps_m[:, 0:C * B].rearrange("p (c b) -> p c b", c=C))
            dve.tensor_scalar(mod_cols[:, C:2 * C], ps_m[:, C * B:2 * C * B].rearrange("p (c b) -> p c b", c=C),
                              1.0, None, ALU.add).then_inc(s["cols_ready"], 1)

            def row_gates():
                dve.wait_ge(s["rows_mod"], 1)
                gate_banks = (ps_kv[0:B, 0, 0:D], ps_qo[0:B, 0, 0:D])
                for g in range(2):
                    dve.tensor_scalar(neg_gate[:, g], gate_banks[g], -1.0, None, ALU.mult)
                    last = dve.tensor_scalar(sign_gate[:, g], gate_banks[g], 0.0, 2.0, ALU.is_ge, ALU.mult)
                last.then_inc(s["gate_sign"], 1)
                dve.wait_ge(s["gate_sign"], 1)
                for g in range(2):
                    dve.tensor_tensor(neg_gate[:, g], gate_banks[g], neg_gate[:, g], ALU.max)
                    last = dve.tensor_scalar(sign_gate[:, g], sign_gate[:, g], -1.0, None, ALU.add)
                last.then_inc(s["gate_abs"], 1)
                dve.wait_ge(s["gate_abs"], 1)
                for g, to in enumerate((GA, GB)):
                    dve.scalar_tensor_tensor(gate_rows[:, to], neg_gate[:, g], 0.25, sign_gate[:, g],
                                             ALU.max, ALU.mult)
                dve.tensor_copy(gate_rows[:, SB], ps_kv[0:B, 1, 0:D])
                dve.tensor_scalar(gate_rows[:, CB], ps_kv[0:B, 1, D:2 * D], 1.0, None,
                                  ALU.add).then_inc(s["gate_min"], 1)
                dve.wait_ge(s["gate_min"], 1)
                dve.wait_ge(bias_in, 32)
                dve.tensor_tensor(gate_rows[:, GABOUT], gate_rows[:, GA], bias_rows[:, 0], ALU.mult)
                dve.tensor_tensor(gate_rows[:, GBBIAS], gate_rows[:, GB], bias_rows[:, 1],
                                  ALU.mult).then_inc(s["gates_ready"], 1)
                dve.wait_ge(s["consts0"], 1)
                dve.wait_ge(small_in, 48)

            def norm1_stats(tiles):
                def stats(m, i, par):
                    if tiles[0] == 0:
                        dve.wait_ge(x_in[par], 16 * i + 16)
                    for j in tiles:
                        last = dve.bn_stats(st1[:, j], xt[:, par, j])
                    if tiles[-1] == J - 1:
                        last.then_inc(s["st1_ready"], 1)
                return stats

            def norm1_mean(m, i, par):
                dve.wait_ge(s["st1_ready"], m + 1)
                after(dve, "nmr1_ready", m)
                held(dve, s["dve_passed"])
                for j in range(J):
                    last = dve.bn_aggr(mv1[:, j], st1[:, j])
                last.then_inc(s["mv1_ready"], 1)

            def norm1_inverse(m, i, par):
                dve.wait_ge(s["sd1_ready"], m + 1)
                after(dve, "xn_ready", m)
                dve.reciprocal(rs1[:, :], sd1[:, :]).then_inc(s["rs1_ready"], 1)

            def norm1_shift(m, i, par):
                dve.wait_ge(s["rs1_ready"], m + 1)
                dve.scalar_tensor_tensor(neg_mr1[:, :], mv1[:, :, 0], -1.0, rs1[:, :],
                                         ALU.mult, ALU.mult).then_inc(s["nmr1_ready"], 1)

            def h_rest(m, i, par):
                dve.wait_ge(s["hhi_ready"], m + 1)
                after(dve, "q_done", m - 1)
                dve.tensor_tensor(hT_lo[:, par], hT[:, :, :], hT_hi[:, par].bitcast(F32),
                                  ALU.subtract).then_inc(s["hlo_ready"], 1)

            def kv_tile(j):
                def product(m, i, par):
                    if j == 0:
                        after(dve, "kvc_done", m)
                    dve.wait_ge(k_copied, J * m + j + 1)
                    dve.tensor_tensor(kv[:, j], ps_kv[:, j % 2, D:2 * D], k_sb[:, j],
                                      ALU.mult).then_inc(kv_ready, 1)
                return product

            def k_inverse(m, i, par):
                dve.wait_ge(s["kn_ready"], m + 1)
                dve.reciprocal(rk[:, :], kn[:, :]).then_inc(s["rk_ready"], 1)

            def q_rest(c):
                def rest(m, i, par):
                    if c == 0:
                        dve.wait_ge(s["qsq_ready"], m + 1)
                        after(dve, "o_done", m)
                    last = dve.scalar_tensor_tensor(q_lo[:, c], ps_qo[:, c], bq_cols[:, c:c + 1],
                                                    q_hi[:, c].bitcast(F32), ALU.add, ALU.subtract)
                    if c == C - 1:
                        last.then_inc(s["qlo_ready"], 1)
                return rest

            def sums_out(m, i, par):
                dve.wait_ge(s["kvc_done"], m + 1)
                after(dve, "wog_ready", m)
                dve.tensor_copy(kv_cols[:, :], ps_kvc).then_inc(s["kvc_ready"], 1)

            def gated_weights(m, i, par):
                dve.wait_ge(gates_in[par], 16 * i + 16)
                dve.wait_ge(s["kvc_ready"], m + 1)
                after(dve, "wohi_ready", m)
                after(dve, "wolo_ready", m)
                for c in range(C):
                    last = dve.scalar_tensor_tensor(wo_g[:, c], wout_sb[:, c], kv_cols[:, c:c + 1],
                                                    gates[:, par, GA], ALU.mult, ALU.mult)
                last.then_inc(s["wog_ready"], 1)

            def gated_rest(m, i, par):
                dve.wait_ge(s["wohi_ready"], m + 1)
                after(dve, "o_done", m)
                dve.tensor_tensor(wo_lo[:, :, :], wo_g[:, :, :], wo_hi[:, :, :].bitcast(F32),
                                  ALU.subtract).then_inc(s["wolo_ready"], 1)

            def q_inverse(m, i, par):
                dve.wait_ge(s["qn_ready"], m + 1)
                after(dve, "x1_ready", m)
                dve.reciprocal(rq[:, :], qn[:, :]).then_inc(s["rq_ready"], 1)

            def attended(m, i, par):
                dve.wait_ge(s["rq_ready"], m + 1)
                dve.wait_ge(s["o_done"], m + 1)
                dve.wait_ge(s["xg_ready"], m + 1)
                after(dve, "resid_ready", m)
                after(dve, "xn2_ready", m)
                for j in range(J):
                    last = dve.scalar_tensor_tensor(x1[:, j], ps_o[:, j], rq[:, j:j + 1], xg[:, par, j],
                                                    ALU.mult, ALU.add)
                last.then_inc(s["x1_ready"], 1)

            def norm2_stats(m, i, par):
                dve.wait_ge(s["x1_ready"], m + 1)
                for j in range(J):
                    last = dve.bn_stats(st2[:, j], x1[:, j])
                last.then_inc(s["st2_ready"], 1)

            def norm2_mean(m, i, par):
                dve.wait_ge(s["st2_ready"], m + 1)
                after(dve, "nmr2_ready", m)
                held(dve, s["dve_passed"])
                for j in range(J):
                    last = dve.bn_aggr(mv2[:, j], st2[:, j])
                last.then_inc(s["mv2_ready"], 1)

            def norm2_inverse(m, i, par):
                dve.wait_ge(s["sd2_ready"], m + 1)
                after(dve, "xn2_ready", m)
                dve.reciprocal(rs2[:, :], sd2[:, :]).then_inc(s["rs2_ready"], 1)

            def norm2_shift(m, i, par):
                dve.wait_ge(s["rs2_ready"], m + 1)
                dve.scalar_tensor_tensor(neg_mr2[:, :], mv2[:, :, 0], -1.0, rs2[:, :],
                                         ALU.mult, ALU.mult).then_inc(s["nmr2_ready"], 1)

            def last_shifted(m, i, par):
                if isinstance(m, int) and m == B - 1:
                    dve.wait_ge(s["h2c_ready"], B)
                    dve.wait_ge(s["xT_ready"], B)
                    dve.tensor_tensor(h2_of(m, par), h2c[:, :, :],
                                      gates[:, par, SB].unsqueeze(1).broadcast_to([P, J, D]),
                                      ALU.add).then_inc(s["h2_ready"], 1)

            def last_residual(m, i, par):
                if isinstance(m, int) and m == B - 1:
                    dve.wait_ge(resid_out[par], 16 * i)
                    dve.tensor_tensor(resid[:, par], x1[:, :, :],
                                      gates[:, par, GBBIAS].unsqueeze(1).broadcast_to([P, J, D]),
                                      ALU.add).then_inc(s["resid_ready"], 1)

            def scaled(m, i, par):
                dve.wait_ge(s["xn2_ready"], m + 1)
                after(dve, "h2_ready", m)
                dve.tensor_tensor(h2c[:, :, :], xn2[:, :, :], gates[:, par, CB].unsqueeze(1).broadcast_to([P, J, D]),
                                  ALU.mult).then_inc(s["h2c_ready"], 1)

            def logits_out(m, i, par):
                dve.wait_ge(s["log_done"], m + 1)
                after(dve, "topno_ready", m)
                dve.tensor_copy(logits[:, :, :], ps_log.rearrange("p (j e) -> p j e", j=J)).then_inc(s["log_ready"], 1)

            def best(m, i, par):
                dve.wait_ge(s["log_ready"], m + 1)
                dve.tensor_copy(logits_all[:, bass.ds(J * m, J), :], logits[:, :, :])
                after(dve, "top_kept", m)
                held(dve, s["dve_passed"])
                for j in range(J):
                    last = dve.max(top8[:, j], logits[:, j])
                last.then_inc(s["top_ready"], 1)

            def best_no(m, i, par):
                dve.wait_ge(s["top_ready"], m + 1)
                dve.tensor_copy(top_all[:, bass.ds(J * m, J), :], top8[:, :, 0:K]).then_inc(s["top_kept"], 1)
                after(dve, "chosen_ready", m)
                held(dve, s["dve_passed"])
                for j in range(J):
                    last = dve.max_index(top8_no[:, j], top8[:, j], logits[:, j])
                last.then_inc(s["topno_ready"], 1)

            def chosen_out(m, i, par):
                dve.wait_ge(s["topno_ready"], m + 1)
                after(dve, "rowin_ready", m)
                dve.tensor_copy(chosen[:, par], top8_no[:, :, 0:K]).then_inc(s["chosen_ready"], 1)

            def marks(m, i, par):
                dve.wait_ge(s["chosen_ready"], m + 1)
                after(dve, "own_ready", m)
                dve.tensor_tensor(onehot[:, par].rearrange("p j k e -> p (j k) e"),
                                  expert_no[:, :].unsqueeze(1).broadcast_to([P, J * K, E]),
                                  chosen[:, par].rearrange("p j k -> p (j k)").unsqueeze(2)
                                  .broadcast_to([P, J * K, E]), ALU.is_equal).then_inc(s["onehot_ready"], 1)

            def ranks_out(m, i, par):
                dve.wait_ge(s["rank_done"], m + 1)
                after(dve, "own_ready", m)
                after(dve, "seen_ready", m)
                dve.tensor_tensor(rank_all[:, :, :, :].rearrange("p j k e -> p j (k e)"), ps_rank[:, 0:J],
                                  seen[:, :].unsqueeze(1).broadcast_to([P, J, K * E]),
                                  ALU.add).then_inc(s["rankall_ready"], 1)

            def own_ranks(m, i, par):
                dve.wait_ge(s["rankall_ready"], m + 1)
                dve.tensor_tensor(seen[:, :], ps_rank[:, J], seen[:, :], ALU.add).then_inc(s["seen_ready"], 1)
                after(dve, "rank_ready", m)
                dve.tensor_tensor(rank_own[:, :, :], rank_all[:, :, :, :].rearrange("p j k e -> p (j k) e"),
                                  onehot[:, par].rearrange("p j k e -> p (j k) e"),
                                  ALU.mult).then_inc(s["own_ready"], 1)

            def rank_sums(m, i, par):
                dve.wait_ge(s["own_ready"], m + 1)
                dve.tensor_reduce(rank[:, :, :].rearrange("p j k -> p (j k)"), rank_own[:, :, :], AX.X,
                                  ALU.add).then_inc(s["rank_ready"], 1)

            def row_parts(m, i, par):
                dve.wait_ge(s["rank_ready"], m + 1)
                dve.tensor_scalar(over[:, :, :], rank[:, :, :], float(CAP), float(2 * ROWS), ALU.is_ge, ALU.mult)
                dve.scalar_tensor_tensor(row_in[:, :, :], chosen[:, par], float(CAP), rank[:, :, :],
                                         ALU.mult, ALU.add).then_inc(s["rowin_ready"], 1)

            def row_sums(m, i, par):
                dve.wait_ge(s["rowin_ready"], m + 1)
                after(dve, "row_ready", m)
                dve.tensor_tensor(row_f[:, :, :], over[:, :, :], row_in[:, :, :], ALU.add).then_inc(s["rowf_ready"], 1)

            def rows_out(m, i, par):
                dve.wait_ge(s["rowf_ready"], m + 1)
                if not isinstance(m, int) or m > 1:
                    dve.wait_ge(scattered[par], 16 * J * K * i)
                dve.scalar_tensor_tensor(row[:, par], row_f[:, :, :].rearrange("p j k -> p (j k)"), float(ROWS),
                                         choice_base[:, :, :].rearrange("p j k -> p (j k)"), ALU.min, ALU.add)
                dve.tensor_scalar(row_all[:, bass.ds(m, 1), :].rearrange("p a c -> p (a c)"),
                                  row_f[:, :, :].rearrange("p j k -> p (j k)"),
                                  float(NOROW), None, ALU.min).then_inc(s["row_ready"], 1)

            pipeline(dve, [(kv_tile(0), 1), (kv_tile(1), 1), (logits_out, -2), (q_rest(0), 0), (best, -2),
                           (q_rest(1), 0), (best_no, -2), (gated_rest, 0), (chosen_out, -2), (kv_tile(2), 1),
                           (marks, -2), (kv_tile(3), 1), (k_inverse, 1), (norm1_stats((0, 1)), 3),
                           (ranks_out, -2), (norm1_stats((2, 3)), 3), (own_ranks, -2), (norm1_mean, 3),
                           (rank_sums, -2), (q_inverse, 0), (row_parts, -2), (row_sums, -2), (rows_out, -2),
                           (attended, 0), (norm2_stats, 0), (sums_out, 1), (norm2_mean, 0),
                           (gated_weights, 1), (norm2_inverse, 0), (norm1_inverse, 3), (norm2_shift, 0),
                           (norm1_shift, 3), (h_rest, 2), (scaled, 0),
                           (last_shifted, 0), (last_residual, -1)], (-2, row_gates))


def experts(nc, sb, ps, sem, w1, w2, w1_raw, w2_raw, in_blocks, out_blocks, ident,
            gates_dram, resid_rows, expert_out0, logits_all, top_all, row_all, weight, part):
    R = B * J
    w1_hi = sb("w1_hi", [P, 2, C, F], F32R)
    w1_lo = sb("w1_lo", [P, 2, C, F], F32R)
    w2_hi = sb("w2_hi", [P, 2, FC, D], F32R)
    w2_lo = sb("w2_lo", [P, 2, FC, D], F32R)
    xin = sb("xin", [P, 2, J, D])
    xT_hi = sb("xT_hi", [P, 2, C, BLK], F32R)
    xT_lo = sb("xT_lo", [P, 2, C, BLK], F32R)
    g = sb("g", [P, 2, 2, BLK])
    g_hi = sb("g_hi", [P, 2, FC, BLK], F32R)
    g_lo = sb("g_lo", [P, 2, FC, BLK], F32R)
    y = sb("y", [P, 2, J, D])
    shifted = sb("shifted", [P, R, E])
    total = sb("total", [P, R])
    second = sb("second", [P, R])
    rows0 = sb("rows0", [P, 2, J], U32)
    picked0 = sb("picked0", [P, 2, J, D])
    gb = sb("gb", [P, D])
    ps_x = ps("ps_x", [P, C, BLK])
    ps_h = ps("ps_h", [P, 2, 2, BLK])
    ps_y = ps("ps_y", [P, 2, 512])
    PAIRS = FC // 2
    M = S * NB

    w1_in, w2_in, passed = sem("w1_in"), sem("w2_in"), sem("w_passed")
    w1hi_ready, w1lo_ready, w2hi_ready, w2lo_ready = map(sem, "w1hi_ready w1lo_ready w2hi_ready w2lo_ready".split())
    xin_in = [sem("xin_in0"), sem("xin_in1")]
    y_out = [sem("y_out0"), sem("y_out1")]
    part_in, gb_in, part_out, scaled_ready, part_ready, rows0_ready = map(
        sem, "part_in gb_in part_out scaled_ready part_ready rows0_ready".split())
    gathered = [sem("first_gathered0"), sem("first_gathered1")]
    shift_ready, exp_ready, total_ready, first_weight_ready, weight_ready = map(
        sem, "shift_ready exp_ready total_ready first_weight_ready weight_ready".split())
    xT_done, xhi_ready, xlo_ready, h_done, g_ready, ghi_ready, glo_ready, y_done, y_ready = map(
        sem, "xT_done xhi_ready xlo_ready h_done g_ready ghi_ready glo_ready y_done y_ready".split())

    with nc.Block() as block:
        H = M // 2

        def after(engine, what, count):
            if not (isinstance(count, int) and count <= 0):
                engine.wait_ge(what, count)

        @block.sync
        def _(sp):
            def load_weights(s, e):
                after(sp, w1lo_ready, s)
                after(sp, w2lo_ready, s)
                sp.dma_start(w1_raw[:, :, :], w1[e].rearrange("(c p) f -> p c f", p=P)).then_inc(w1_in, 16)
                sp.dma_start(w2_raw[:, :, :], w2[e].rearrange("(c p) d -> p c d", p=P)).then_inc(w2_in, 16)

            def load_block(m, i, par):
                after(sp, xT_done, m - 1)
                sp.dma_start(xin[:, par], in_blocks[m]).then_inc(xin_in[par], 16)

            def store_block(m, k, par):
                sp.wait_ge(y_ready, J * m + J)
                sp.dma_start(out_blocks[k][m - k * H], y[:, par]).then_inc(y_out[par], 16)

            def load_part(n):
                after(sp, part_out, 16 * n)
                sp.dma_start(part[:, :, :], resid_rows[n]).then_inc(part_in, 16)
                after(sp, scaled_ready, n)
                sp.dma_start(gb[:, :], gates_dram[n].rearrange("(a g d) -> a g d", a=1, g=GATES)[:, GB]
                             .broadcast_to([P, D])).then_inc(gb_in, 16)

            def store_part(n):
                sp.wait_ge(part_ready, n + 1)
                sp.dma_start(resid_rows[n], part[:, :, :]).then_inc(part_out, 16)

            load_block(0, 0, 0)
            load_block(1, 0, 1)
            load_weights(1, 1)

            def turn(i, k, first=False, last=False):
                m = 4 * i if isinstance(i, int) else sp.snap(4 * i)
                for b in range(4):
                    if not (last and b >= 2):
                        load_block(m + b + 2, 0, b % 2)
                    if k == 1 and not (first and b < 2):
                        store_part(m + b - H - 2)
                    if k == 1 and not (first and b < 1):
                        load_part(m + b - H - 1)
                    if b % 2 == 1 and not last:
                        load_weights(2 * i + 2 + b // 2, (2 * i + 2 + b // 2) % E)
                    if not (isinstance(i, int) and i == 0 and b == 0):
                        store_block(m + b - 1, 0 if first and b == 0 else k, (b - 1) % 2)

            turn(0, 0)
            with sp.Fori(1, M // 8) as i:
                turn(i, 0)
            turn(M // 8, 1, first=True)
            with sp.Fori(M // 8 + 1, M // 4 - 1) as i:
                turn(i, 1)
            turn(M // 4 - 1, 1, last=True)
            store_part(B - 2)
            load_part(B - 1)
            store_block(M - 1, 1, (M - 1) % 2)
            for par in (0, 1):
                sp.wait_ge(y_out[par], 16 * M // 2)
            sp.wait_ge(part_out, 16 * (B - 1))

        @block.gpsimd
        def _(pool):
            def split(s, par, guard):
                pool.wait_ge(w1_in, 16 * s)
                if guard:
                    pool.wait_ge(h_done, (s - 1) * NB * PAIRS)
                    held(pool, passed)
                pool.tensor_copy(w1_hi[:, par], w1_raw[:, :, :]).then_inc(w1hi_ready, 1)
                pool.wait_ge(w1hi_ready, s + 1)
                pool.tensor_tensor(w1_lo[:, par], w1_raw[:, :, :], w1_hi[:, par].bitcast(F32),
                                   ALU.subtract).then_inc(w1lo_ready, 1)
                pool.wait_ge(w2_in, 16 * s)
                if guard:
                    pool.wait_ge(y_done, (s - 1) * NB * J)
                    held(pool, passed)
                pool.tensor_copy(w2_hi[:, par], w2_raw[:, :, :]).then_inc(w2hi_ready, 1)
                pool.wait_ge(w2hi_ready, s + 1)
                pool.tensor_tensor(w2_lo[:, par], w2_raw[:, :, :], w2_hi[:, par].bitcast(F32),
                                   ALU.subtract).then_inc(w2lo_ready, 1)

            def gather(n, i, par):
                if not isinstance(n, int) or n > 1:
                    pool.wait_ge(gathered[par], 16 * J * i)
                    held(pool, passed)
                pool.tensor_copy(rows0[:, par], row_all[:, bass.ds(n, 1), :]
                                 .rearrange("p a (j k) -> p (a j) k", k=K)[:, :, 0]).then_inc(rows0_ready, 1)
                pool.wait_ge(rows0_ready, n + 1)
                if not isinstance(n, int) or n > 1:
                    pool.wait_ge(part_ready, n - 1)
                    held(pool, passed)
                for j in range(J):
                    pool.indirect_dma_start(out=picked0[:, par, j], out_offset=None, in_=expert_out0,
                                            in_offset=bass.IndirectOffsetOnAxis(ap=rows0[:, par, j:j + 1], axis=0)
                                            ).then_inc(gathered[par], 16)

            split(1, 1, False)
            with pool.Fori(1, S // 4) as i:
                split(2 * i, 0, True)
                split(2 * i + 1, 1, True)
            split(S // 2, 0, True)
            split(S // 2 + 1, 1, True)
            for par in (0, 1):
                pool.wait_ge(y_out[par], 16 * H // 2)
            gather(0, 0, 0)
            gather(1, 0, 1)
            with pool.Fori(1, S // 4) as i:
                split(2 * i + S // 2, 0, True)
                gather(4 * i - 2, 2 * i - 1, 0)
                gather(4 * i - 1, 2 * i - 1, 1)
                split(2 * i + S // 2 + 1, 1, True)
                gather(4 * i, 2 * i, 0)
                gather(4 * i + 1, 2 * i, 1)
            gather(B - 2, B // 2 - 1, 0)
            gather(B - 1, B // 2 - 1, 1)

        @block.scalar
        def _(act):
            def x_hi(m, par):
                act.wait_ge(xT_done, m + 1)
                after(act, h_done, PAIRS * (m - 1))
                act.activation(xT_hi[:, par], ps_x[:, :, :], ACT.Copy).then_inc(xhi_ready, 1)

            def gelu(m, par, q):
                act.wait_ge(h_done, PAIRS * m + q + 1)
                after(act, glo_ready, PAIRS * m + q - 1)
                act.activation(g[:, q % 2], ps_h[:, q % 2], ACT.Gelu_apprx_tanh).then_inc(g_ready, 1)
                act.wait_ge(g_ready, PAIRS * m + q + 1)
                if q == 0:
                    after(act, y_done, J * (m - 1))
                act.activation(g_hi[:, par, 2 * q:2 * q + 2], g[:, q % 2], ACT.Copy).then_inc(ghi_ready, 1)

            act.activation(w1_hi[:, 0], w1_raw[:, :, :], ACT.Copy).then_inc(w1hi_ready, 1)
            x_hi(0, 0)
            act.activation(w2_hi[:, 0], w2_raw[:, :, :], ACT.Copy).then_inc(w2hi_ready, 1)
            act.wait_ge(shift_ready, 1)
            act.activation(shifted[:, :, :], shifted[:, :, :], ACT.Exp).then_inc(exp_ready, 1)
            act.activation(second[:, :], second[:, :], ACT.Exp).then_inc(exp_ready, 1)

            def block_of(m, par, last=False):
                for q in range(PAIRS):
                    gelu(m, par, q)
                    if q == 1 and not last:
                        x_hi(m + 1, 1 - par)

            block_of(0, 0)
            block_of(1, 1)
            with act.Fori(1, M // 2 - 1) as i:
                block_of(2 * i, 0)
                block_of(2 * i + 1, 1)
            block_of(M - 2, 0)
            block_of(M - 1, 1, last=True)

        @block.tensor
        def _(pe):
            def turn_x(m, i, par):
                pe.wait_ge(xin_in[par], 16 * i + 16)
                after(pe, xhi_ready, m)
                after(pe, xlo_ready, m)
                for j in range(J):
                    for c in range(C):
                        last = pe.transpose(ps_x[:, c, j * P:(j + 1) * P], xin[:, par, j, c * P:(c + 1) * P],
                                            ident[:, :])
                last.then_inc(xT_done, 1)

            def hidden(m, par, w, q):
                if q == 0:
                    pe.wait_ge(xhi_ready, m + 1)
                    pe.wait_ge(xlo_ready, m + 1)
                after(pe, g_ready, PAIRS * m + q - 1)
                for f in (2 * q, 2 * q + 1):
                    to = ps_h[:, q % 2, f % 2]
                    fs = slice(f * P, (f + 1) * P)
                    for c in range(C):
                        pe.matmul(to, w1_hi[:, w, c, fs], xT_hi[:, par, c], start=(c == 0), stop=False)
                        pe.matmul(to, w1_hi[:, w, c, fs], xT_lo[:, par, c], start=False, stop=False)
                        last = pe.matmul(to, w1_lo[:, w, c, fs], xT_hi[:, par, c], start=False, stop=(c == C - 1))
                last.then_inc(h_done, 1)

            def result(m, par, w, j):
                if j == 0:
                    pe.wait_ge(ghi_ready, PAIRS * m + PAIRS)
                    pe.wait_ge(glo_ready, PAIRS * m + PAIRS)
                after(pe, y_ready, J * m + j - 1)
                to = ps_y[:, j % 2, 0:D]
                rows = slice(j * P, (j + 1) * P)
                for f in range(FC):
                    pe.matmul(to, g_hi[:, par, f, rows], w2_hi[:, w, f], start=(f == 0), stop=False)
                    pe.matmul(to, g_hi[:, par, f, rows], w2_lo[:, w, f], start=False, stop=False)
                    last = pe.matmul(to, g_lo[:, par, f, rows], w2_hi[:, w, f], start=False, stop=(f == FC - 1))
                last.then_inc(y_done, 1)

            def block_of(m, i, b, first=False, last=False):
                if b % 2 == 0:
                    pe.wait_ge(w1lo_ready, 2 * i + b // 2 + 1)
                if b % 2 == 1:
                    pe.wait_ge(w2lo_ready, 2 * i + b // 2 + 1)
                for q in range(PAIRS):
                    hidden(m, b % 2, b // 2, q)
                    if q == 0 and not last:
                        turn_x(m + 1, 2 * i + (b + 1) // 2, (b + 1) % 2)
                    if not first:
                        result(m - 1, (b - 1) % 2, (b - 1) % 4 // 2, q)

            turn_x(0, 0, 0)
            for b in range(4):
                block_of(b, 0, b, first=(b == 0))
            with pe.Fori(1, M // 4 - 1) as i:
                for b in range(4):
                    block_of(4 * i + b, i, b)
            for b in range(4):
                block_of(M - 4 + b, M // 4 - 1, b, last=(b == 3))
            for j in range(J):
                result(M - 1, 1, 1, j)

        @block.vector
        def _(dve):
            def x_lo(m, par):
                dve.wait_ge(xhi_ready, m + 1)
                dve.tensor_tensor(xT_lo[:, par], ps_x[:, :, :], xT_hi[:, par].bitcast(F32),
                                  ALU.subtract).then_inc(xlo_ready, 1)

            def g_rest(m, par, q):
                dve.wait_ge(ghi_ready, PAIRS * m + q + 1)
                dve.tensor_tensor(g_lo[:, par, 2 * q:2 * q + 2], g[:, q % 2],
                                  g_hi[:, par, 2 * q:2 * q + 2].bitcast(F32), ALU.subtract).then_inc(glo_ready, 1)

            def first_share(n, i, par):
                dve.wait_ge(gathered[par], 16 * J * (i + 1))
                dve.wait_ge(gb_in, 16 * n + 16)
                for j in range(J):
                    last = dve.scalar_tensor_tensor(picked0[:, par, j], picked0[:, par, j],
                                                    weight[:, bass.ds(J * n + j, 1), 0], gb[:, :],
                                                    ALU.mult, ALU.mult)
                last.then_inc(scaled_ready, 1)
                dve.wait_ge(scaled_ready, n + 1)
                dve.wait_ge(part_in, 16 * n + 16)
                dve.tensor_tensor(part[:, :, :], part[:, :, :], picked0[:, par], ALU.add).then_inc(part_ready, 1)

            def result(m, i, par, j):
                dve.wait_ge(y_done, J * m + j + 1)
                if j == 0 and not (isinstance(i, int) and i == 0):
                    dve.wait_ge(y_out[par], 16 * i)
                dve.tensor_copy(y[:, par, j], ps_y[:, j % 2, 0:D]).then_inc(y_ready, 1)

            dve.tensor_tensor(shifted[:, :, :], logits_all[:, :, :], top_all[:, :, 0:1].broadcast_to([P, R, E]),
                              ALU.subtract)
            dve.tensor_tensor(second[:, :], top_all[:, :, 1], top_all[:, :, 0], ALU.subtract).then_inc(shift_ready, 1)
            dve.wait_ge(w1hi_ready, 1)
            dve.tensor_tensor(w1_lo[:, 0], w1_raw[:, :, :], w1_hi[:, 0].bitcast(F32),
                              ALU.subtract).then_inc(w1lo_ready, 1)
            x_lo(0, 0)
            dve.wait_ge(w2hi_ready, 1)
            dve.tensor_tensor(w2_lo[:, 0], w2_raw[:, :, :], w2_hi[:, 0].bitcast(F32),
                              ALU.subtract).then_inc(w2lo_ready, 1)
            dve.wait_ge(exp_ready, 2)
            dve.tensor_reduce(total[:, :], shifted[:, :, :], AX.X, ALU.add).then_inc(total_ready, 1)
            dve.wait_ge(total_ready, 1)
            dve.reciprocal(weight[:, :, 0], total[:, :]).then_inc(first_weight_ready, 1)
            dve.wait_ge(first_weight_ready, 1)
            dve.tensor_tensor(weight[:, :, 1], second[:, :], weight[:, :, 0], ALU.mult).then_inc(weight_ready, 1)
            dve.wait_ge(weight_ready, 1)

            def block_of(m, i, par, first=False, last=False, share=False):
                for q in range(PAIRS):
                    if q == PAIRS - 1 and share:
                        first_share(m - H - 1, i - H // 2 + (par - 1) // 2, 1 - par)
                    g_rest(m, par, q)
                    if q == 1 and not last:
                        x_lo(m + 1, 1 - par)
                    if not first:
                        result(m - 1, i + (par - 1) // 2, 1 - par, q)

            block_of(0, 0, 0, first=True)
            block_of(1, 0, 1)
            block_of(2, 1, 0)
            block_of(3, 1, 1)
            with dve.Fori(2, H // 2) as i:
                block_of(2 * i, i, 0)
                block_of(2 * i + 1, i, 1)
            block_of(H, H // 2, 0)
            block_of(H + 1, H // 2, 1, share=True)
            with dve.Fori(H // 2 + 1, M // 2 - 1) as i:
                block_of(2 * i, i, 0, share=True)
                block_of(2 * i + 1, i, 1, share=True)
            block_of(M - 2, M // 2 - 1, 0, share=True)
            block_of(M - 1, M // 2 - 1, 1, last=True, share=True)
            for j in range(J):
                result(M - 1, M // 2 - 1, 1, j)
            first_share(B - 1, B // 2 - 1, 1)


def combine(nc, sb, ps, sem, gates_dram, resid_rows, expert_out1, out_rows, row_all, weight, part, ident):
    DEPTH = 4
    rows = sb("rows", [P, B, J], U32)
    picked = sb("picked", [P, DEPTH, J, D])
    resid = sb("resid_c", [P, DEPTH, J, D])
    res = sb("res", [P, DEPTH, J, D])
    gb_rows = sb("gb_rows", [B, D])
    ps_gb = ps("ps_gb", [P, B, D])
    resid_in, gathered, out_done = [[sem(f"{name}{d}") for d in range(DEPTH)]
                                    for name in ("residc_in", "gathered", "out_done")]
    gb_rows_in, rows_ready, gb_ready, mix_ready, res_ready = map(
        sem, "gb_rows_in rows_ready gb_ready mix_ready res_ready".split())

    with nc.Block() as block:
        def after(engine, what, count):
            if not (isinstance(count, int) and count <= 0):
                engine.wait_ge(what, count)

        @block.sync
        def _(sp):
            def load(n, d):
                after(sp, res_ready, n - DEPTH + 1)
                sp.dma_start(resid[:, d], resid_rows[n]).then_inc(resid_in[d], 16)

            def store(n, d):
                sp.wait_ge(res_ready, n + 1)
                sp.dma_start(out_rows[n], res[:, d]).then_inc(out_done[d], 16)

            sp.dma_start(gb_rows[:, :], gates_dram.rearrange("b (g d) -> b g d", g=GATES)[:, GB]
                         ).then_inc(gb_rows_in, 16)
            for n in range(DEPTH):
                load(n, n)
            with sp.Fori(0, B // DEPTH - 2) as i:
                for d in range(DEPTH):
                    store(DEPTH * i + d, d)
                    load(DEPTH * i + d + DEPTH, d)
            for n in range(B - 2 * DEPTH, B):
                store(n, n % DEPTH)
                if n + DEPTH < B - 1:
                    load(n + DEPTH, n % DEPTH)
            for d in range(DEPTH):
                sp.wait_ge(out_done[d], 16 * B // DEPTH)

        @block.gpsimd
        def _(pool):
            pool.tensor_copy(rows[:, :, :], row_all[:, :, :].rearrange("p b (j k) -> p b j k", k=K)[:, :, :, 1]
                             ).then_inc(rows_ready, 1)
            pool.wait_ge(rows_ready, 1)
            for n in range(B):
                if n >= DEPTH:
                    pool.wait_ge(mix_ready, n - DEPTH + 1)
                for j in range(J):
                    pool.indirect_dma_start(out=picked[:, n % DEPTH, j], out_offset=None, in_=expert_out1,
                                            in_offset=bass.IndirectOffsetOnAxis(ap=rows[:, n, j:j + 1], axis=0)
                                            ).then_inc(gathered[n % DEPTH], 16)

        @block.tensor
        def _(pe):
            pe.wait_ge(gb_rows_in, 16)
            for n in range(B):
                last = pe.matmul(ps_gb[:, n], ident[0:B, n:n + 1].broadcast_to([B, P]), gb_rows[:, :],
                                 start=True, stop=True)
                if n % 2 == 1:
                    last.then_inc(gb_ready, 1)

        @block.vector
        def _(dve):
            def mixed(n, i, d, last_batch=False):
                dve.wait_ge(gathered[d], 16 * J * (i + 1))
                dve.wait_ge(gb_ready, (DEPTH // 2) * i + d // 2 + 1)
                if not isinstance(i, int) or i > 0:
                    dve.wait_ge(out_done[d], 16 * i)
                for j in range(J):
                    last = dve.scalar_tensor_tensor(res[:, d, j], picked[:, d, j],
                                                    weight[:, bass.ds(J * n + j, 1), 1],
                                                    ps_gb[:, bass.ds(n, 1)].rearrange("p a d -> p (a d)"),
                                                    ALU.mult, ALU.mult)
                last.then_inc(mix_ready, 1)
                dve.wait_ge(mix_ready, n + 1)
                if last_batch:
                    dve.tensor_tensor(res[:, d], res[:, d], part[:, :, :], ALU.add).then_inc(res_ready, 1)
                else:
                    dve.wait_ge(resid_in[d], 16 * i + 16)
                    dve.tensor_tensor(res[:, d], res[:, d], resid[:, d], ALU.add).then_inc(res_ready, 1)

            for n in range(DEPTH):
                mixed(n, 0, n)
            with dve.Fori(1, B // DEPTH - 1) as i:
                for d in range(DEPTH):
                    mixed(DEPTH * i + d, i, d)
            for n in range(B - DEPTH, B):
                mixed(n, n // DEPTH, n % DEPTH, last_batch=(n == B - 1))


_INS = ["L0_attn_x", "L0_attn_Wqkv", "L0_attn_bqkv", "L0_attn_Wout", "L0_attn_bout", "L0_ffn_router_w",
        "L0_ffn_w1", "L0_ffn_w2", "L0_ffn_bias", "L0_c", "L0_wmod"]


def kernel(**inputs):
    import numpy as np
    import concourse.bacc as bacc
    from concourse.bass_utils import run_bass_kernel_spmd

    nc = bacc.Bacc("TRN2", target_bir_lowering=False, num_devices=1)
    arrays, args = {}, []
    for name in _INS:
        a = np.ascontiguousarray(inputs[name])
        arrays[f"in_{name}"] = a
        args.append(nc.dram_tensor(f"in_{name}", a.shape, mybir.dt.from_np(a.dtype), kind="ExternalInput").ap())
    args.append(nc.dram_tensor("out_dram", (B, T, D), F32, kind="ExternalOutput").ap())
    adaln_moe_kernel(nc, *args)
    result = run_bass_kernel_spmd(nc, [arrays], core_ids=[0])
    return result.results[0]["out_dram"]
```
